# Optimizing a Trainium2 kernel written in Bass

```python
import numpy as np
import jax
import jax.numpy as jnp

def _softmax(x, axis=-1):
    return jax.nn.softmax(x, axis=axis)

def _gelu(x):
    return jax.nn.gelu(x, approximate=True)

def _silu(x):
    return jax.nn.silu(x)

def _sigmoid(x):
    return jax.nn.sigmoid(x)

def _layernorm(x, axis=-1, eps=1e-05):
    m = jnp.mean(x, axis=axis, keepdims=True)
    v = jnp.var(x, axis=axis, keepdims=True)
    return (x - m) / jnp.sqrt(v + eps)

def _scatter_add(tgt, idx, src, axis=0):
    return tgt.at[idx].add(src)

def _segment_sum(src, seg, n):
    return jax.ops.segment_sum(src, seg, n)
kernel_name = 'mk_vit_tower_cls_d1_tok_img256_r4_c111fc'

def setup_inputs(seed: int=0):
    np.random.seed(seed)
    _w = jnp.asarray

    def _rec_inputs():
        import jax
        import jax.numpy as jnp
        _rk = jax.random.key(seed)
        x = -0.000596345 + 1.00056 * jax.random.normal(jax.random.fold_in(_rk, 1), (128, 64, 64, 3), jnp.float32)
        cls_tok = 0.02 * jax.random.normal(jax.random.fold_in(_rk, 5), (1, 1, 64), jnp.float32)
        return (x, cls_tok)
    x, cls_tok = _rec_inputs()

    def _L0_tok_setup():
        import jax, jax.numpy as jnp
        import numpy as np
        B, H, W = (16, 64, 64)
        WIDTH, LAYERS, M1, M2 = (32, 4, 12, 12)
        EPS = 1e-05

        def layer_norm(x, g, b):
            mu = jnp.mean(x, axis=-1, keepdims=True)
            var = jnp.mean((x - mu) ** 2, axis=-1, keepdims=True)
            return (x - mu) * jax.lax.rsqrt(var + EPS) * g + b

        def gelu(x):
            return jax.nn.gelu(x, approximate=False)

        def spectral_conv(x, w1, w2):
            b, c, h, w = x.shape
            x_ft = jnp.fft.rfft2(x)
            out_ft = jnp.zeros((b, w1.shape[1], h, w // 2 + 1), dtype=x_ft.dtype)
            out_ft = out_ft.at[:, :, :M1, :M2].set(jnp.einsum('bixy,ioxy->boxy', x_ft[:, :, :M1, :M2], w1))
            out_ft = out_ft.at[:, :, -M1:, :M2].set(jnp.einsum('bixy,ioxy->boxy', x_ft[:, :, -M1:, :M2], w2))
            return jnp.fft.irfft2(out_ft, s=(h, w))
        key = jax.random.key(seed)
        ks = jax.random.split(key, 16)
        scale = 1.0 / (WIDTH * WIDTH)
        d = {'x': jax.random.normal(ks[0], (B, H, W, 3), jnp.float32), 'fc0_w': jax.random.normal(ks[1], (3, WIDTH), jnp.float32) * 0.5, 'fc0_b': jnp.zeros((WIDTH,), jnp.float32), 'ln0_g': jnp.ones((WIDTH,), jnp.float32), 'ln0_b': jnp.zeros((WIDTH,), jnp.float32), 'w1r': jax.random.uniform(ks[2], (LAYERS, WIDTH, WIDTH, M1, M2), jnp.float32) * scale, 'w1i': jax.random.uniform(ks[3], (LAYERS, WIDTH, WIDTH, M1, M2), jnp.float32) * scale, 'w2r': jax.random.uniform(ks[4], (LAYERS, WIDTH, WIDTH, M1, M2), jnp.float32) * scale, 'w2i': jax.random.uniform(ks[5], (LAYERS, WIDTH, WIDTH, M1, M2), jnp.float32) * scale, 'conv_w': jax.random.normal(ks[6], (LAYERS, WIDTH, WIDTH), jnp.float32) * (1.0 / np.sqrt(WIDTH)), 'conv_b': jnp.zeros((LAYERS, WIDTH), jnp.float32), 'ln_g': jnp.ones((LAYERS, WIDTH), jnp.float32), 'ln_b': jnp.zeros((LAYERS, WIDTH), jnp.float32), 'fc1_w': jax.random.normal(ks[7], (WIDTH, 128), jnp.float32) * (1.0 / np.sqrt(WIDTH)), 'fc1_b': jnp.zeros((128,), jnp.float32), 'fc2_w': jax.random.normal(ks[8], (128, 64), jnp.float32) * (1.0 / np.sqrt(128)), 'fc2_b': jnp.zeros((64,), jnp.float32), 'fc3_w': jax.random.normal(ks[9], (64, 1), jnp.float32) * (1.0 / np.sqrt(64)), 'fc3_b': jnp.zeros((1,), jnp.float32)}
        return d
    _L0_tok_all = _L0_tok_setup()
    _L0_tok_in = {k: v for k, v in _L0_tok_all.items() if k in ('fc0_w', 'fc0_b', 'ln0_g', 'ln0_b', 'w1r', 'w1i', 'w2r', 'w2i', 'conv_w', 'conv_b', 'ln_g', 'ln_b', 'fc1_w', 'fc1_b', 'fc2_w', 'fc2_b', 'fc3_w', 'fc3_b')}
    del _L0_tok_all

    def _L0_attn_setup():
        import jax, jax.numpy as jnp
        import numpy as np
        B, L, D, N, R = (8, 512, 64, 16, 16)
        key = jax.random.key(seed)
        ks = jax.random.split(key, 6)
        s = 0.02
        x = jax.random.normal(ks[0], (B, L, D), jnp.float32)
        W_xproj = jax.random.normal(ks[1], (R + 3 * N, D), jnp.float32) * s
        W_xbproj = jax.random.normal(ks[2], (R, D), jnp.float32) * s
        W_dt = jax.random.normal(ks[3], (D, R), jnp.float32) * s
        b_dt = jax.random.normal(ks[4], (D,), jnp.float32) * s
        A_log = jnp.log(jnp.broadcast_to(jnp.arange(1, N + 1, dtype=jnp.float32), (D, N)))
        D_skip = jnp.ones((D,), jnp.float32)
        W_out = jax.random.normal(ks[5], (D, D), jnp.float32) * s
        return dict(x=x, W_xproj=W_xproj, W_xbproj=W_xbproj, W_dt=W_dt, b_dt=b_dt, A_log=A_log, D_skip=D_skip, W_out=W_out)
    _L0_attn_all = _L0_attn_setup()
    _L0_attn_in = {k: v for k, v in _L0_attn_all.items() if k in ('W_xproj', 'W_xbproj', 'W_dt', 'b_dt', 'A_log', 'D_skip', 'W_out')}
    del _L0_attn_all

    def _L0_ffn_setup():
        import jax, jax.numpy as jnp
        import numpy as np
        B, T, C = (64, 96, 64)
        NH, NKV = (4, 2)
        HD = C // NH
        NREP = NH // NKV
        NE, TOPK = (8, 2)
        HID = int(8 / 3 * C)
        EPS_RMS = 1e-06

        def _rope_tables(t_len):
            inv_freq = 1.0 / 10000.0 ** (np.arange(0, HD, 2, dtype=np.float32) / HD)
            t = np.arange(t_len, dtype=np.float32)
            freqs = np.outer(t, inv_freq)
            emb = np.concatenate([freqs, freqs], axis=-1)
            return (jnp.asarray(np.cos(emb)), jnp.asarray(np.sin(emb)))

        def _rotate_half(x):
            h = x.shape[-1] // 2
            return jnp.concatenate([-x[..., h:], x[..., :h]], axis=-1)

        def _rmsnorm(v, w):
            return v * jax.lax.rsqrt(jnp.mean(v * v, axis=-1, keepdims=True) + EPS_RMS) * w
        key = jax.random.key(seed)
        ks = jax.random.split(key, 10)
        s = lambda k, shape: jax.random.normal(k, shape, jnp.float32) * 0.02
        return {'x': jax.random.normal(ks[0], (B, T, C), jnp.float32), 'ln1_w': jnp.ones((C,), jnp.float32), 'ln2_w': jnp.ones((C,), jnp.float32), 'wq': s(ks[1], (NH * HD, C)), 'wk': s(ks[2], (NKV * HD, C)), 'wv': s(ks[3], (NKV * HD, C)), 'wo': s(ks[4], (C, C)), 'router_w': s(ks[5], (NE, C)), 'w1': s(ks[6], (NE, HID, C)), 'w2': s(ks[7], (NE, C, HID)), 'w3': s(ks[8], (NE, HID, C))}
    _L0_ffn_all = _L0_ffn_setup()
    _L0_ffn_in = {k: v for k, v in _L0_ffn_all.items() if k in ('ln1_w', 'ln2_w', 'wq', 'wk', 'wv', 'wo', 'router_w', 'w1', 'w2', 'w3')}
    del _L0_ffn_all
    return {'x': x, 'cls_tok': cls_tok, 'L0_tok_fc0_w': _L0_tok_in['fc0_w'], 'L0_tok_fc0_b': _L0_tok_in['fc0_b'], 'L0_tok_ln0_g': _L0_tok_in['ln0_g'], 'L0_tok_ln0_b': _L0_tok_in['ln0_b'], 'L0_tok_w1r': _L0_tok_in['w1r'], 'L0_tok_w1i': _L0_tok_in['w1i'], 'L0_tok_w2r': _L0_tok_in['w2r'], 'L0_tok_w2i': _L0_tok_in['w2i'], 'L0_tok_conv_w': _L0_tok_in['conv_w'], 'L0_tok_conv_b': _L0_tok_in['conv_b'], 'L0_tok_ln_g': _L0_tok_in['ln_g'], 'L0_tok_ln_b': _L0_tok_in['ln_b'], 'L0_tok_fc1_w': _L0_tok_in['fc1_w'], 'L0_tok_fc1_b': _L0_tok_in['fc1_b'], 'L0_tok_fc2_w': _L0_tok_in['fc2_w'], 'L0_tok_fc2_b': _L0_tok_in['fc2_b'], 'L0_tok_fc3_w': _L0_tok_in['fc3_w'], 'L0_tok_fc3_b': _L0_tok_in['fc3_b'], 'L0_attn_W_xproj': _L0_attn_in['W_xproj'], 'L0_attn_W_xbproj': _L0_attn_in['W_xbproj'], 'L0_attn_W_dt': _L0_attn_in['W_dt'], 'L0_attn_b_dt': _L0_attn_in['b_dt'], 'L0_attn_A_log': _L0_attn_in['A_log'], 'L0_attn_D_skip': _L0_attn_in['D_skip'], 'L0_attn_W_out': _L0_attn_in['W_out'], 'L0_ffn_ln1_w': _L0_ffn_in['ln1_w'], 'L0_ffn_ln2_w': _L0_ffn_in['ln2_w'], 'L0_ffn_wq': _L0_ffn_in['wq'], 'L0_ffn_wk': _L0_ffn_in['wk'], 'L0_ffn_wv': _L0_ffn_in['wv'], 'L0_ffn_wo': _L0_ffn_in['wo'], 'L0_ffn_router_w': _L0_ffn_in['router_w'], 'L0_ffn_w1': _L0_ffn_in['w1'], 'L0_ffn_w2': _L0_ffn_in['w2'], 'L0_ffn_w3': _L0_ffn_in['w3']}

def reference(x, cls_tok, L0_tok_fc0_w, L0_tok_fc0_b, L0_tok_ln0_g, L0_tok_ln0_b, L0_tok_w1r, L0_tok_w1i, L0_tok_w2r, L0_tok_w2i, L0_tok_conv_w, L0_tok_conv_b, L0_tok_ln_g, L0_tok_ln_b, L0_tok_fc1_w, L0_tok_fc1_b, L0_tok_fc2_w, L0_tok_fc2_b, L0_tok_fc3_w, L0_tok_fc3_b, L0_attn_W_xproj, L0_attn_W_xbproj, L0_attn_W_dt, L0_attn_b_dt, L0_attn_A_log, L0_attn_D_skip, L0_attn_W_out, L0_ffn_ln1_w, L0_ffn_ln2_w, L0_ffn_wq, L0_ffn_wk, L0_ffn_wv, L0_ffn_wo, L0_ffn_router_w, L0_ffn_w1, L0_ffn_w2, L0_ffn_w3):
    import jax
    import jax.numpy as jnp

    def _L0_tok_ref(x, fc0_w, fc0_b, ln0_g, ln0_b, w1r, w1i, w2r, w2i, conv_w, conv_b, ln_g, ln_b, fc1_w, fc1_b, fc2_w, fc2_b, fc3_w, fc3_b):
        import jax, jax.numpy as jnp
        import numpy as np
        B, H, W = (16, 64, 64)
        WIDTH, LAYERS, M1, M2 = (32, 4, 12, 12)
        EPS = 1e-05

        def layer_norm(x, g, b):
            mu = jnp.mean(x, axis=-1, keepdims=True)
            var = jnp.mean((x - mu) ** 2, axis=-1, keepdims=True)
            return (x - mu) * jax.lax.rsqrt(var + EPS) * g + b

        def gelu(x):
            return jax.nn.gelu(x, approximate=False)

        def spectral_conv(x, w1, w2):
            b, c, h, w = x.shape
            x_ft = jnp.fft.rfft2(x)
            out_ft = jnp.zeros((b, w1.shape[1], h, w // 2 + 1), dtype=x_ft.dtype)
            out_ft = out_ft.at[:, :, :M1, :M2].set(jnp.einsum('bixy,ioxy->boxy', x_ft[:, :, :M1, :M2], w1))
            out_ft = out_ft.at[:, :, -M1:, :M2].set(jnp.einsum('bixy,ioxy->boxy', x_ft[:, :, -M1:, :M2], w2))
            return jnp.fft.irfft2(out_ft, s=(h, w))
        h = layer_norm(x @ fc0_w + fc0_b, ln0_g, ln0_b)
        h = jnp.transpose(h, (0, 3, 1, 2))
        for i in range(LAYERS):
            w1 = w1r[i] + 1j * w1i[i]
            w2 = w2r[i] + 1j * w2i[i]
            x1 = spectral_conv(h, w1, w2)
            x2 = jnp.einsum('bchw,oc->bohw', h, conv_w[i]) + conv_b[i][None, :, None, None]
            h = x1 + x2
            h = jnp.transpose(h, (0, 2, 3, 1))
            h = layer_norm(h, ln_g[i], ln_b[i])
            if i < LAYERS - 1:
                h = gelu(h)
            h = jnp.transpose(h, (0, 3, 1, 2))
        h = jnp.transpose(h, (0, 2, 3, 1))
        h = gelu(h @ fc1_w + fc1_b)
        h = gelu(h @ fc2_w + fc2_b)
        h = h @ fc3_w + fc3_b
        return h[..., 0]

    def _L0_attn_ref(x, W_xproj, W_xbproj, W_dt, b_dt, A_log, D_skip, W_out):
        import jax, jax.numpy as jnp
        import numpy as np
        B, L, D, N, R = (8, 512, 64, 16, 16)
        A = -jnp.exp(A_log)
        xf = jnp.flip(x, axis=1)
        x_dbl = x @ W_xproj.T
        delta_r, Bf, Bb, C = jnp.split(x_dbl, [R, R + N, R + 2 * N], axis=-1)
        delta = jax.nn.softplus(delta_r @ W_dt.T + b_dt)
        delta_b = jax.nn.softplus(xf @ W_xbproj.T @ W_dt.T + b_dt)
        deltaA = jnp.exp(delta[..., None] * A)
        dBu = delta[..., None] * Bf[..., None, :] * x[..., None] + delta_b[..., None] * Bb[..., None, :] * xf[..., None]

        def step(h, inp):
            dA, du, c = inp
            h = dA * h + du
            return (h, jnp.einsum('bdn,bn->bd', h, c))
        h0 = jnp.zeros((x.shape[0], D, N), x.dtype)
        _, ys = jax.lax.scan(step, h0, (jnp.swapaxes(deltaA, 0, 1), jnp.swapaxes(dBu, 0, 1), jnp.swapaxes(C, 0, 1)))
        y = jnp.swapaxes(ys, 0, 1)
        y = y + x * D_skip + xf * D_skip
        return y @ W_out.T

    def _L0_ffn_ref(x, ln1_w, ln2_w, wq, wk, wv, wo, router_w, w1, w2, w3):
        import jax, jax.numpy as jnp
        import numpy as np
        B, T, C = (64, 96, 64)
        NH, NKV = (4, 2)
        HD = C // NH
        NREP = NH // NKV
        NE, TOPK = (8, 2)
        HID = int(8 / 3 * C)
        EPS_RMS = 1e-06

        def _rope_tables(t_len):
            inv_freq = 1.0 / 10000.0 ** (np.arange(0, HD, 2, dtype=np.float32) / HD)
            t = np.arange(t_len, dtype=np.float32)
            freqs = np.outer(t, inv_freq)
            emb = np.concatenate([freqs, freqs], axis=-1)
            return (jnp.asarray(np.cos(emb)), jnp.asarray(np.sin(emb)))

        def _rotate_half(x):
            h = x.shape[-1] // 2
            return jnp.concatenate([-x[..., h:], x[..., :h]], axis=-1)

        def _rmsnorm(v, w):
            return v * jax.lax.rsqrt(jnp.mean(v * v, axis=-1, keepdims=True) + EPS_RMS) * w
        Bx, Tx, Cx = x.shape
        h = _rmsnorm(x, ln1_w)
        q = (h @ wq.T).reshape(Bx, Tx, NH, HD).transpose(0, 2, 1, 3)
        k = (h @ wk.T).reshape(Bx, Tx, NKV, HD).transpose(0, 2, 1, 3)
        v = (h @ wv.T).reshape(Bx, Tx, NKV, HD).transpose(0, 2, 1, 3)
        cos, sin = _rope_tables(Tx)
        cos, sin = (cos[None, None], sin[None, None])
        q = q * cos + _rotate_half(q) * sin
        k = k * cos + _rotate_half(k) * sin
        k = jnp.repeat(k, NREP, axis=1)
        v = jnp.repeat(v, NREP, axis=1)
        scores = jnp.einsum('bhtd,bhsd->bhts', q, k) / jnp.sqrt(jnp.float32(HD))
        causal = jnp.tril(jnp.ones((Tx, Tx), dtype=bool))
        scores = jnp.where(causal[None, None], scores, jnp.float32(-1e+30))
        att = jax.nn.softmax(scores, axis=-1)
        y = jnp.einsum('bhts,bhsd->bhtd', att, v).transpose(0, 2, 1, 3).reshape(Bx, Tx, Cx)
        x = x + y @ wo.T
        flat = _rmsnorm(x, ln2_w).reshape(-1, Cx)
        probs = jax.nn.softmax(flat @ router_w.T, axis=-1)
        tp, ti = jax.lax.top_k(probs, TOPK)
        tp = tp / (jnp.sum(tp, axis=-1, keepdims=True) + 1e-09)
        weights = jnp.sum(tp[..., None] * jax.nn.one_hot(ti, NE, dtype=flat.dtype), axis=1)
        out = jnp.zeros_like(flat)
        for e in range(NE):
            hh = jax.nn.silu(flat @ w1[e].T) * (flat @ w3[e].T)
            out = out + weights[:, e:e + 1] * (hh @ w2[e].T)
        return x + out.reshape(Bx, Tx, Cx)
    h = _L0_tok_ref(x, L0_tok_fc0_w, L0_tok_fc0_b, L0_tok_ln0_g, L0_tok_ln0_b, L0_tok_w1r, L0_tok_w1i, L0_tok_w2r, L0_tok_w2i, L0_tok_conv_w, L0_tok_conv_b, L0_tok_ln_g, L0_tok_ln_b, L0_tok_fc1_w, L0_tok_fc1_b, L0_tok_fc2_w, L0_tok_fc2_b, L0_tok_fc3_w, L0_tok_fc3_b)
    h = jnp.concatenate([jnp.broadcast_to(cls_tok, (h.shape[0], 1, h.shape[2])), h], axis=1)
    h = h + _L0_attn_ref(_layernorm(h, axis=-1), L0_attn_W_xproj, L0_attn_W_xbproj, L0_attn_W_dt, L0_attn_b_dt, L0_attn_A_log, L0_attn_D_skip, L0_attn_W_out)
    h = h + _L0_ffn_ref(_layernorm(h, axis=-1), L0_ffn_ln1_w, L0_ffn_ln2_w, L0_ffn_wq, L0_ffn_wk, L0_ffn_wv, L0_ffn_wo, L0_ffn_router_w, L0_ffn_w1, L0_ffn_w2, L0_ffn_w3)
    return h

_drawn_inputs = setup_inputs


def setup_inputs(seed=0):
    import zlib

    import numpy as np

    out = dict(_drawn_inputs(seed))
    spreads = {'L0_tok_fc0_b': (0.0, 0.1),
     'L0_tok_ln0_g': (1.0, 0.2),
     'L0_tok_ln0_b': (0.0, 0.1),
     'L0_tok_conv_b': (0.0, 0.1),
     'L0_tok_ln_g': (1.0, 0.2),
     'L0_tok_ln_b': (0.0, 0.1),
     'L0_tok_fc1_b': (0.0, 0.1),
     'L0_tok_fc2_b': (0.0, 0.1),
     'L0_attn_D_skip': (1.0, 0.2),
     'L0_ffn_ln1_w': (1.0, 0.6),
     'L0_ffn_ln2_w': (1.0, 0.6)}
    factors = {'L0_tok_w1r': 8.0,
     'L0_tok_w1i': 8.0,
     'L0_tok_w2r': 8.0,
     'L0_tok_w2i': 8.0,
     'L0_attn_W_xbproj': 8.0,
     'L0_attn_W_dt': 8.0,
     'L0_attn_b_dt': 8.0,
     'L0_attn_A_log': 8.0,
     'L0_ffn_wq': 8.0,
     'L0_ffn_wk': 8.0,
     'L0_ffn_wv': 8.0,
     'L0_ffn_wo': 8.0,
     'L0_ffn_router_w': 8.0,
     'L0_ffn_w1': 8.0,
     'L0_ffn_w2': 8.0,
     'L0_ffn_w3': 8.0}
    for name, (base, spread) in spreads.items():
        noise = np.random.default_rng([zlib.crc32(name.encode()), seed]).standard_normal(out[name].shape)
        drawn = base * np.exp(spread * noise) if base else spread * noise
        out[name] = jnp.asarray(drawn.astype(out[name].dtype))
    for name, factor in factors.items():
        out[name] = (out[name] * factor).astype(out[name].dtype)
    return out
```

```python
from contextlib import ExitStack

import concourse.bass as bass
import numpy as np
from concourse import mybir

F32 = mybir.dt.float32
ACT = mybir.ActivationFunctionType
ALU = mybir.AluOpType
AX = mybir.AxisListType

NI = 128
S = 64
C = 32
LAYERS = 4
NK = 13
NY = 12
T26 = 2 * NK
B24 = 2 * NY
PX = 2048
CH = 512
MODE = 4 * C
EPS = 1e-5


def constants():
    x = np.arange(S)
    ang = 2 * np.pi / S
    bx = np.zeros((S, NK, 2))
    by = np.zeros((S, NY, 2))
    for k in range(NK):
        bx[:, k, 0], bx[:, k, 1] = np.cos(ang * k * x), np.sin(ang * k * x)
    for k in range(NY):
        by[:, k, 0], by[:, k, 1] = np.cos(ang * k * x), np.sin(ang * k * x)
    bx, by = bx.reshape(S, T26), by.reshape(S, B24)
    alpha = np.repeat(np.where(np.arange(NY) == 0, 1.0, 2.0) / (S * S), 2)
    t = {}
    t["ident"] = np.eye(128)
    forward = bx.reshape(S, NK, 2).transpose(0, 2, 1).reshape(S, T26)
    t["f1"] = np.kron(np.eye(2), forward)
    t["f2"] = np.kron(by, np.eye(2))
    t["ga"] = np.kron(np.eye(2), bx.T)
    t["gb"] = np.kron((by * alpha).T, np.eye(4))
    t["maskc"] = np.kron(np.eye(4), np.ones((C, C)))
    t["center"] = np.eye(C) - 1.0 / C
    t["center_dc"] = (np.eye(C) - 1.0 / C) * (S * S)
    r = np.zeros((4, 97))
    for p in range(96):
        r[p % 3, p] = 1
    r[3, 96] = 1
    t["rinp"] = r
    m = np.zeros((97, 32))
    for p in range(96):
        m[p, p // 3] = 1
    m[96, :] = 1
    t["maski"] = m
    sign = {(0, 0): {(0, 0): (1, 1), (1, 1): (-1, 1), (0, 1): (1, 1), (1, 0): (1, -1)},
            (1, 1): {(0, 0): (-1, 1), (1, 1): (1, 1), (0, 1): (-1, 1), (1, 0): (-1, -1)},
            (1, 0): {(0, 0): (-1, 1), (1, 1): (1, 1), (0, 1): (1, -1), (1, 0): (1, 1)},
            (0, 1): {(0, 0): (-1, -1), (1, 1): (1, -1), (0, 1): (1, 1), (1, 0): (1, -1)}}
    s = np.zeros((128, 8))
    for q in range(4):
        for row in range(128):
            b, a = row // 64, row % 2
            s[row, 2 * q], s[row, 2 * q + 1] = sign[(q // 2, q % 2)][(a, b)]
    t["sign"] = s
    return {k: v.astype(np.float32) for k, v in t.items()}


def mixing_weights(w1r, w1i, w2r, w2i):
    L = w1r.shape[0]
    out = np.zeros((L, NY, 2, C, 2, 4, NK, C), np.float32)
    for b in range(2):
        for a in range(2):
            for kind in range(2):
                first, second = (w1r, w2r) if (a ^ b ^ kind) == 0 else (w1i, w2i)
                out[:, :, b, :, a, 2 * kind, 0:12, :] = np.transpose(first, (0, 4, 1, 3, 2))
                out[:, :, b, :, a, 2 * kind + 1, 1:13, :] = np.transpose(second, (0, 4, 1, 3, 2))[:, :, :, ::-1, :]
    return out.reshape(L, NY, 128, 4 * NK * C)


def build_tokenizer(nc, io, place, h0, debug=None):
    pairs = NI // 2
    halves = pairs // 2
    with ExitStack() as ctx:
        def sb(name, shape):
            return ctx.enter_context(nc.sbuf_tensor("sb_" + name, shape, F32))

        def sem(name):
            return ctx.enter_context(nc.semaphore(name))

        table = sb("table", [128, max(p[2] for p in place.values())])

        def const(name):
            r, a, b = place[name]
            return table[0:r, a:b]

        act_d = nc.dram_tensor("act_scratch", (pairs, 128, PX), F32).ap()
        x_d = nc.dram_tensor("spectrum_in", (NI, NY, 4 * C * NK), F32).ap()
        y_d = nc.dram_tensor("spectrum_out", (NI, NY, NK, MODE), F32).ap()

        image_in = [sb(f"image_in{p}", [128, 3 * S]) for p in range(2)]
        image_t = sb("image_t", [97, 256])
        fc0_rows = sb("fc0_rows", [4, C])
        fc0_center = sb("fc0_center", [4, C])
        fc0_mean = sb("fc0_mean", [4, 1])
        fc0_rep = sb("fc0_rep", [97, C])
        fc0_block = sb("fc0_block", [97, 32 * C])
        conv_raw = sb("conv_raw", [C, C])
        conv_rep = sb("conv_rep", [C, 128])
        conv_col = sb("conv_col", [128, C])
        conv_block = sb("conv_block", [128, 128])
        bias_raw = sb("bias_raw", [C, 1])
        bias_cols = sb("bias_cols", [C, 128])
        ones = sb("ones", [128, 128])
        gain = sb("gain", [128, 1])
        shift = sb("shift", [128, 1])
        fc1_pad = sb("fc1_pad", [128, 4 * 128])
        fc1_bias = sb("fc1_bias", [128, 1])
        fc2_w = sb("fc2_w", [128, 64])
        fc2_bias = sb("fc2_bias", [128, 1])
        fc3_pad = sb("fc3_pad", [128, 2])
        fc3_bias = sb("fc3_bias", [128, 1])
        act_in = [sb(f"act_in{p}", [128, PX]) for p in range(2)]
        z_in = [sb(f"z_in{p}", [2 * T26, B24 * C]) for p in range(2)]
        v_sb = sb("v_sb", [4 * B24, 1024])
        square = [sb(f"square{p}", [128, CH]) for p in range(2)]
        var = [sb(f"var{p}", [128, 16]) for p in range(2)]
        rstd = [sb(f"rstd{p}", [128, 16]) for p in range(2)]
        minus_half = sb("minus_half", [128, 16])
        eps = sb("eps", [128, 16])
        unit = [sb(f"unit{p}", [128, CH]) for p in range(2)]
        act_out = [sb(f"act_out{p}", [128, PX]) for p in range(2)]
        pix = sb("pix", [128, PX])
        f1_sb = sb("f1_sb", [128, 32 * T26])
        f2_sb = [sb(f"f2_sb{p}", [112, 16 * T26]) for p in range(2)]
        dense1 = [sb(f"dense1_{p}", [128, CH]) for p in range(2)]
        dense2 = [sb(f"dense2_{p}", [128, CH]) for p in range(2)]
        head = [sb(f"head{p}", [128, S]) for p in range(2)]
        w_raw = [sb(f"w_raw{p}", [128, 4 * NK * C]) for p in range(2)]
        w_sum = sb("w_sum", [128, 4 * NK])
        w_cen = [sb(f"w_cen{p}", [128, 4 * NK * C]) for p in range(2)]
        w_neg = sb("w_neg", [128, 4 * NK * C])
        w_mix = [sb(f"w_mix{p}", [128, NK * MODE]) for p in range(2)]
        x_in = [sb(f"x_in{p}", [NI, NK * MODE]) for p in range(2)]
        x_t = [sb(f"x_t{p}", [128, 4 * NI]) for p in range(2)]
        y_sb = [sb(f"y_sb{p}", [NI, NK * MODE]) for p in range(2)]

        H = [ctx.enter_context(nc.psum_tensor(f"H{j}", [128, CH], F32)) for j in range(4)]
        TC = ctx.enter_context(nc.psum_tensor("TC", [128, CH], F32))
        TP = ctx.enter_context(nc.psum_tensor("TP", [128, CH], F32))
        M = [ctx.enter_context(nc.psum_tensor(f"M{j}", [128, CH], F32)) for j in range(2)]

        table_in = sem("table_in")
        param_in = sem("param_in")
        layer_in = sem("layer_in")
        set_up = sem("set_up")
        prep_pe = sem("prep_pe")
        conv_set = sem("conv_set")
        conv_pe = sem("conv_pe")
        ld = [sem(f"pixels_in{p}") for p in range(2)]
        zl = [sem(f"z_loaded{p}") for p in range(2)]
        st_a = [sem(f"act_stored{p}") for p in range(2)]
        st_x = [sem(f"f2_stored{p}") for p in range(2)]
        st_h = [sem(f"head_stored{p}") for p in range(2)]
        a_done = sem("stepA_done")
        v_ready = sem("v_ready")
        h_ready = sem("h_ready")
        sq_ready = sem("sq_ready")
        var_ready = sem("var_ready")
        var_eps = sem("var_eps")
        rstd_ready = sem("rstd_ready")
        unit_ready = sem("unit_ready")
        tc_ready = sem("tc_ready")
        act_ready = sem("act_ready")
        tp_ready = sem("tp_ready")
        pix_ready = sem("pix_ready")
        f1_done = sem("f1_done")
        f1_ready = sem("f1_ready")
        f2_done = sem("f2_done")
        f2_ready = sem("f2_ready")
        w_in = [sem(f"w_in{p}") for p in range(2)]
        x_inq = [sem(f"x_inq{p}") for p in range(2)]
        y_out = [sem(f"y_out{p}") for p in range(2)]
        w_sum_s = sem("w_summed")
        w_cen_s = sem("w_centered")
        w_neg_s = sem("w_signed")
        w_mix_s = sem("w_mixed")
        xt_pe = sem("xt_transposed")
        xt_s = sem("xt_copied")
        y_pe = sem("y_product")
        y_s = sem("y_copied")
        fc1_done = sem("fc1_done")
        fc1_act = sem("fc1_act")
        fc2_done = sem("fc2_done")
        fc2_act = sem("fc2_act")
        fc3_done = sem("fc3_done")
        head_ready = sem("head_ready")

        def at_least(eng, s, n):
            if not isinstance(n, int) or n > 0:
                eng.wait_ge(s, n)

        images = io["x"].rearrange("(n i) h w c -> n (i h) (w c)", i=2)
        y_view = y_d.rearrange("(n i) y k m -> n i k m y", i=2)
        heads = h0.rearrange("(n i) x y -> n (i x) y", i=2)
        x_view = x_d.rearrange("(n i) y m -> n i y m", i=2)
        GROUPS = [(0, 4), (4, 4), (8, 4), (12, 1)]

        def sp_load(e, P, p, n, first):
            if first:
                at_least(e, h_ready, 8 * P + 4 * p - 4)
                e.dma_start(image_in[p][:, :], images[n]).then_inc(ld[p], 16)
                return
            at_least(e, h_ready, 8 * P + 4 * p - 4)
            e.dma_start(act_in[p][:, :], act_d[n]).then_inc(ld[p], 16)
            for i in range(2):
                src = y_d[n * 2 + i].rearrange("y k (a m) -> (k a) y m", a=2)
                e.dma_start(z_in[p][i * T26:(i + 1) * T26, :].rearrange("t (y m) -> t y m", y=NY), src).then_inc(zl[p], 16)

        def sp_store(e, P, p, n, last):
            if last:
                e.wait_ge(head_ready, 8 * (P - 4 * halves) + 4 * p + 4)
                e.dma_start(heads[n], head[p][:, :]).then_inc(st_h[p], 16)
                return
            e.wait_ge(act_ready, 8 * P + 4 * p + 4)
            e.dma_start(act_d[n], act_out[p][:, :]).then_inc(st_a[p], 16)
            e.wait_ge(f2_ready, 2 * P + p + 1)
            for i in range(2):
                e.dma_start(x_d[n * 2 + i].rearrange("y (b m) -> (y b) m", b=4),
                            f2_sb[p][64 * i:64 * i + 48, :]).then_inc(st_x[p], 16)

        def pe_pair(e, P, p, first, last, layer):
            it = 2 * P + p
            g0 = 4 * it
            if first:
                e.wait_ge(ld[p], 16 * (P + 1))
                for u in range(2):
                    at_least(e, (f2_ready, f1_ready)[u], (it, 2 * it)[u])
                    e.transpose(M[u][0:96, 0:128], image_in[p][:, 96 * u:96 * u + 96],
                                const("ident")).then_inc(a_done, 1)
            else:
                e.wait_ge(zl[p], 32 * (P - halves + 1))
                for u in range(2):
                    if u == 0:
                        e.wait_ge(f2_ready, it) if not last else at_least(e, f2_ready, 2 * 4 * halves)
                    else:
                        e.wait_ge(f1_ready, 2 * it) if not last else at_least(e, f1_ready, 4 * 4 * halves)
                    if last:
                        at_least(e, fc1_act, 16 * (it - 8 * halves))
                    for g in range(4):
                        og = 4 * u + g
                        z = z_in[p][:, :].rearrange("t (y g) -> t y g", g=8)[:, :, og]
                        mm = e.matmul(M[u][0:96, 128 * g:128 * g + 128], z, const("ga"), start=True, stop=True)
                    mm.then_inc(a_done, 1)
                e.wait_ge(ld[p], 16 * (P + 1))

            def conv(j):
                if first or not last:
                    at_least(e, unit_ready, g0 + j + 1 - 4)
                else:
                    e.wait_ge(unit_ready, g0 + j + 1 - 4)
                    at_least(e, head_ready, g0 - 16 * halves * 2 + j + 1 - 4)
                if first:
                    return
                if j == 0:
                    e.wait_ge(y_s, 48 * (layer + 1))
                for u in range(4):
                    b = 4 * j + u
                    e.matmul(H[j][:, 128 * u:128 * u + 128], act_in[p][:, 128 * b:128 * b + 128],
                             conv_block[:, :], start=(u == 0), stop=False, skip_group_check=True)

            def spectral(j):
                if first:
                    e.wait_ge(v_ready, 2 * it + 2)
                    e.matmul(H[j][:, :], image_t[:, 128 * (j // 2):128 * (j // 2) + 128],
                             fc0_block[:, 512 * (j % 2):512 * (j % 2) + 512],
                             start=True, stop=True).then_inc(h_ready, 1)
                    return
                e.wait_ge(v_ready, 2 * it + 2)
                for og in range(8):
                    mm = e.matmul(H[j][:, :].rearrange("p (y g) -> p y g", g=8)[:, :, og],
                                  v_sb[:, 128 * og:128 * og + 128], const("gb")[:, 64 * j:64 * j + 64],
                                  start=False, stop=(og == 7), skip_group_check=True)
                mm.then_inc(h_ready, 1)

            def to_channels(j):
                e.wait_ge(unit_ready, g0 + j + 1)
                at_least(e, act_ready, g0 + j)
                for u in range(4):
                    mm = e.transpose(TC[:, 128 * u:128 * u + 128], unit[j % 2][:, 128 * u:128 * u + 128],
                                     const("ident"))
                mm.then_inc(tc_ready, 1)

            def to_pixels(j):
                e.wait_ge(act_ready, g0 + j + 1)
                at_least(e, pix_ready, g0 + j)
                for u in range(4):
                    b = 4 * j + u
                    mm = e.transpose(TP[:, 128 * u:128 * u + 128], act_out[p][:, 128 * b:128 * b + 128],
                                     const("ident"))
                mm.then_inc(tp_ready, 1)

            def dense(j):
                gh = g0 + j - 16 * halves * 2
                for w in range(2):
                    for v in range(2):
                        e.wait_ge(act_ready, g0 + j + 1)
                        at_least(e, fc1_act, 4 * gh + 2 * w + v - 1)
                        e.matmul(M[v][:, :], fc1_pad[:, 128 * (2 * w + v):128 * (2 * w + v) + 128],
                                 act_out[p][:, 512 * j:512 * j + 512], start=True, stop=True).then_inc(fc1_done, 1)
                    for v in range(2):
                        e.wait_ge(fc1_act, 4 * gh + 2 * w + v + 1)
                        if v == 0:
                            at_least(e, fc2_act, 2 * gh + w)
                        mm = e.matmul(TP[64 * v:64 * v + 64, :], fc2_w[:, :], dense1[v][:, :], start=True, stop=True,
                                      skip_group_check=True)
                    mm.then_inc(fc2_done, 1)
                    e.wait_ge(fc2_act, 2 * gh + w + 1)
                    for u in range(4):
                        mm = e.matmul(H[j][:, 4 * u + 2 * w:4 * u + 2 * w + 2],
                                      dense2[w][:, 128 * u:128 * u + 128], fc3_pad[:, :],
                                      start=True, stop=True, skip_group_check=True)
                mm.then_inc(fc3_done, 1)

            conv(0)
            conv(1)
            spectral(0)
            spectral(1)
            to_channels(0)
            conv(2)
            spectral(2)
            to_channels(1)
            if last:
                dense(0)
            else:
                to_pixels(0)
            conv(3)
            spectral(3)
            to_channels(2)
            if last:
                dense(1)
            else:
                to_pixels(1)
            to_channels(3)
            if last:
                dense(2)
                dense(3)
                return
            to_pixels(2)
            to_pixels(3)
            e.wait_ge(pix_ready, g0 + 4)
            for u in range(2):
                for g in range(8):
                    cp = 8 * u + g
                    cols = pix[:, :].rearrange("p (y h c) -> p y h c", h=2, c=16)[:, :, :, cp]
                    mm = e.matmul(M[u][:, 52 * g:52 * g + 52], cols, const("f1"), start=True, stop=True)
                mm.then_inc(f1_done, 1)
            e.wait_ge(f1_ready, 2 * it + 2)
            for i in range(2):
                src = f1_sb[:, :].rearrange("p (c i t) -> p c i t", c=16, i=2)[:, :, i, :]
                mm = e.matmul(M[0][64 * i:64 * i + 48, 0:16 * T26], const("f2"), src, start=True, stop=True,
                              skip_group_check=True)
            mm.then_inc(f2_done, 1)

        def act_pair(e, P, p, first, last):
            it = 2 * P + p
            g0 = 4 * it
            gelu = ACT.Identity if (first or last) else ACT.Gelu
            for u in range(2):
                if first:
                    e.wait_ge(a_done, 2 * it + u + 1)
                    e.activation(image_t[0:96, 128 * u:128 * u + 128], M[u][0:96, 0:128],
                                 ACT.Copy).then_inc(v_ready, 1)
                else:
                    e.wait_ge(a_done, 2 * it + u + 1)
                    e.activation(v_sb[:, 512 * u:512 * u + 512], M[u][0:96, :], ACT.Copy).then_inc(v_ready, 1)

            def squares(j):
                e.wait_ge(h_ready, g0 + j + 1)
                at_least(e, var_ready, g0 + j - 1)
                e.activation(square[j % 2][:, :], H[j][:, :], ACT.Square, scale=float(C) ** -0.5).then_inc(sq_ready, 1)

            def gelus(j):
                e.wait_ge(tc_ready, g0 + j + 1)
                if not last and j == 0:
                    at_least(e, st_a[p], 16 * P)
                e.activation(act_out[p][:, 512 * j:512 * j + 512], TC[:, :], gelu, bias=shift[:, 0:1],
                             scale=gain[:, 0:1]).then_inc(act_ready, 1)

            def dense(j):
                gh = g0 + j - 16 * halves * 2
                for w in range(2):
                    for v in range(2):
                        e.wait_ge(fc1_done, 4 * gh + 2 * w + v + 1)
                        at_least(e, fc2_done, 2 * gh + w)
                        e.activation(dense1[v][:, :], M[v][:, :], ACT.Gelu, bias=fc1_bias[:, 0:1],
                                     scale=1.0).then_inc(fc1_act, 1)
                    e.wait_ge(fc2_done, 2 * gh + w + 1)
                    at_least(e, fc3_done, gh)
                    e.activation(dense2[w][:, :], TP[:, :], ACT.Gelu, bias=fc2_bias[:, 0:1],
                                 scale=1.0).then_inc(fc2_act, 1)

            squares(0)
            squares(1)
            gelus(0)
            squares(2)
            gelus(1)
            if last:
                dense(0)
            squares(3)
            gelus(2)
            if last:
                dense(1)
            gelus(3)
            if last:
                dense(2)
                dense(3)
                return
            for u in range(2):
                e.wait_ge(f1_done, 2 * it + u + 1)
                e.activation(f1_sb[:, 416 * u:416 * u + 416], M[u][:, 0:416], ACT.Copy).then_inc(f1_ready, 1)

        def dve_pair(e, P, p, first, last):
            it = 2 * P + p
            g0 = 4 * it

            def normal(j):
                e.wait_ge(sq_ready, g0 + j + 1)
                e.tensor_reduce(var[j % 2][:, :], square[j % 2][:, :].rearrange("p (y c) -> p y c", c=C), AX.X,
                                ALU.add).then_inc(var_ready, 1)
                e.wait_ge(rstd_ready, g0 + j + 1)
                at_least(e, tc_ready, g0 + j - 1)
                e.tensor_tensor(unit[j % 2][:, :].rearrange("p (y c) -> p y c", c=C),
                                H[j][:, :].rearrange("p (y c) -> p y c", c=C),
                                rstd[j % 2][:, :].unsqueeze(2).to_broadcast([128, 16, C]), ALU.mult).then_inc(unit_ready, 1)

            def pixels(j):
                e.wait_ge(tp_ready, g0 + j + 1)
                e.tensor_copy(pix[:, 512 * j:512 * j + 512], TP[:, :]).then_inc(pix_ready, 1)

            def heads_out(j):
                gh = g0 + j - 16 * halves * 2
                e.wait_ge(fc3_done, gh + 1)
                if j == 0:
                    at_least(e, st_h[p], 16 * (P - 4 * halves))
                e.tensor_scalar(head[p][:, 16 * j:16 * j + 16], H[j][:, 0:16], fc3_bias[:, 0:1], None,
                                ALU.add).then_inc(head_ready, 1)

            normal(0)
            normal(1)
            if last:
                normal(2)
                heads_out(0)
                normal(3)
                for j in range(1, 4):
                    heads_out(j)
                return
            normal(2)
            pixels(0)
            normal(3)
            for j in range(1, 4):
                pixels(j)
            e.wait_ge(f2_done, it + 1)
            at_least(e, st_x[p], 32 * P)
            for i in range(2):
                cp = e.tensor_copy(f2_sb[p][64 * i:64 * i + 48, :], M[0][64 * i:64 * i + 48, 0:16 * T26])
            cp.then_inc(f2_ready, 1)

        def pool_pair(e, P, p):
            g0 = 8 * P + 4 * p
            for j in range(4):
                e.wait_ge(var_ready, g0 + j + 1)
                e.tensor_tensor(var[j % 2][:, :], var[j % 2][:, :], eps[:, :], ALU.add).then_inc(var_eps, 1)
                e.wait_ge(var_eps, g0 + j + 1)
                e.tensor_tensor(rstd[j % 2][:, :], var[j % 2][:, :], minus_half[:, :], ALU.pow).then_inc(rstd_ready, 1)

        def since(eng, s, before, n):
            if not isinstance(n, int) or n > 0:
                eng.wait_ge(s, before + n)

        def sp_mix_load(e, m, p, layer):
            q, ky = 2 * m + p, 2 * m + p
            since(e, w_cen_s, NY * layer, q - 1)
            e.dma_start(w_raw[p][:, :], io["w_mix"][layer, ky]).then_inc(w_in[p], 16)
            since(e, xt_pe, 4 * NY * layer, 4 * (q - 1))
            e.dma_start(x_in[p][:, :], x_d[:, ky, :]).then_inc(x_inq[p], 16)

        def sp_mix_store(e, m, p, layer):
            ky = 2 * m + p
            e.wait_ge(y_s, 4 * NY * layer + 4 * ky + 4)
            e.dma_start(y_d[:, ky, :, :], y_sb[p][:, :].rearrange("n (k m) -> n k m", k=NK)).then_inc(y_out[p], 16)

        def pe_mix(e, m, p, layer, zero):
            q, q0 = 2 * m + p, NY * layer
            e.wait_ge(x_inq[p], 16 * (NY // 2 * layer + m + 1))
            xv = x_in[p][:, :].rearrange("n (m k) -> n m k", k=NK)

            def turn(s):
                k0, n = GROUPS[s]
                since(e, xt_s, 4 * q0, 4 * q + s - 1)
                for k in range(k0, k0 + n):
                    mm = e.transpose(H[s % 2][:, NI * (k - k0):NI * (k - k0) + NI], xv[:, :, k],
                                     const("ident")[0:NI, 0:NI])
                mm.then_inc(xt_pe, 1)

            turn(0)
            for s, (k0, n) in enumerate(GROUPS):
                if s < 3:
                    turn(s + 1)
                e.wait_ge(xt_s, 4 * (q0 + q) + s + 1)
                e.wait_ge(w_mix_s, 4 * (q0 + q) + 4)
                since(e, y_s, 4 * q0, 4 * q + s - 1)
                for k in range(k0, k0 + n):
                    dc = zero and k == 0
                    mm = e.matmul(H[2 + s % 2][0:NI, 128 * (k - k0):128 * (k - k0) + 128],
                                  x_t[s % 2][:, NI * (k - k0):NI * (k - k0) + NI],
                                  w_mix[p][:, 128 * k:128 * k + 128], start=True, stop=not dc, skip_group_check=True)
                    if dc:
                        mm = e.matmul(H[2][0:NI, 0:C], bias_cols[:, 0:NI], const("center_dc"),
                                      start=False, stop=True, skip_group_check=True)
                mm.then_inc(y_pe, 1)

        def act_mix(e, m, p, layer):
            q, q0 = 2 * m + p, NY * layer

            def turned(s):
                n = GROUPS[s][1]
                e.wait_ge(xt_pe, 4 * (q0 + q) + s + 1)
                since(e, y_pe, 4 * q0, 4 * q + s - 1)
                e.activation(x_t[s % 2][:, 0:NI * n], H[s % 2][:, 0:NI * n], ACT.Copy).then_inc(xt_s, 1)

            turned(0)
            for s, (k0, n) in enumerate(GROUPS):
                if s < 3:
                    turned(s + 1)
                e.wait_ge(y_pe, 4 * (q0 + q) + s + 1)
                if s == 0:
                    since(e, y_out[p], 16 * (NY // 2) * layer, 16 * m)
                e.activation(y_sb[p][:, 128 * k0:128 * (k0 + n)], H[2 + s % 2][0:NI, 0:128 * n],
                             ACT.Copy).then_inc(y_s, 1)

        def dve_mix(e, m, p, layer):
            q, q0 = 2 * m + p, NY * layer
            e.wait_ge(w_in[p], 16 * (NY // 2 * layer + m + 1))
            raw = w_raw[p][:, :].rearrange("r (k o) -> r k o", o=C)
            e.tensor_reduce(w_sum[:, :], raw, AX.X, ALU.add).then_inc(w_sum_s, 1)
            e.wait_ge(w_sum_s, q0 + q + 1)
            since(e, w_neg_s, 4 * q0, 4 * (q - 1))
            e.scalar_tensor_tensor(out=w_cen[p][:, :].rearrange("r (k o) -> r k o", o=C),
                                   in0=w_sum[:, :].unsqueeze(2).to_broadcast([128, 4 * NK, C]), scalar=-1.0 / C,
                                   in1=raw, op0=ALU.mult, op1=ALU.add).then_inc(w_cen_s, 1)
            e.wait_ge(w_cen_s, q0 + q + 1)
            since(e, y_pe, 4 * q0, 4 * (q - 1))
            for s in range(4):
                kind = 2 * (1 if s in (1, 2) else 0)
                e.wait_ge(w_neg_s, 4 * (q0 + q) + s + 1)
                e.scalar_tensor_tensor(
                    out=w_mix[p][:, :].rearrange("r (k s o) -> r k s o", k=NK, s=4)[:, :, s, :],
                    in0=w_cen[p][:, NK * C * kind:NK * C * (kind + 1)].rearrange("r (k o) -> r k o", o=C),
                    scalar=const("sign")[:, 2 * s:2 * s + 1],
                    in1=w_neg[:, NK * C * s:NK * C * (s + 1)].rearrange("r (k o) -> r k o", o=C),
                    op0=ALU.mult, op1=ALU.add).then_inc(w_mix_s, 1)

        def pool_mix(e, m, p, layer):
            q, q0 = 2 * m + p, NY * layer
            e.wait_ge(w_cen_s, q0 + q + 1)
            for s in range(4):
                kind = 2 * (1 if s in (1, 2) else 0) + 1
                since(e, w_mix_s, 4 * q0, 4 * (q - 1) + s + 1)
                e.tensor_tensor(w_neg[:, NK * C * s:NK * C * (s + 1)], w_cen[p][:, NK * C * kind:NK * C * (kind + 1)],
                                const("sign")[:, 2 * s + 1:2 * s + 2].to_broadcast([128, NK * C]),
                                ALU.mult).then_inc(w_neg_s, 1)

        def sp_layer(e, n, layer, norm):
            if layer is not None:
                e.dma_start(conv_raw[:, :], io["conv_w"][layer]).then_inc(layer_in, 16)
                e.dma_start(bias_raw[:, :], io["conv_b"][layer].unsqueeze(1)).then_inc(layer_in, 16)
            g, b = norm
            for u in range(4):
                if layer is not None and u < 2:
                    e.wait_ge(st_a[u], 16 * halves * (layer + 1))
                elif layer is not None:
                    e.wait_ge(st_x[u - 2], 32 * halves * (layer + 1))
                e.dma_start(gain[32 * u:32 * u + 32, :], g.unsqueeze(1)).then_inc(layer_in, 16)
                e.dma_start(shift[32 * u:32 * u + 32, :], b.unsqueeze(1)).then_inc(layer_in, 16)

        def dve_layer(e, n):
            e.wait_ge(layer_in, 128 + 160 * (n + 1))
            e.tensor_copy(conv_rep[:, :].rearrange("o (g c) -> o g c", g=4),
                          conv_raw[:, :].unsqueeze(1).to_broadcast([C, 4, C])).then_inc(conv_set, 1)
            e.tensor_scalar(bias_cols[:, :], ones[0:C, :], bias_raw[:, 0:1], None, ALU.mult).then_inc(conv_set, 1)
            e.wait_ge(conv_pe, n + 1)
            e.tensor_copy(conv_col[:, :], TP[:, 0:C]).then_inc(conv_set, 1)
            e.wait_ge(conv_set, 4 * n + 3)
            e.tensor_tensor(conv_block[:, :].rearrange("p (g o) -> p g o", g=4),
                            const("maskc").rearrange("p (g o) -> p g o", g=4),
                            conv_col[:, :].unsqueeze(1).to_broadcast([128, 4, C]), ALU.mult).then_inc(conv_set, 1)

        def pe_layer(e, n):
            e.wait_ge(conv_set, 4 * n + 2)
            e.matmul(TP[:, 0:C], conv_rep[:, :], const("center"), start=True, stop=True).then_inc(conv_pe, 1)
            e.wait_ge(conv_set, 4 * n + 4)

        def whole_pass(fori, start, pair, first, last):
            m0 = 0
            if isinstance(start, int):
                pair(start, 0, first, last)
                pair(start, 1, first, last)
                m0 = 1
            with fori(m0, halves) as m:
                pair(start + m, 0, first, last)
                pair(start + m, 1, first, last)

        block = ctx.enter_context(nc.Block())

        @block.sync
        def _(e):
            fori = e.Fori
            e.dma_start(table[:, :], io["tables"]).then_inc(table_in, 16)
            e.dma_start(fc0_rows[0:3, :], io["fc0_w"]).then_inc(param_in, 16)
            e.dma_start(fc0_rows[3:4, :], io["fc0_b"].unsqueeze(0)).then_inc(param_in, 16)
            e.wait_ge(set_up, 5)
            for g in range(4):
                e.dma_start(fc1_pad[32 * g:32 * g + 32, 128 * g:128 * g + 128], io["fc1_w"]).then_inc(param_in, 16)
            e.dma_start(fc1_bias[:, :], io["fc1_b"].unsqueeze(1)).then_inc(param_in, 16)
            e.dma_start(fc2_w[:, :], io["fc2_w"]).then_inc(param_in, 16)
            for g in range(2):
                e.dma_start(fc2_bias[64 * g:64 * g + 64, :], io["fc2_b"].unsqueeze(1)).then_inc(param_in, 16)
                e.dma_start(fc3_pad[64 * g:64 * g + 64, g:g + 1], io["fc3_w"]).then_inc(param_in, 16)
            e.dma_start(fc3_bias[:, :], io["fc3_b"].partition_broadcast(128)).then_inc(param_in, 16)
            sp_layer(e, 0, None, (io["ln0_g"], io["ln0_b"]))

            def one_pass(first, last, start):
                base = start
                if first:
                    for p in range(2):
                        sp_load(e, 0, p, p, True)
                    if halves > 1:
                        sp_step(first, last, base, 0)
                    if halves > 2:
                        with fori(1, halves - 1) as m:
                            sp_step(first, last, base, m)
                else:
                    for p in range(2):
                        sp_load(e, base, p, p, False)
                    if halves > 1:
                        with fori(0, halves - 1) as m:
                            sp_step(first, last, base, m)
                for p in range(2):
                    sp_store(e, base + halves - 1, p, 2 * (halves - 1) + p, last)

            def sp_step(first, last, base, m):
                for p in range(2):
                    sp_load(e, base + m + 1, p, 2 * (m + 1) + p, first)
                    sp_store(e, base + m, p, 2 * m + p, last)

            def mix(layer):
                for p in range(2):
                    sp_mix_load(e, 0, p, layer)
                with fori(0, NY // 2 - 1) as m:
                    for p in range(2):
                        sp_mix_load(e, m + 1, p, layer)
                        sp_mix_store(e, m, p, layer)
                for p in range(2):
                    sp_mix_store(e, NY // 2 - 1, p, layer)

            def layer_body(layer, last):
                e.wait_ge(act_ready, 8 * halves * (layer + 1))
                sp_layer(e, layer + 1, layer, (io["ln_g"][layer], io["ln_b"][layer]))
                mix(layer)
                for p in range(2):
                    e.wait_ge(y_out[p], 16 * (NY // 2) * (layer + 1))
                one_pass(False, last, halves * (layer + 1))

            one_pass(True, False, 0)
            with fori(0, LAYERS - 1) as layer:
                layer_body(layer, False)
            layer_body(LAYERS - 1, True)
            for p in range(2):
                e.wait_ge(st_h[p], 16 * halves)

        @block.tensor
        def _(e):
            fori = e.Fori
            e.wait_ge(table_in, 16)
            e.wait_ge(set_up, 5)
            e.matmul(TP[0:97, 0:C], const("rinp"), fc0_center[:, :], start=True, stop=True).then_inc(prep_pe, 1)
            e.wait_ge(set_up, 7)
            whole_pass(fori, 0, lambda P, p, f, l: pe_pair(e, P, p, f, l, None), True, False)

            def body(layer, last):
                e.wait_ge(h_ready, 8 * halves * (layer + 1))
                e.wait_ge(pix_ready, 8 * halves * (layer + 1))
                e.wait_ge(unit_ready, 8 * halves * (layer + 1))
                pe_layer(e, layer)
                for p in range(2):
                    pe_mix(e, 0, p, layer, p == 0)
                with fori(1, NY // 2) as m:
                    for p in range(2):
                        pe_mix(e, m, p, layer, False)
                if last:
                    e.wait_ge(param_in, 16 * 13)
                whole_pass(fori, halves * (layer + 1),
                           lambda P, p, f, l: pe_pair(e, P, p, f, l, layer), False, last)

            with fori(0, LAYERS - 1) as layer:
                body(layer, False)
            body(LAYERS - 1, True)

        @block.scalar
        def _(e):
            fori = e.Fori
            e.wait_ge(layer_in, 128)
            e.wait_ge(set_up, 3)
            pair = lambda P, p, f, l: act_pair(e, P, p, f, l)
            whole_pass(fori, 0, pair, True, False)

            def body(layer, last):
                for p in range(2):
                    act_mix(e, 0, p, layer)
                with fori(1, NY // 2) as m:
                    for p in range(2):
                        act_mix(e, m, p, layer)
                e.wait_ge(layer_in, 128 + 160 * (layer + 1))
                if last:
                    e.wait_ge(param_in, 16 * 13)
                whole_pass(fori, halves * (layer + 1), pair, False, last)

            with fori(0, LAYERS - 1) as layer:
                body(layer, False)
            body(LAYERS - 1, True)

        @block.vector
        def _(e):
            fori = e.Fori
            e.memset(fc1_pad[:, :], 0.0).then_inc(set_up, 1)
            e.memset(fc3_pad[:, :], 0.0).then_inc(set_up, 1)
            e.memset(image_t[96:97, :], 1.0).then_inc(set_up, 1)
            e.memset(ones[:, :], 1.0)
            e.memset(minus_half[:, :], -0.5)
            e.memset(eps[:, :], EPS)
            e.wait_ge(param_in, 32)
            e.tensor_reduce(fc0_mean[:, :], fc0_rows[:, :], AX.X, ALU.add).then_inc(set_up, 1)
            e.wait_ge(set_up, 4)
            e.scalar_tensor_tensor(out=fc0_center[:, :], in0=fc0_mean[:, 0:1].to_broadcast([4, C]), scalar=-1.0 / C,
                                   in1=fc0_rows[:, :], op0=ALU.mult, op1=ALU.add).then_inc(set_up, 1)
            e.wait_ge(prep_pe, 1)
            e.tensor_copy(fc0_rep[:, :], TP[0:97, 0:C]).then_inc(set_up, 1)
            e.wait_ge(set_up, 6)
            e.tensor_tensor(fc0_block[:, :].rearrange("p (y c) -> p y c", c=C),
                            const("maski").unsqueeze(2).to_broadcast([97, 32, C]),
                            fc0_rep[:, :].unsqueeze(1).to_broadcast([97, 32, C]), ALU.mult).then_inc(set_up, 1)
            pair = lambda P, p, f, l: dve_pair(e, P, p, f, l)
            whole_pass(fori, 0, pair, True, False)

            def body(layer, last):
                dve_layer(e, layer)
                for p in range(2):
                    dve_mix(e, 0, p, layer)
                with fori(1, NY // 2) as m:
                    for p in range(2):
                        dve_mix(e, m, p, layer)
                if last:
                    e.wait_ge(param_in, 16 * 13)
                whole_pass(fori, halves * (layer + 1), pair, False, last)

            with fori(0, LAYERS - 1) as layer:
                body(layer, False)
            body(LAYERS - 1, True)

        @block.gpsimd
        def _(e):
            fori = e.Fori
            e.wait_ge(set_up, 7)
            pair = lambda P, p, f, l: pool_pair(e, P, p)
            whole_pass(fori, 0, pair, True, False)

            def body(layer, last):
                for p in range(2):
                    pool_mix(e, 0, p, layer)
                with fori(1, NY // 2) as m:
                    for p in range(2):
                        pool_mix(e, m, p, layer)
                whole_pass(fori, halves * (layer + 1), pair, False, last)

            with fori(0, LAYERS - 1) as layer:
                body(layer, False)
            body(LAYERS - 1, True)

T = S + 1
D = S
NS = 16
R = 16
NH, HD, NKV = 4, 16, 2
NE = 8
HID = 170
HH = HID // 2
Q = 4
GI = 2 * Q
TOK = Q * T


def block_tables():
    t = {}
    t["ident"] = np.eye(128)
    t["mean"] = np.kron(np.eye(2), np.full((D, D), 1.0 / D))
    rot = np.zeros((HD, HD))
    for j in range(HD // 2):
        rot[j, j + HD // 2] = -1
        rot[j + HD // 2, j] = 1
    t["rot"] = np.kron(np.eye(2 * NH), rot).T
    inv = 1.0 / 10000.0 ** (np.arange(0, HD, 2, dtype=np.float32) / HD)
    freqs = np.outer(np.arange(T, dtype=np.float32), inv)
    emb = np.concatenate([freqs, freqs], axis=-1)
    t["cos"] = np.tile(np.cos(emb).T, (2 * NH, 1))
    t["sin"] = np.tile(np.sin(emb).T, (2 * NH, 1))
    t["heads"] = np.tile(np.kron(np.eye(NH), np.ones((HD, 1))), (2, 1)) * HD ** -0.5
    t["causal"] = np.where(np.tril(np.ones((T, T), bool)), 0.0, -1e30)
    t["order"] = np.tile((NE - np.arange(NE))[None, :], (T, 1))
    return {k: v.astype(np.float32) for k, v in t.items()}


def pack(tables):
    at, place, cols = 0, {}, []
    for name, v in tables.items():
        v = np.asarray(v)
        block = np.zeros((128, v.shape[1]), np.float32)
        block[:v.shape[0]] = v
        place[name] = (v.shape[0], at, at + v.shape[1])
        cols.append(block)
        at += v.shape[1]
    return np.concatenate(cols, axis=1), place


def twice(w):
    out = np.zeros((2, w.shape[0], 2, w.shape[1]), np.float32)
    out[0, :, 0], out[1, :, 1] = w, w
    return out.reshape(2 * w.shape[0], 2 * w.shape[1])


def stacked(w):
    return np.concatenate([w, w], axis=0)


def block_weights(a):
    t = {}
    wx = np.asarray(a["L0_attn_W_xproj"])
    wf = np.zeros((D, D), np.float32)
    wf[:, 0:3 * NS] = wx[R:].T
    t["wx"] = twice(wf)
    t["wxr"] = twice(wx[:R])
    t["wxb"] = twice(np.asarray(a["L0_attn_W_xbproj"]))
    t["wdt"] = twice(np.asarray(a["L0_attn_W_dt"]).T)
    t["b_dt"] = stacked(np.asarray(a["L0_attn_b_dt"])[:, None])
    t["a_log"] = stacked(np.asarray(a["L0_attn_A_log"]))
    t["d_skip"] = stacked(np.asarray(a["L0_attn_D_skip"])[:, None])
    t["wout"] = twice(np.asarray(a["L0_attn_W_out"]).T)
    t["ln1"] = stacked(np.asarray(a["L0_ffn_ln1_w"])[:, None])
    t["ln2"] = stacked(np.asarray(a["L0_ffn_ln2_w"])[:, None])
    wq = np.asarray(a["L0_ffn_wq"])
    wk = np.repeat(np.asarray(a["L0_ffn_wk"]).reshape(NKV, 1, HD, D), NH // NKV, axis=1).reshape(D, D)
    wv = np.repeat(np.asarray(a["L0_ffn_wv"]).reshape(NKV, 1, HD, D), NH // NKV, axis=1).reshape(D, D)
    t["wq_t"], t["wq"] = twice(wq.T), twice(wq)
    t["wk_t"], t["wk"] = twice(wk.T), twice(wk)
    t["wv"] = twice(wv.T)
    t["wo"] = twice(np.asarray(a["L0_ffn_wo"]).T)
    t["router"] = twice(np.asarray(a["L0_ffn_router_w"]).T)
    t["cls"] = stacked(np.asarray(a["cls_tok"]).reshape(D, 1))
    for n in ("w1", "w3"):
        t[n] = stacked(np.transpose(np.asarray(a["L0_ffn_" + n]), (2, 0, 1)).reshape(D, NE * HID))
    w2 = np.transpose(np.asarray(a["L0_ffn_w2"]), (2, 0, 1)).reshape(2, HH, NE, D)
    t["w2"] = np.transpose(w2, (1, 2, 0, 3)).reshape(HH, NE * 2 * D)
    return t


def build_block(nc, io, tplace, wplace, h0, out):
    groups = NI // GI
    with ExitStack() as ctx:
        def sb(name, shape):
            return ctx.enter_context(nc.sbuf_tensor("blk_" + name, shape, F32))

        def sem(name):
            return ctx.enter_context(nc.semaphore("b_" + name))

        tables = sb("tables", [128, max(p[2] for p in tplace.values())])
        weights = sb("weights", [128, max(p[2] for p in wplace.values())])

        def const(name):
            r, a, b = tplace[name]
            return tables[0:r, a:b]

        def wt(name):
            r, a, b = wplace[name]
            return weights[0:r, a:b]

        w_delta = sb("w_delta", [128, 128])
        w_delta_b = sb("w_delta_b", [128, 128])
        wq_rot = sb("wq_rot", [128, 128])
        wk_rot = sb("wk_rot", [128, 128])
        wskip = sb("wskip", [128, 128])
        neg_a = sb("neg_a", [128, NS])
        select = sb("select", [128, 3 * NS * 128])
        rows = sb("rows", [S, GI * D])
        h_in = sb("h_in", [128, TOK])
        cen = sb("cen", [128, TOK])
        sqr = sb("sqr", [128, TOK])
        log = sb("log", [128, TOK])
        ve = sb("ve", [128, TOK])
        y0 = sb("y0", [128, TOK])
        y1 = sb("y1", [128, TOK])
        rs = sb("rs", [128, TOK])
        xn = sb("xn", [128, TOK])
        xf = sb("xf", [128, TOK])
        mag = [sb(f"mag{k}", [128, TOK]) for k in range(2)]
        soft = [sb(f"soft{k}", [128, TOK]) for k in range(2)]
        pos = [sb(f"pos{k}", [128, TOK]) for k in range(2)]
        delta = [sb(f"delta{k}", [128, TOK]) for k in range(2)]
        du = sb("du", [128, TOK])
        dub = sb("dub", [128, TOK])
        bc = sb("bc", [128, TOK])
        dA = sb("dA", [128, NS * TOK])
        dB = sb("dB", [128, NS * TOK])
        dB2 = [sb(f"dB2_{p}", [128, TOK]) for p in range(2)]
        h1 = sb("h1", [128, TOK])
        r = sb("r", [128, TOK])
        un = sb("un", [128, TOK])
        qf = sb("qf", [128, TOK])
        kf = sb("kf", [128, TOK])
        tmp = sb("tmp", [128, TOK])
        kx = dA[:, 0:Q * NH * T]
        sc = dB[0:T, 0:GI * NH * T]
        pt = [sb(f"pt{p}", [T, NH * T]) for p in range(2)]
        v_sb = sb("v", [T, GI * D])
        mx = sb("mx", [T, GI * NH])
        sm = sb("sm", [T, GI * NH])
        rc = sb("rc", [T, GI * NH])
        yn = sb("yn", [T, GI * D])
        yt = sb("yt", [128, TOK])
        x2 = sb("x2", [128, TOK])
        lg = [sb(f"lg{k}", [T, GI * NE]) for k in range(6)]
        st = [sb(f"st{k}", [T, GI]) for k in range(6)]
        silu = [sb(f"silu{p}", [HH, TOK]) for p in range(2)]
        hid = [[sb(f"hid{p}{k}", [HH, TOK]) for k in range(4)] for p in range(2)]
        acc = [sb(f"acc{p}", [T, GI * D]) for p in range(2)]
        part = sb("part", [T, GI * D])
        res = sb("res", [128, TOK])
        fin = sb("fin", [T, GI * D])
        B = [ctx.enter_context(nc.psum_tensor(f"bank{j}", [128, 512], F32)) for j in range(8)]

        PER = dict(
            rows_t=1, h_in=2, mean=2, cen=2, square=4, variance=4, var_eps=4, log=4, guess=4, newton=12, scale=4,
            normed=4, flipped=1, proj=1, soft_mag=2, soft_exp=2, soft_log=2, soft_pos=2, delta=2, du=2, bc=1,
            decay=NS, reset=1, bcast=NS, drive=NS, input=NS, scan=1, c_cast=NS, read=NS, scan_out=1, h1=1,
            qk=1, v=1, v_copied=1, rope=6, kx=Q, scores=GI, masked=GI, peak=1, shifted=1, expd=1, total=1, recip=1,
            p_turned=GI, p_copied=GI, yv=1, y_norm=1, y_turned=1, y_copied=1, wo=1, x2=1, router=1, gate=21,
            gate_exp=1, up=4 * NE, silu=4 * NE, hidden=4 * NE, down=NE, gated=NE, summed=NE, residual=1, res_turned=1,
            fin=1)
        sig = {name: sem(name) for name in PER}
        loaded = sem("weights_loaded")
        rows_in = sem("rows_in")
        stored = sem("stored")
        prep = sem("prepared")
        prep_pe = sem("prepared_pe")
        prep_act = sem("prepared_act")

        def wait(e, name, g, c=None):
            e.wait_ge(sig[name], PER[name] * g + (PER[name] if c is None else c))

        def by_token(ap):
            return ap.rearrange("p (q t) -> p q t", t=T)

        h0_rows = h0.rearrange("(g m) x y -> g x m y", m=GI)
        out_rows = out.rearrange("(g m) t d -> g t m d", m=GI)
        IMAGES = [(q, i) for q in range(Q) for i in range(2)]
        block = ctx.enter_context(nc.Block())

        @block.sync
        def _(e):
            e.dma_start(tables[:, :], io["block_tables"]).then_inc(loaded, 16)
            e.dma_start(weights[:, :], io["block_weights"]).then_inc(loaded, 16)

            def load(g):
                e.dma_start(rows[:, :].rearrange("x (m y) -> x m y", m=GI), h0_rows[g]).then_inc(rows_in, 16)

            def store(g):
                wait(e, "fin", g)
                e.dma_start(out_rows[g], fin[:, :].rearrange("t (m d) -> t m d", m=GI)).then_inc(stored, 16)

            load(0)
            with e.Fori(0, groups - 1) as g:
                store(g)
                e.wait_ge(stored, 16 * (g + 1))
                load(g + 1)
            store(groups - 1)
            e.wait_ge(stored, 16 * groups)

        NORMS = ((0, True), (1, True), (2, False), (3, False))

        @block.tensor
        def _(e):
            e.wait_ge(loaded, 32)
            e.matmul(B[0][:, 0:128], wt("wxr"), wt("wdt"), start=True, stop=True)
            e.matmul(B[1][:, 0:128], wt("wxb"), wt("wdt"), start=True, stop=True)
            e.matmul(B[2][:, 0:128], wt("wq"), const("rot"), start=True, stop=True)
            e.matmul(B[3][:, 0:128], wt("wk"), const("rot"), start=True, stop=True).then_inc(prep_pe, 1)
            e.wait_ge(prep, 7)

            def norm(g, k, centred, src):
                if centred:
                    e.matmul(B[1][:, 0:TOK], const("mean"), src[:, :], start=True, stop=True).then_inc(sig["mean"], 1)
                wait(e, "square", g, k + 1)
                e.matmul(B[2][:, 0:TOK], const("mean"), sqr[:, :], start=True, stop=True).then_inc(sig["variance"], 1)

            with e.Fori(0, groups) as g:
                e.wait_ge(rows_in, 16 * (g + 1))
                for q in range(Q):
                    mm = e.matmul(B[0][:, T * q + 1:T * q + T], rows[:, 128 * q:128 * q + 128],
                                  const("ident")[0:S, 0:S], start=True, stop=True, skip_group_check=True)
                mm.then_inc(sig["rows_t"], 1)
                wait(e, "h_in", g)
                norm(g, 0, True, h_in)
                wait(e, "normed", g, 1)
                wait(e, "flipped", g)
                e.matmul(B[0][:, 0:TOK], w_delta[:, :], xn[:, :], start=True, stop=True)
                e.matmul(B[1][:, 0:TOK], w_delta_b[:, :], xf[:, :], start=True, stop=True)
                e.matmul(B[2][:, 0:TOK], wt("wx"), xn[:, :], start=True, stop=True).then_inc(sig["proj"], 1)
                wait(e, "bc", g)

                def spread(row, bank):
                    return e.matmul(B[bank][:, 0:TOK], select[:, 128 * row:128 * row + 128], bc[:, :],
                                    start=True, stop=True)

                for n in range(NS):
                    if n >= 2:
                        wait(e, "drive", g, n - 1)
                    spread(n, 3 + 2 * (n % 2))
                    spread(NS + n, 4 + 2 * (n % 2)).then_inc(sig["bcast"], 1)
                e.matmul(B[7][:, 0:TOK], wskip[:, :], xn[:, :], start=True, stop=False)
                e.matmul(B[7][:, 0:TOK], wskip[:, :], xf[:, :], start=False, stop=False)
                wait(e, "drive", g)
                for n in range(NS + 1):
                    if n < NS:
                        if n >= 2:
                            wait(e, "read", g, n - 1)
                        spread(2 * NS + n, 3 + n % 2).then_inc(sig["c_cast"], 1)
                    if n > 0:
                        wait(e, "read", g, n)
                        mm = e.matmul(B[7][:, 0:TOK], wt("wout"), dB[:, TOK * (n - 1):TOK * n],
                                      start=False, stop=(n == NS))
                mm.then_inc(sig["scan_out"], 1)
                wait(e, "h1", g)
                norm(g, 1, True, h1)
                norm(g, 2, False, None)
                wait(e, "normed", g, 3)
                for b, w in enumerate((wt("wq_t"), wq_rot[:, :], wt("wk_t"), wk_rot[:, :])):
                    if b == 2:
                        wait(e, "var_eps", g, 3)
                    mm = e.matmul(B[b][:, 0:TOK], w, un[:, :], start=True, stop=True)
                mm.then_inc(sig["qk"], 1)
                for q in range(Q):
                    mm = e.matmul(B[4][0:T, 128 * q:128 * q + 128], un[:, T * q:T * q + T], wt("wv"),
                                  start=True, stop=True, skip_group_check=True)
                mm.then_inc(sig["v"], 1)
                wait(e, "rope", g)
                for m, (q, i) in enumerate(IMAGES):
                    a = 64 * i
                    wait(e, "kx", g, q + 1)
                    if m >= 4:
                        wait(e, "masked", g, m - 3)
                    e.matmul(B[m % 4][0:T, 0:NH * T], qf[a:a + 64, T * q:T * q + T],
                             kx[a:a + 64, NH * T * q:NH * T * (q + 1)], start=True, stop=True).then_inc(sig["scores"], 1)
                wait(e, "expd", g)
                wait(e, "v_copied", g)
                for m in range(GI + 1):
                    if m < GI:
                        if m >= 2:
                            wait(e, "p_copied", g, m - 1)
                        for h in range(NH):
                            mm = e.transpose(B[m % 2][0:T, T * h:T * h + T],
                                             sc[:, T * (NH * m + h):T * (NH * m + h) + T], const("ident")[0:T, 0:T])
                        mm.then_inc(sig["p_turned"], 1)
                    if m > 0:
                        wait(e, "p_copied", g, m)
                        for h in range(NH):
                            at = D * (m - 1) + HD * h
                            mm = e.matmul(B[5][0:T, at:at + HD], pt[(m - 1) % 2][:, T * h:T * h + T],
                                          v_sb[:, at:at + HD], start=True, stop=True, skip_group_check=True)
                mm.then_inc(sig["yv"], 1)
                wait(e, "y_norm", g)
                for m, (q, i) in enumerate(IMAGES):
                    mm = e.matmul(B[2][64 * i:64 * i + 64, T * q:T * q + T], yn[:, D * m:D * m + D],
                                  const("ident")[0:T, 0:T], start=True, stop=True, skip_group_check=True)
                mm.then_inc(sig["y_turned"], 1)
                wait(e, "y_copied", g)
                e.matmul(B[3][:, 0:TOK], wt("wo"), yt[:, :], start=True, stop=True).then_inc(sig["wo"], 1)
                wait(e, "x2", g)
                norm(g, 3, False, None)
                wait(e, "normed", g, 4)
                for q in range(Q):
                    mm = e.matmul(B[6][0:T, 2 * NE * q:2 * NE * (q + 1)], un[:, T * q:T * q + T], wt("router"),
                                  start=True, stop=True, skip_group_check=True)
                mm.then_inc(sig["router"], 1)
                for x in range(NE + 1):
                    if x < NE:
                        for k in range(4):
                            i, half, n = k // 2, k % 2, 4 * x + k
                            a, c = 64 * i, HID * x + HH * half
                            if n >= 2:
                                wait(e, "hidden", g, n - 1)
                            e.matmul(B[2 * (n % 2)][0:HH, 0:TOK], wt("w1")[a:a + 64, c:c + HH], un[a:a + 64, :],
                                     start=True, stop=True)
                            e.matmul(B[2 * (n % 2) + 1][0:HH, 0:TOK], wt("w3")[a:a + 64, c:c + HH], un[a:a + 64, :],
                                     start=True, stop=True).then_inc(sig["up"], 1)
                    if x > 0:
                        y = x - 1
                        wait(e, "hidden", g, 4 * y + 4)
                        if y >= 2:
                            wait(e, "gated", g, y - 1)
                        for m, (q, i) in enumerate(IMAGES):
                            for half in range(2):
                                mm = e.matmul(B[4 + y % 2][0:T, D * m:D * m + D],
                                              hid[y % 2][2 * i + half][:, T * q:T * q + T],
                                              wt("w2")[:, D * (2 * y + half):D * (2 * y + half) + D],
                                              start=(half == 0), stop=(half == 1), skip_group_check=True)
                        mm.then_inc(sig["down"], 1)
                wait(e, "residual", g)
                for q in range(Q):
                    mm = e.matmul(B[7][0:T, 128 * q:128 * q + 128], res[:, T * q:T * q + T], const("ident"),
                                  start=True, stop=True, skip_group_check=True)
                mm.then_inc(sig["res_turned"], 1)

        @block.scalar
        def _(e):
            e.preload_act_table_set("natural_log_exp_and_others")
            e.wait_ge(loaded, 32)
            e.activation(neg_a[:, :], wt("a_log"), ACT.Exp).then_inc(prep_act, 1)

            def norm(g, k):
                if k < 2:
                    wait(e, "cen", g, k + 1)
                elif k == 2:
                    wait(e, "normed", g, 2)
                else:
                    wait(e, "x2", g)
                src = (cen, cen, r, x2)[k]
                e.activation(sqr[:, :], src[:, :], ACT.Square).then_inc(sig["square"], 1)
                wait(e, "var_eps", g, k + 1)
                e.activation(log[:, :], ve[:, :], ACT.Ln).then_inc(sig["log"], 1)
                wait(e, "log", g, k + 1)
                e.activation(y0[:, :], log[:, :], ACT.Exp, scale=-0.5).then_inc(sig["guess"], 1)

            with e.Fori(0, groups) as g:
                norm(g, 0)
                wait(e, "proj", g)
                e.activation(bc[:, :], B[2][:, 0:TOK], ACT.Copy).then_inc(sig["bc"], 1)
                for k in range(2):
                    e.activation(mag[k][:, :], B[k][:, 0:TOK], ACT.Abs, bias=wt("b_dt")).then_inc(sig["soft_mag"], 1)
                for k in range(2):
                    wait(e, "soft_mag", g, k + 1)
                    e.activation(soft[k][:, :], mag[k][:, :], ACT.Exp, scale=-1.0).then_inc(sig["soft_exp"], 1)
                for k in range(2):
                    wait(e, "soft_exp", g, k + 1)
                    e.activation(mag[k][:, :], soft[k][:, :], ACT.Ln, bias=1.0).then_inc(sig["soft_log"], 1)
                wait(e, "delta", g, 1)
                for n in range(NS):
                    e.activation(dA[:, TOK * n:TOK * n + TOK], delta[0][:, :], ACT.Exp,
                                 scale=neg_a[:, n:n + 1]).then_inc(sig["decay"], 1)
                norm(g, 1)
                norm(g, 2)
                wait(e, "v", g)
                e.activation(v_sb[:, :], B[4][0:T, :], ACT.Copy).then_inc(sig["v_copied"], 1)
                wait(e, "shifted", g)
                e.activation(sc, sc, ACT.Exp).then_inc(sig["expd"], 1)
                for m in range(GI):
                    wait(e, "p_turned", g, m + 1)
                    e.activation(pt[m % 2][:, :], B[m % 2][0:T, 0:NH * T], ACT.Copy).then_inc(sig["p_copied"], 1)
                wait(e, "y_turned", g)
                e.activation(yt[:, :], B[2][:, 0:TOK], ACT.Copy).then_inc(sig["y_copied"], 1)
                norm(g, 3)
                wait(e, "gate", g, 2)
                e.activation(lg[1][:, :], lg[0][:, :], ACT.Exp).then_inc(sig["gate_exp"], 1)
                for n in range(4 * NE):
                    wait(e, "up", g, n + 1)
                    if n >= 2:
                        wait(e, "hidden", g, n - 1)
                    e.activation(silu[n % 2][:, :], B[2 * (n % 2)][0:HH, 0:TOK], ACT.Silu).then_inc(sig["silu"], 1)

        @block.vector
        def _(e):
            e.wait_ge(prep_pe, 1)
            for k, w in enumerate((w_delta, w_delta_b, wq_rot, wk_rot)):
                e.tensor_copy(w[:, :], B[k][:, 0:128]).then_inc(prep, 1)
            e.tensor_scalar(wskip[:, :], wt("wout"), wt("d_skip"), None, ALU.mult).then_inc(prep, 1)
            e.wait_ge(prep_act, 1)
            e.tensor_scalar(neg_a[:, :], neg_a[:, :], -1.0, None, ALU.mult).then_inc(prep, 1)
            for row in range(3 * NS):
                cp = e.tensor_copy(select[:, 128 * row:128 * row + 128].rearrange("p (i d) -> p i d", i=2),
                                   const("ident").rearrange("p (i d) -> p i d", i=2)[:, :, row:row + 1]
                                   .to_broadcast([128, 2, D]))
            cp.then_inc(prep, 1)

            def norm(g, k, src, dst, eps, weight):
                if k < 2:
                    wait(e, "mean", g, k + 1)
                    e.tensor_tensor(cen[:, :], src[:, :], B[1][:, 0:TOK], ALU.subtract).then_inc(sig["cen"], 1)
                    src = cen
                wait(e, "variance", g, k + 1)
                e.tensor_scalar(ve[:, :], B[2][:, 0:TOK], eps, None, ALU.add).then_inc(sig["var_eps"], 1)
                wait(e, "guess", g, k + 1)
                e.tensor_tensor(y1[:, :], y0[:, :], y0[:, :], ALU.mult).then_inc(sig["newton"], 1)
                wait(e, "newton", g, 3 * k + 1)
                e.tensor_tensor(rs[:, :], y1[:, :], ve[:, :], ALU.mult).then_inc(sig["newton"], 1)
                wait(e, "newton", g, 3 * k + 2)
                e.tensor_scalar(y1[:, :], rs[:, :], -0.5, 1.5, ALU.mult, ALU.add).then_inc(sig["newton"], 1)
                wait(e, "newton", g, 3 * k + 3)
                e.tensor_tensor(rs[:, :], y1[:, :], y0[:, :], ALU.mult).then_inc(sig["scale"], 1)
                wait(e, "scale", g, k + 1)
                if weight is None:
                    e.tensor_tensor(dst[:, :], src[:, :], rs[:, :], ALU.mult).then_inc(sig["normed"], 1)
                else:
                    e.scalar_tensor_tensor(out=dst[:, :], in0=src[:, :], scalar=weight, in1=rs[:, :],
                                           op0=ALU.mult, op1=ALU.mult).then_inc(sig["normed"], 1)

            with e.Fori(0, groups) as g:
                wait(e, "rows_t", g)
                e.tensor_copy(by_token(h_in[:, :])[:, :, 1:T], by_token(B[0][:, 0:TOK])[:, :, 1:T])\
                    .then_inc(sig["h_in"], 1)
                e.tensor_copy(by_token(h_in[:, :])[:, :, 0:1], wt("cls").unsqueeze(1).to_broadcast([128, Q, 1]))\
                    .then_inc(sig["h_in"], 1)
                wait(e, "h_in", g)
                norm(g, 0, h_in, xn, EPS, None)
                wait(e, "normed", g, 1)
                e.tensor_copy(by_token(xf[:, :]), by_token(xn[:, :])[:, :, ::-1]).then_inc(sig["flipped"], 1)
                wait(e, "soft_mag", g)
                for k in range(2):
                    e.tensor_scalar(pos[k][:, :], B[k][:, 0:TOK], wt("b_dt"), 0.0, ALU.add, ALU.max)\
                        .then_inc(sig["soft_pos"], 1)
                for k in range(2):
                    wait(e, "soft_pos", g, k + 1)
                    wait(e, "soft_log", g, k + 1)
                    e.tensor_tensor(delta[k][:, :], pos[k][:, :], mag[k][:, :], ALU.add).then_inc(sig["delta"], 1)
                for k, (dst, src) in enumerate(((du, xn), (dub, xf))):
                    wait(e, "delta", g, k + 1)
                    e.tensor_tensor(dst[:, :], delta[k][:, :], src[:, :], ALU.mult).then_inc(sig["du"], 1)
                wait(e, "du", g)
                for n in range(NS):
                    wait(e, "bcast", g, n + 1)
                    e.tensor_tensor(dB[:, TOK * n:TOK * n + TOK], B[3 + 2 * (n % 2)][:, 0:TOK], du[:, :], ALU.mult)
                    if n >= 2:
                        wait(e, "input", g, n - 1)
                    e.tensor_tensor(dB2[n % 2][:, :], B[4 + 2 * (n % 2)][:, 0:TOK], dub[:, :], ALU.mult)\
                        .then_inc(sig["drive"], 1)
                wait(e, "decay", g)
                e.memset(dA[:, :].rearrange("p (n t) -> p n t", t=T)[:, :, 0:1], 0.0).then_inc(sig["reset"], 1)
                wait(e, "input", g)
                wait(e, "reset", g)
                e.tensor_tensor_scan(dB[:, :], dA[:, :], dB[:, :], 0.0, ALU.mult, ALU.add).then_inc(sig["scan"], 1)
                wait(e, "scan", g)
                for n in range(NS):
                    wait(e, "c_cast", g, n + 1)
                    e.tensor_tensor(dB[:, TOK * n:TOK * n + TOK], dB[:, TOK * n:TOK * n + TOK],
                                    B[3 + n % 2][:, 0:TOK], ALU.mult).then_inc(sig["read"], 1)
                wait(e, "scan_out", g)
                e.tensor_tensor(h1[:, :], h_in[:, :], B[7][:, 0:TOK], ALU.add).then_inc(sig["h1"], 1)
                wait(e, "h1", g)
                norm(g, 1, h1, r, EPS, None)
                wait(e, "normed", g, 2)
                norm(g, 2, r, un, 1e-6, wt("ln1"))
                wait(e, "qk", g)
                for k, dst in enumerate((qf, kf)):
                    cos = const("cos").unsqueeze(1).to_broadcast([128, Q, T])
                    sin = const("sin").unsqueeze(1).to_broadcast([128, Q, T])
                    if k:
                        wait(e, "rope", g, 3)
                    e.tensor_tensor(by_token(dst[:, :]), by_token(B[2 * k][:, 0:TOK]), cos, ALU.mult)\
                        .then_inc(sig["rope"], 1)
                    e.tensor_tensor(by_token(tmp[:, :]), by_token(B[2 * k + 1][:, 0:TOK]), sin, ALU.mult)\
                        .then_inc(sig["rope"], 1)
                    wait(e, "rope", g, 3 * k + 2)
                    e.tensor_tensor(dst[:, :], dst[:, :], tmp[:, :], ALU.add).then_inc(sig["rope"], 1)
                wait(e, "rope", g)
                for q in range(Q):
                    e.tensor_tensor(kx[:, NH * T * q:NH * T * (q + 1)].rearrange("p (h t) -> p h t", t=T),
                                    kf[:, T * q:T * q + T].unsqueeze(1).to_broadcast([128, NH, T]),
                                    const("heads").unsqueeze(2).to_broadcast([128, NH, T]), ALU.mult)\
                        .then_inc(sig["kx"], 1)
                rows_v = sc.rearrange("t (m s) -> t m s", s=T)
                for m in range(GI):
                    wait(e, "scores", g, m + 1)
                    e.tensor_tensor(rows_v[:, NH * m:NH * m + NH, :],
                                    B[m % 4][0:T, 0:NH * T].rearrange("t (h s) -> t h s", s=T),
                                    const("causal").unsqueeze(1).to_broadcast([T, NH, T]), ALU.add)\
                        .then_inc(sig["masked"], 1)
                wait(e, "masked", g)
                e.tensor_reduce(mx[:, :], rows_v, AX.X, ALU.max).then_inc(sig["peak"], 1)
                wait(e, "peak", g)
                e.tensor_tensor(rows_v, rows_v, mx[:, :].unsqueeze(2).to_broadcast([T, GI * NH, T]), ALU.subtract)\
                    .then_inc(sig["shifted"], 1)
                wait(e, "expd", g)
                e.tensor_reduce(sm[:, :], rows_v, AX.X, ALU.add).then_inc(sig["total"], 1)
                wait(e, "total", g)
                e.reciprocal(rc[:, :], sm[:, :]).then_inc(sig["recip"], 1)
                wait(e, "recip", g)
                wait(e, "yv", g)
                e.tensor_tensor(yn[:, :].rearrange("t (m d) -> t m d", d=HD),
                                B[5][0:T, :].rearrange("t (m d) -> t m d", d=HD),
                                rc[:, :].unsqueeze(2).to_broadcast([T, GI * NH, HD]), ALU.mult)\
                    .then_inc(sig["y_norm"], 1)
                wait(e, "wo", g)
                e.tensor_tensor(x2[:, :], r[:, :], B[3][:, 0:TOK], ALU.add).then_inc(sig["x2"], 1)
                wait(e, "x2", g)
                norm(g, 3, x2, un, 1e-6, wt("ln2"))
                e.tensor_tensor(res[:, :], h1[:, :], x2[:, :], ALU.add).then_inc(sig["residual"], 1)

                def e8(ap):
                    return ap.rearrange("t (m e) -> t m e", e=NE)

                def over(ap):
                    return ap.unsqueeze(2).to_broadcast([T, GI, NE])

                count = [0]

                def step(ins):
                    count[0] += 1
                    ins.then_inc(sig["gate"], 1)
                    wait(e, "gate", g, count[0])

                order = const("order").unsqueeze(1).to_broadcast([T, GI, NE])
                wait(e, "router", g)
                logits = e8(B[6][0:T, 0:GI * NE])
                step(e.tensor_reduce(st[0][:, :], logits, AX.X, ALU.max))
                step(e.tensor_tensor(e8(lg[0][:, :]), logits, over(st[0][:, :]), ALU.subtract))
                wait(e, "gate_exp", g)
                step(e.tensor_reduce(st[1][:, :], e8(lg[1][:, :]), AX.X, ALU.add))
                step(e.reciprocal(st[2][:, :], st[1][:, :]))
                step(e.tensor_tensor(e8(lg[0][:, :]), e8(lg[1][:, :]), over(st[2][:, :]), ALU.mult))

                def top(probs, peak, code, chosen):
                    step(e.tensor_reduce(st[peak][:, :], e8(lg[probs][:, :]), AX.X, ALU.max))
                    step(e.tensor_tensor(e8(lg[code][:, :]), e8(lg[probs][:, :]), over(st[peak][:, :]), ALU.is_equal))
                    step(e.tensor_tensor(e8(lg[code][:, :]), e8(lg[code][:, :]), order, ALU.mult))
                    step(e.tensor_reduce(st[0][:, :], e8(lg[code][:, :]), AX.X, ALU.max))
                    step(e.tensor_tensor(e8(lg[chosen][:, :]), e8(lg[code][:, :]), over(st[0][:, :]), ALU.is_equal))

                top(0, 3, 1, 2)
                step(e.scalar_tensor_tensor(out=lg[3][:, :], in0=lg[2][:, :], scalar=-2.0, in1=lg[0][:, :],
                                            op0=ALU.mult, op1=ALU.add))
                top(3, 4, 1, 4)
                step(e.tensor_tensor(lg[2][:, :], lg[2][:, :], lg[4][:, :], ALU.add))
                step(e.tensor_tensor(lg[2][:, :], lg[2][:, :], lg[0][:, :], ALU.mult))
                step(e.scalar_tensor_tensor(out=st[5][:, :], in0=st[3][:, :], scalar=1e-9, in1=st[4][:, :],
                                            op0=ALU.add, op1=ALU.add))
                step(e.reciprocal(st[1][:, :], st[5][:, :]))
                step(e.tensor_tensor(e8(lg[5][:, :]), e8(lg[2][:, :]), over(st[1][:, :]), ALU.mult))
                assert count[0] == PER["gate"], count

                def gated(x):
                    wait(e, "down", g, x + 1)
                    o = B[4 + x % 2][0:T, :].rearrange("t (m d) -> t m d", d=D)
                    w = e8(lg[5][:, :])[:, :, x:x + 1].to_broadcast([T, GI, D])
                    dst = acc[0] if x == 0 else part
                    if x > 1:
                        wait(e, "summed", g, x)
                    e.tensor_tensor(dst[:, :].rearrange("t (m d) -> t m d", d=D), o, w, ALU.mult)\
                        .then_inc(sig["gated"], 1)
                    wait(e, "gated", g, x + 1)
                    if x == 0:
                        e.tensor_copy(acc[1][:, 0:1], acc[0][:, 0:1]).then_inc(sig["summed"], 1)
                    else:
                        e.tensor_tensor(acc[0][:, :], acc[0][:, :], part[:, :], ALU.add).then_inc(sig["summed"], 1)

                for n in range(4 * NE):
                    x = n // 4
                    if n % 4 == 0 and x >= 2:
                        wait(e, "down", g, x - 1)
                    wait(e, "silu", g, n + 1)
                    e.tensor_tensor(hid[x % 2][n % 4][:, :], silu[n % 2][:, :], B[2 * (n % 2) + 1][0:HH, 0:TOK],
                                    ALU.mult).then_inc(sig["hidden"], 1)
                    if n % 4 == 3 and x > 0:
                        gated(x - 1)
                gated(NE - 1)
                wait(e, "summed", g)
                wait(e, "res_turned", g)
                e.tensor_tensor(fin[:, :], acc[0][:, :], B[7][0:T, :], ALU.add).then_inc(sig["fin"], 1)

        @block.gpsimd
        def _(e):
            with e.Fori(0, groups) as g:
                for n in range(NS):
                    wait(e, "drive", g, n + 1)
                    e.tensor_tensor(dB[:, TOK * n:TOK * n + TOK], dB[:, TOK * n:TOK * n + TOK], dB2[n % 2][:, :],
                                    ALU.add).then_inc(sig["input"], 1)


_TOKENIZER = ['x', 'fc0_w', 'fc0_b', 'ln0_g', 'ln0_b', 'conv_w', 'conv_b', 'ln_g', 'ln_b', 'fc1_w', 'fc1_b',
              'fc2_w', 'fc2_b', 'fc3_w', 'fc3_b']
_OUTS = [((NI, T, D), 'float32')]


def build(nc, io, out, place, block_place, weight_place):
    h0 = nc.dram_tensor("tokens", (NI, S, S), F32).ap()
    build_tokenizer(nc, io, place, h0)
    build_block(nc, io, block_place, weight_place, h0, out)


def kernel(**inputs):
    import numpy as _np
    import concourse.bacc as _bacc
    from concourse import mybir as _mybir
    from concourse.bass_utils import run_bass_kernel_spmd as _run

    a = {name: _np.asarray(v) for name, v in inputs.items()}
    laid = {name: a[name if name == 'x' else 'L0_tok_' + name] for name in _TOKENIZER}
    laid["tables"], place = pack(constants())
    laid["w_mix"] = mixing_weights(*(a['L0_tok_' + name] for name in ('w1r', 'w1i', 'w2r', 'w2i')))
    laid["block_tables"], block_place = pack(block_tables())
    laid["block_weights"], weight_place = pack(block_weights(a))

    nc = _bacc.Bacc("TRN2", target_bir_lowering=False, num_devices=1)
    arrays, io = {}, {}
    for name, v in laid.items():
        v = _np.ascontiguousarray(v)
        arrays[f"in_{name}_dram"] = v
        io[name] = nc.dram_tensor(f"in_{name}_dram", v.shape, _mybir.dt.from_np(v.dtype), kind="ExternalInput").ap()
    outs = [nc.dram_tensor(f"out_{i}_dram", shape, _mybir.dt.from_np(_np.dtype(dtype)), kind="ExternalOutput").ap()
            for i, (shape, dtype) in enumerate(_OUTS)]
    build(nc, io, outs[0], place, block_place, weight_place)
    r = _run(nc, [arrays], core_ids=[0])
    return r.results[0]["out_0_dram"]
```

```python
from contextlib import ExitStack

import concourse.bass as bass
import numpy as np
from concourse import mybir

F32 = mybir.dt.float32
ACT = mybir.ActivationFunctionType
ALU = mybir.AluOpType
AX = mybir.AxisListType

NI = 128
S = 64
C = 32
LAYERS = 4
NK = 13
NY = 12
T26 = 2 * NK
B24 = 2 * NY
PX = 2048
CH = 512
MODE = 4 * C
EPS = 1e-5


def constants():
    x = np.arange(S)
    ang = 2 * np.pi / S
    bx = np.zeros((S, NK, 2))
    by = np.zeros((S, NY, 2))
    for k in range(NK):
        bx[:, k, 0], bx[:, k, 1] = np.cos(ang * k * x), np.sin(ang * k * x)
    for k in range(NY):
        by[:, k, 0], by[:, k, 1] = np.cos(ang * k * x), np.sin(ang * k * x)
    bx, by = bx.reshape(S, T26), by.reshape(S, B24)
    alpha = np.repeat(np.where(np.arange(NY) == 0, 1.0, 2.0) / (S * S), 2)
    t = {}
    t["ident"] = np.eye(128)
    forward = bx.reshape(S, NK, 2).transpose(0, 2, 1).reshape(S, T26)
    t["f1"] = np.kron(np.eye(2), forward)
    t["f2"] = np.kron(by, np.eye(2))
    t["ga"] = np.kron(np.eye(2), bx.T)
    t["gb"] = np.kron((by * alpha).T, np.eye(4))
    t["maskc"] = np.kron(np.eye(4), np.ones((C, C)))
    t["center"] = np.eye(C) - 1.0 / C
    t["center_dc"] = (np.eye(C) - 1.0 / C) * (S * S)
    r = np.zeros((4, 97))
    for p in range(96):
        r[p % 3, p] = 1
    r[3, 96] = 1
    t["rinp"] = r
    m = np.zeros((97, 32))
    for p in range(96):
        m[p, p // 3] = 1
    m[96, :] = 1
    t["maski"] = m
    sign = {(0, 0): {(0, 0): (1, 1), (1, 1): (-1, 1), (0, 1): (1, 1), (1, 0): (1, -1)},
            (1, 1): {(0, 0): (-1, 1), (1, 1): (1, 1), (0, 1): (-1, 1), (1, 0): (-1, -1)},
            (1, 0): {(0, 0): (-1, 1), (1, 1): (1, 1), (0, 1): (1, -1), (1, 0): (1, 1)},
            (0, 1): {(0, 0): (-1, -1), (1, 1): (1, -1), (0, 1): (1, 1), (1, 0): (1, -1)}}
    s = np.zeros((128, 8))
    for q in range(4):
        for row in range(128):
            b, a = row // 64, row % 2
            s[row, 2 * q], s[row, 2 * q + 1] = sign[(q // 2, q % 2)][(a, b)]
    t["sign"] = s
    return {k: v.astype(np.float32) for k, v in t.items()}


def mixing_weights(w1r, w1i, w2r, w2i):
    L = w1r.shape[0]
    out = np.zeros((L, NY, 2, C, 2, 4, NK, C), np.float32)
    for b in range(2):
        for a in range(2):
            for kind in range(2):
                first, second = (w1r, w2r) if (a ^ b ^ kind) == 0 else (w1i, w2i)
                out[:, :, b, :, a, 2 * kind, 0:12, :] = np.transpose(first, (0, 4, 1, 3, 2))
                out[:, :, b, :, a, 2 * kind + 1, 1:13, :] = np.transpose(second, (0, 4, 1, 3, 2))[:, :, :, ::-1, :]
    return out.reshape(L, NY, 128, 4 * NK * C)


def build_tokenizer(nc, io, place, h0, debug=None):
    pairs = NI // 2
    halves = pairs // 2
    with ExitStack() as ctx:
        def sb(name, shape):
            return ctx.enter_context(nc.sbuf_tensor("sb_" + name, shape, F32))

        def sem(name):
            return ctx.enter_context(nc.semaphore(name))

        table = sb("table", [128, max(p[2] for p in place.values())])

        def const(name):
            r, a, b = place[name]
            return table[0:r, a:b]

        act_d = nc.dram_tensor("act_scratch", (pairs, 128, PX), F32).ap()
        x_d = nc.dram_tensor("spectrum_in", (NI, NY, 4 * C * NK), F32).ap()
        y_d = nc.dram_tensor("spectrum_out", (NI, NY, NK, MODE), F32).ap()

        image_in = [sb(f"image_in{p}", [128, 3 * S]) for p in range(2)]
        image_t = sb("image_t", [97, 256])
        fc0_rows = sb("fc0_rows", [4, C])
        fc0_center = sb("fc0_center", [4, C])
        fc0_mean = sb("fc0_mean", [4, 1])
        fc0_rep = sb("fc0_rep", [97, C])
        fc0_block = sb("fc0_block", [97, 32 * C])
        conv_raw = sb("conv_raw", [C, C])
        conv_rep = sb("conv_rep", [C, 128])
        conv_col = sb("conv_col", [128, C])
        conv_block = sb("conv_block", [128, 128])
        bias_raw = sb("bias_raw", [C, 1])
        bias_cols = sb("bias_cols", [C, 128])
        ones = sb("ones", [128, 128])
        gain = sb("gain", [128, 1])
        shift = sb("shift", [128, 1])
        fc1_pad = sb("fc1_pad", [128, 4 * 128])
        fc1_bias = sb("fc1_bias", [128, 1])
        fc2_w = sb("fc2_w", [128, 64])
        fc2_bias = sb("fc2_bias", [128, 1])
        fc3_pad = sb("fc3_pad", [128, 2])
        fc3_bias = sb("fc3_bias", [128, 1])
        act_in = [sb(f"act_in{p}", [128, PX]) for p in range(2)]
        z_in = [sb(f"z_in{p}", [2 * T26, B24 * C]) for p in range(2)]
        v_sb = sb("v_sb", [4 * B24, 1024])
        square = [sb(f"square{p}", [128, CH]) for p in range(2)]
        var = [sb(f"var{p}", [128, 16]) for p in range(2)]
        rstd = [sb(f"rstd{p}", [128, 16]) for p in range(2)]
        minus_half = sb("minus_half", [128, 16])
        eps = sb("eps", [128, 16])
        unit = [sb(f"unit{p}", [128, CH]) for p in range(2)]
        act_out = [sb(f"act_out{p}", [128, PX]) for p in range(2)]
        pix = sb("pix", [128, PX])
        f1_sb = sb("f1_sb", [128, 32 * T26])
        f2_sb = [sb(f"f2_sb{p}", [112, 16 * T26]) for p in range(2)]
        dense1 = [sb(f"dense1_{p}", [128, CH]) for p in range(4)]
        dense2 = [sb(f"dense2_{p}", [128, CH]) for p in range(2)]
        head = [sb(f"head{p}", [128, S]) for p in range(2)]
        w_raw = [sb(f"w_raw{p}", [128, 4 * NK * C]) for p in range(2)]
        w_sum = [sb(f"w_sum{p}", [128, 4 * NK]) for p in range(2)]
        w_cen = [sb(f"w_cen{p}", [128, 4 * NK * C]) for p in range(2)]
        w_neg = sb("w_neg", [128, 4 * NK * C])
        w_mix = [sb(f"w_mix{p}", [128, NK * MODE]) for p in range(2)]
        x_in = [sb(f"x_in{p}", [NI, NK * MODE]) for p in range(2)]
        x_t = [sb(f"x_t{p}", [128, 4 * NI]) for p in range(2)]
        y_sb = [sb(f"y_sb{p}", [NI, NK * MODE]) for p in range(2)]

        H = [ctx.enter_context(nc.psum_tensor(f"H{j}", [128, CH], F32)) for j in range(4)]
        TC = ctx.enter_context(nc.psum_tensor("TC", [128, CH], F32))
        TP = ctx.enter_context(nc.psum_tensor("TP", [128, CH], F32))
        M = [ctx.enter_context(nc.psum_tensor(f"M{j}", [128, CH], F32)) for j in range(2)]

        table_in = sem("table_in")
        param_in = sem("param_in")
        layer_in = sem("layer_in")
        set_up = sem("set_up")
        prep_pe = sem("prep_pe")
        conv_set = sem("conv_set")
        conv_pe = sem("conv_pe")
        ld = [sem(f"pixels_in{p}") for p in range(2)]
        zl = [sem(f"z_loaded{p}") for p in range(2)]
        st_a = [sem(f"act_stored{p}") for p in range(2)]
        st_x = [sem(f"f2_stored{p}") for p in range(2)]
        st_h = [sem(f"head_stored{p}") for p in range(2)]
        a_done = sem("stepA_done")
        v_ready = sem("v_ready")
        h_ready = sem("h_ready")
        sq_ready = sem("sq_ready")
        var_ready = sem("var_ready")
        var_eps = sem("var_eps")
        rstd_ready = sem("rstd_ready")
        unit_ready = sem("unit_ready")
        tc_ready = sem("tc_ready")
        act_ready = sem("act_ready")
        tp_ready = sem("tp_ready")
        pix_ready = sem("pix_ready")
        f1_done = sem("f1_done")
        f1_ready = sem("f1_ready")
        f2_done = sem("f2_done")
        f2_ready = sem("f2_ready")
        w_in = [sem(f"w_in{p}") for p in range(2)]
        x_inq = [sem(f"x_inq{p}") for p in range(2)]
        y_out = [sem(f"y_out{p}") for p in range(2)]
        w_sum_s = sem("w_summed")
        w_cen_s = sem("w_centered")
        w_neg_s = sem("w_signed")
        w_mix_s = sem("w_mixed")
        xt_pe = sem("xt_transposed")
        xt_s = sem("xt_copied")
        y_pe = sem("y_product")
        y_s = sem("y_copied")
        fc1_done = sem("fc1_done")
        fc1_act = sem("fc1_act")
        fc2_done = sem("fc2_done")
        fc2_act = sem("fc2_act")
        fc3_done = sem("fc3_done")
        head_ready = sem("head_ready")

        def at_least(eng, s, n):
            if not isinstance(n, int) or n > 0:
                eng.wait_ge(s, n)

        images = io["x"].rearrange("(n i) h w c -> n (i h) (w c)", i=2)
        y_view = y_d.rearrange("(n i) y k m -> n i k m y", i=2)
        heads = h0.rearrange("(n i) x y -> n (i x) y", i=2)
        x_view = x_d.rearrange("(n i) y m -> n i y m", i=2)
        GROUPS = [(0, 4), (4, 4), (8, 4), (12, 1)]

        def sp_load(e, P, p, n, first):
            if first:
                at_least(e, h_ready, 8 * P + 4 * p - 4)
                e.dma_start(image_in[p][:, :], images[n]).then_inc(ld[p], 16)
                return
            at_least(e, h_ready, 8 * P + 4 * p - 4)
            e.dma_start(act_in[p][:, :], act_d[n]).then_inc(ld[p], 16)
            for i in range(2):
                src = y_d[n * 2 + i].rearrange("y k (a m) -> (k a) y m", a=2)
                e.dma_start(z_in[p][i * T26:(i + 1) * T26, :].rearrange("t (y m) -> t y m", y=NY), src).then_inc(zl[p], 16)

        def sp_store(e, P, p, n, last):
            if last:
                e.wait_ge(head_ready, 8 * (P - 4 * halves) + 4 * p + 4)
                e.dma_start(heads[n], head[p][:, :]).then_inc(st_h[p], 16)
                return
            e.wait_ge(act_ready, 8 * P + 4 * p + 4)
            e.dma_start(act_d[n], act_out[p][:, :]).then_inc(st_a[p], 16)
            e.wait_ge(f2_ready, 2 * P + p + 1)
            for i in range(2):
                e.dma_start(x_d[n * 2 + i].rearrange("y (b m) -> (y b) m", b=4),
                            f2_sb[p][64 * i:64 * i + 48, :]).then_inc(st_x[p], 16)

        HEAD0 = 4 * LAYERS * pairs

        def behind(g0, p, j, lag, front, back):
            if j >= lag:
                return (g0 + j - lag, p, j - lag) if front else None
            return (g0 + j - lag, 1 - p, j - lag + 4) if back else None

        def pe_step(e, P, p, front, back, first, last, layer):
            it = 2 * P + p
            g0 = 4 * it

            def bank(j):
                return H[j % 2] if last else H[j]

            def inverse_x():
                e.wait_ge(ld[p] if first else zl[p], 16 * (P + 1) if first else 32 * (P - halves + 1))
                for u in range(2):
                    if last and back:
                        e.wait_ge(fc1_act, 4 * (g0 - HEAD0 - 4) + 3 + u)
                    elif u == 1:
                        at_least(e, f2_ready, it - 1)
                    if first:
                        e.transpose(M[u][0:96, 0:128], image_in[p][:, 96 * u:96 * u + 96],
                                    const("ident")).then_inc(a_done, 1)
                        continue
                    for g in range(4):
                        z = z_in[p][:, :].rearrange("t (y g) -> t y g", g=8)[:, :, 4 * u + g]
                        mm = e.matmul(M[u][0:96, 128 * g:128 * g + 128], z, const("ga"), start=True, stop=True)
                    mm.then_inc(a_done, 1)

            def conv(j):
                at_least(e, unit_ready, g0 + j + 1 - (2 if last else 4))
                if first:
                    return
                if j == 0:
                    e.wait_ge(ld[p], 16 * (P + 1))
                    e.wait_ge(y_s, 48 * (layer + 1))
                for u in range(4):
                    b = 4 * j + u
                    e.matmul(bank(j)[:, 128 * u:128 * u + 128], act_in[p][:, 128 * b:128 * b + 128],
                             conv_block[:, :], start=(u == 0), stop=False, skip_group_check=True)

            def inverse_y(j):
                if j == 0:
                    e.wait_ge(v_ready, 2 * it + 2)
                if first:
                    e.matmul(bank(j)[:, :], image_t[:, 128 * (j // 2):128 * (j // 2) + 128],
                             fc0_block[:, 512 * (j % 2):512 * (j % 2) + 512],
                             start=True, stop=True).then_inc(h_ready, 1)
                    return
                for og in range(8):
                    mm = e.matmul(bank(j)[:, :].rearrange("p (y g) -> p y g", g=8)[:, :, og],
                                  v_sb[:, 128 * og:128 * og + 128], const("gb")[:, 64 * j:64 * j + 64],
                                  start=False, stop=(og == 7), skip_group_check=True)
                mm.then_inc(h_ready, 1)

            def to_channels(c, q, k):
                e.wait_ge(unit_ready, c + 1)
                at_least(e, act_ready, c)
                for u in range(4):
                    mm = e.transpose(TC[:, 128 * u:128 * u + 128], unit[k % 2][:, 128 * u:128 * u + 128],
                                     const("ident"))
                mm.then_inc(tc_ready, 1)

            def to_pixels(c, q, k):
                e.wait_ge(act_ready, c + 1)
                at_least(e, pix_ready, c)
                for u in range(4):
                    b = 4 * k + u
                    mm = e.transpose(TP[:, 128 * u:128 * u + 128], act_out[q][:, 128 * b:128 * b + 128],
                                     const("ident"))
                mm.then_inc(tp_ready, 1)

            def forward_x():
                e.wait_ge(pix_ready, g0)
                if not front:
                    at_least(e, f2_ready, it - 1)
                for u in range(2):
                    for g in range(8):
                        cols = pix[:, :].rearrange("p (y h c) -> p y h c", h=2, c=16)[:, :, :, 8 * u + g]
                        mm = e.matmul(M[u][:, 52 * g:52 * g + 52], cols, const("f1"), start=True, stop=True)
                    mm.then_inc(f1_done, 1)

            def forward_y():
                e.wait_ge(f1_ready, 2 * it)
                for i in range(2):
                    src = f1_sb[:, :].rearrange("p (c i t) -> p c i t", c=16, i=2)[:, :, i, :]
                    mm = e.matmul(M[1][64 * i:64 * i + 48, 0:16 * T26], const("f2"), src, start=True, stop=True,
                                  skip_group_check=True)
                mm.then_inc(f2_done, 1)

            def dense1_of(w, c, q, k, j):
                n = c - HEAD0
                for v in range(2):
                    at_least(e, fc1_act, 4 * n + 2 * w + v - 1)
                    if w == 0 and v == 0:
                        e.wait_ge(act_ready, c + 1)
                        if j == 0 and front:
                            e.wait_ge(v_ready, 2 * it + 2)
                    e.matmul(M[v][:, :], fc1_pad[:, 128 * (2 * w + v):128 * (2 * w + v) + 128],
                             act_out[q][:, 512 * k:512 * k + 512], start=True, stop=True).then_inc(fc1_done, 1)

            def dense2_of(w, c):
                n = c - HEAD0
                e.wait_ge(fc1_act, 4 * n + 2 * w + 2)
                for v in range(2):
                    mm = e.matmul((TP, H[3])[w][64 * v:64 * v + 64, :], fc2_w[:, :], dense1[2 * w + v][:, :],
                                  start=True, stop=True, skip_group_check=True)
                mm.then_inc(fc2_done, 1)

            def dense3_of(c):
                n = c - HEAD0
                e.wait_ge(fc2_act, 2 * n + 2)
                at_least(e, head_ready, n)
                for w in range(2):
                    for u in range(4):
                        mm = e.matmul(H[2][:, 4 * u + 2 * w:4 * u + 2 * w + 2],
                                      dense2[w][:, 128 * u:128 * u + 128], fc3_pad[:, :],
                                      start=True, stop=True, skip_group_check=True)
                mm.then_inc(fc3_done, 1)

            if front:
                inverse_x()
            for j in range(4):
                two, three, four = (behind(g0, p, j, lag, front, back) for lag in (2, 3, 4))
                if front:
                    conv(j)
                if last and four:
                    dense2_of(1, four[0])
                if last and three:
                    dense1_of(0, *three, j)
                if last and four:
                    dense3_of(four[0])
                if not last and three:
                    to_pixels(*three)
                if not last and back and j == 3:
                    forward_y()
                if first and two:
                    to_channels(*two)
                if front:
                    inverse_y(j)
                if not last and back and j == 2:
                    forward_x()
                if last and three:
                    dense1_of(1, *three, j)
                if two and not first:
                    to_channels(*two)
                if last and three:
                    dense2_of(0, three[0])

        def act_step(e, P, p, front, back, first, last):
            it = 2 * P + p
            g0 = 4 * it
            gelu = ACT.Identity if (first or last) else ACT.Gelu

            def squares(j):
                e.wait_ge(h_ready, g0 + j + 1)
                at_least(e, var_ready, g0 + j - 1)
                e.activation(square[j % 2][:, :], (H[j % 2] if last else H[j])[:, :], ACT.Square,
                             scale=float(C) ** -0.5).then_inc(sq_ready, 1)

            def gelus(c, q, k):
                e.wait_ge(tc_ready, c + 1)
                if not last and k == 0:
                    at_least(e, st_a[p], 16 * P)
                e.activation(act_out[q][:, 512 * k:512 * k + 512], TC[:, :], gelu, bias=shift[:, 0:1],
                             scale=gain[:, 0:1]).then_inc(act_ready, 1)

            def dense1_of(w, c):
                n = c - HEAD0
                for v in range(2):
                    e.wait_ge(fc1_done, 4 * n + 2 * w + v + 1)
                    e.activation(dense1[2 * w + v][:, :], M[v][:, :], ACT.Gelu, bias=fc1_bias[:, 0:1],
                                 scale=1.0).then_inc(fc1_act, 1)

            def dense2_of(w, c):
                n = c - HEAD0
                e.wait_ge(fc2_done, 2 * n + w + 1)
                e.activation(dense2[w][:, :], (TP, H[3])[w][:, :], ACT.Gelu, bias=fc2_bias[:, 0:1],
                             scale=1.0).then_inc(fc2_act, 1)

            if front:
                for u in range(2):
                    e.wait_ge(a_done, 2 * it + u + 1)
                    if first:
                        e.activation(image_t[0:96, 128 * u:128 * u + 128], M[u][0:96, 0:128],
                                     ACT.Copy).then_inc(v_ready, 1)
                    else:
                        e.activation(v_sb[:, 512 * u:512 * u + 512], M[u][0:96, :], ACT.Copy).then_inc(v_ready, 1)
            for j in range(4):
                two, three, four = (behind(g0, p, j, lag, front, back) for lag in (2, 3, 4))
                if last and four:
                    dense2_of(1, four[0])
                if last and three:
                    dense1_of(0, three[0])
                if first and two:
                    gelus(*two)
                if front:
                    squares(j)
                if not last and back and j == 2:
                    for u in range(2):
                        e.wait_ge(f1_done, 2 * it + u - 1)
                        e.activation(f1_sb[:, 416 * u:416 * u + 416], M[u][:, 0:416], ACT.Copy).then_inc(f1_ready, 1)
                if last and three:
                    dense1_of(1, three[0])
                if two and not first:
                    gelus(*two)
                if last and three:
                    dense2_of(0, three[0])

        def dve_step(e, P, p, front, back, first, last):
            it = 2 * P + p
            g0 = 4 * it

            def variance(j):
                e.wait_ge(sq_ready, g0 + j + 1)
                e.tensor_reduce(var[j % 2][:, :], square[j % 2][:, :].rearrange("p (y c) -> p y c", c=C), AX.X,
                                ALU.add).then_inc(var_ready, 1)

            def normal(c, q, k):
                e.wait_ge(rstd_ready, c + 1)
                at_least(e, tc_ready, c - 1)
                e.tensor_tensor(unit[k % 2][:, :].rearrange("p (y c) -> p y c", c=C),
                                (H[k % 2] if last else H[k])[:, :].rearrange("p (y c) -> p y c", c=C),
                                rstd[k % 2][:, :].unsqueeze(2).to_broadcast([128, 16, C]), ALU.mult).then_inc(unit_ready, 1)

            def pixels(c, q, k):
                e.wait_ge(tp_ready, c + 1)
                e.tensor_copy(pix[:, 512 * k:512 * k + 512], TP[:, :]).then_inc(pix_ready, 1)

            def spectrum():
                e.wait_ge(f2_done, it)
                at_least(e, st_x[1 - p], 32 * (P if p else P - 1))
                for i in range(2):
                    cp = e.tensor_copy(f2_sb[1 - p][64 * i:64 * i + 48, :], M[1][64 * i:64 * i + 48, 0:16 * T26])
                cp.then_inc(f2_ready, 1)

            def heads_out(c, q, k):
                e.wait_ge(fc3_done, c - HEAD0 + 1)
                if k == 0:
                    at_least(e, st_h[q], 16 * ((P if p else P - 1) - LAYERS * halves))
                e.tensor_scalar(head[q][:, 16 * k:16 * k + 16], H[2][:, 0:16], fc3_bias[:, 0:1], None,
                                ALU.add).then_inc(head_ready, 1)

            for j in range(4):
                one, three, four = (behind(g0, p, j, lag, front, back) for lag in (1, 3, 4))
                if not last and three:
                    pixels(*three)
                if last and four:
                    heads_out(*four)
                if not last and back and j == 3:
                    spectrum()
                if front:
                    variance(j)
                if one:
                    normal(*one)

        def pool_step(e, P, p, front):
            g0 = 8 * P + 4 * p
            if not front:
                return
            for j in range(4):
                e.wait_ge(var_ready, g0 + j + 1)
                e.tensor_tensor(var[j % 2][:, :], var[j % 2][:, :], eps[:, :], ALU.add).then_inc(var_eps, 1)
                e.wait_ge(var_eps, g0 + j + 1)
                e.tensor_tensor(rstd[j % 2][:, :], var[j % 2][:, :], minus_half[:, :], ALU.pow).then_inc(rstd_ready, 1)

        def since(eng, s, before, n):
            if not isinstance(n, int) or n > 0:
                eng.wait_ge(s, before + n)

        def sp_mix_load(e, m, p, layer):
            q, ky = 2 * m + p, 2 * m + p
            if not (isinstance(m, int) and m == 0):
                since(e, w_cen_s, NY * layer, q - 1)
                e.dma_start(w_raw[p][:, :], io["w_mix"][layer, ky]).then_inc(w_in[p], 16)
            since(e, xt_pe, 4 * NY * layer, 4 * (q - 1))
            e.dma_start(x_in[p][:, :], x_d[:, ky, :]).then_inc(x_inq[p], 16)

        def sp_mix_store(e, m, p, layer):
            ky = 2 * m + p
            e.wait_ge(y_s, 4 * NY * layer + 4 * ky + 4)
            e.dma_start(y_d[:, ky, :, :], y_sb[p][:, :].rearrange("n (k m) -> n k m", k=NK)).then_inc(y_out[p], 16)

        def pe_mix(e, m, p, layer, zero):
            q, q0 = 2 * m + p, NY * layer
            e.wait_ge(x_inq[p], 16 * (NY // 2 * layer + m + 1))
            xv = x_in[p][:, :].rearrange("n (m k) -> n m k", k=NK)

            def turn(s):
                k0, n = GROUPS[s]
                since(e, xt_s, 4 * q0, 4 * q + s - 1)
                for k in range(k0, k0 + n):
                    mm = e.transpose(H[s % 2][:, NI * (k - k0):NI * (k - k0) + NI], xv[:, :, k],
                                     const("ident")[0:NI, 0:NI])
                mm.then_inc(xt_pe, 1)

            turn(0)
            for s, (k0, n) in enumerate(GROUPS):
                if s < 3:
                    turn(s + 1)
                e.wait_ge(xt_s, 4 * (q0 + q) + s + 1)
                e.wait_ge(w_mix_s, 4 * (q0 + q) + 4)
                since(e, y_s, 4 * q0, 4 * q + s - 1)
                for k in range(k0, k0 + n):
                    dc = zero and k == 0
                    mm = e.matmul(H[2 + s % 2][0:NI, 128 * (k - k0):128 * (k - k0) + 128],
                                  x_t[s % 2][:, NI * (k - k0):NI * (k - k0) + NI],
                                  w_mix[p][:, 128 * k:128 * k + 128], start=True, stop=not dc, skip_group_check=True)
                    if dc:
                        mm = e.matmul(H[2][0:NI, 0:C], bias_cols[:, 0:NI], const("center_dc"),
                                      start=False, stop=True, skip_group_check=True)
                mm.then_inc(y_pe, 1)

        def act_mix(e, m, p, layer):
            q, q0 = 2 * m + p, NY * layer

            def turned(s):
                n = GROUPS[s][1]
                e.wait_ge(xt_pe, 4 * (q0 + q) + s + 1)
                since(e, y_pe, 4 * q0, 4 * q + s - 1)
                e.activation(x_t[s % 2][:, 0:NI * n], H[s % 2][:, 0:NI * n], ACT.Copy).then_inc(xt_s, 1)

            turned(0)
            for s, (k0, n) in enumerate(GROUPS):
                if s < 3:
                    turned(s + 1)
                e.wait_ge(y_pe, 4 * (q0 + q) + s + 1)
                if s == 0:
                    since(e, y_out[p], 16 * (NY // 2) * layer, 16 * m)
                e.activation(y_sb[p][:, 128 * k0:128 * (k0 + n)], H[2 + s % 2][0:NI, 0:128 * n],
                             ACT.Copy).then_inc(y_s, 1)

        def dve_center(e, m, p, layer):
            q, q0 = 2 * m + p, NY * layer
            e.wait_ge(w_in[p], 16 * (NY // 2 * layer + m + 1))
            raw = w_raw[p][:, :].rearrange("r (k o) -> r k o", o=C)
            e.tensor_reduce(w_sum[p][:, :], raw, AX.X, ALU.add).then_inc(w_sum_s, 1)
            e.wait_ge(w_sum_s, q0 + q + 1)
            since(e, w_neg_s, 4 * q0, 4 * (q - 1))
            e.scalar_tensor_tensor(out=w_cen[p][:, :].rearrange("r (k o) -> r k o", o=C),
                                   in0=w_sum[p][:, :].unsqueeze(2).to_broadcast([128, 4 * NK, C]), scalar=-1.0 / C,
                                   in1=raw, op0=ALU.mult, op1=ALU.add).then_inc(w_cen_s, 1)

        def dve_mix(e, m, p, layer):
            q, q0 = 2 * m + p, NY * layer
            since(e, y_pe, 4 * q0, 4 * (q - 1))
            for s in range(4):
                kind = 2 * (1 if s in (1, 2) else 0)
                e.wait_ge(w_neg_s, 4 * (q0 + q) + s + 1)
                e.scalar_tensor_tensor(
                    out=w_mix[p][:, :].rearrange("r (k s o) -> r k s o", k=NK, s=4)[:, :, s, :],
                    in0=w_cen[p][:, NK * C * kind:NK * C * (kind + 1)].rearrange("r (k o) -> r k o", o=C),
                    scalar=const("sign")[:, 2 * s:2 * s + 1],
                    in1=w_neg[:, NK * C * s:NK * C * (s + 1)].rearrange("r (k o) -> r k o", o=C),
                    op0=ALU.mult, op1=ALU.add).then_inc(w_mix_s, 1)

        def pool_mix(e, m, p, layer):
            q, q0 = 2 * m + p, NY * layer
            e.wait_ge(w_cen_s, q0 + q + 1)
            for s in range(4):
                kind = 2 * (1 if s in (1, 2) else 0) + 1
                since(e, w_mix_s, 4 * q0, 4 * (q - 1) + s + 1)
                e.tensor_tensor(w_neg[:, NK * C * s:NK * C * (s + 1)], w_cen[p][:, NK * C * kind:NK * C * (kind + 1)],
                                const("sign")[:, 2 * s + 1:2 * s + 2].to_broadcast([128, NK * C]),
                                ALU.mult).then_inc(w_neg_s, 1)

        def sp_layer(e, n, layer, norm):
            if layer is not None:
                e.dma_start(conv_raw[:, :], io["conv_w"][layer]).then_inc(layer_in, 16)
                e.dma_start(bias_raw[:, :], io["conv_b"][layer].unsqueeze(1)).then_inc(layer_in, 16)
            g, b = norm
            for u in range(4):
                if layer is not None and u < 2:
                    e.wait_ge(st_a[u], 16 * halves * (layer + 1))
                elif layer is not None:
                    e.wait_ge(st_x[u - 2], 32 * halves * (layer + 1))
                e.dma_start(gain[32 * u:32 * u + 32, :], g.unsqueeze(1)).then_inc(layer_in, 16)
                e.dma_start(shift[32 * u:32 * u + 32, :], b.unsqueeze(1)).then_inc(layer_in, 16)

        def dve_layer(e, n):
            e.wait_ge(layer_in, 128 + 160 * (n + 1))
            e.tensor_copy(conv_rep[:, :].rearrange("o (g c) -> o g c", g=4),
                          conv_raw[:, :].unsqueeze(1).to_broadcast([C, 4, C])).then_inc(conv_set, 1)
            e.tensor_scalar(bias_cols[:, :], ones[0:C, :], bias_raw[:, 0:1], None, ALU.mult).then_inc(conv_set, 1)
            e.wait_ge(conv_pe, n + 1)
            e.tensor_copy(conv_col[:, :], TP[:, 0:C]).then_inc(conv_set, 1)
            e.wait_ge(conv_set, 4 * n + 3)
            e.tensor_tensor(conv_block[:, :].rearrange("p (g o) -> p g o", g=4),
                            const("maskc").rearrange("p (g o) -> p g o", g=4),
                            conv_col[:, :].unsqueeze(1).to_broadcast([128, 4, C]), ALU.mult).then_inc(conv_set, 1)

        def pe_layer(e, n):
            e.wait_ge(conv_set, 4 * n + 2)
            e.matmul(TP[:, 0:C], conv_rep[:, :], const("center"), start=True, stop=True).then_inc(conv_pe, 1)
            e.wait_ge(conv_set, 4 * n + 4)

        def whole_pass(fori, start, step, first, last):
            peeled = 2 if first or last else 1
            for m in range(peeled):
                step(start + m, 0, True, m > 0, first, last)
                step(start + m, 1, True, True, first, last)
            if halves > peeled:
                with fori(peeled, halves) as m:
                    step(start + m, 0, True, True, first, last)
                    step(start + m, 1, True, True, first, last)
            step(start + halves, 0, False, True, first, last)

        block = ctx.enter_context(nc.Block())

        @block.sync
        def _(e):
            fori = e.Fori
            e.dma_start(table[:, :], io["tables"]).then_inc(table_in, 16)
            e.dma_start(fc0_rows[0:3, :], io["fc0_w"]).then_inc(param_in, 16)
            e.dma_start(fc0_rows[3:4, :], io["fc0_b"].unsqueeze(0)).then_inc(param_in, 16)
            e.wait_ge(set_up, 5)
            for g in range(4):
                e.dma_start(fc1_pad[32 * g:32 * g + 32, 128 * g:128 * g + 128], io["fc1_w"]).then_inc(param_in, 16)
            e.dma_start(fc1_bias[:, :], io["fc1_b"].unsqueeze(1)).then_inc(param_in, 16)
            e.dma_start(fc2_w[:, :], io["fc2_w"]).then_inc(param_in, 16)
            for g in range(2):
                e.dma_start(fc2_bias[64 * g:64 * g + 64, :], io["fc2_b"].unsqueeze(1)).then_inc(param_in, 16)
                e.dma_start(fc3_pad[64 * g:64 * g + 64, g:g + 1], io["fc3_w"]).then_inc(param_in, 16)
            e.dma_start(fc3_bias[:, :], io["fc3_b"].partition_broadcast(128)).then_inc(param_in, 16)
            sp_layer(e, 0, None, (io["ln0_g"], io["ln0_b"]))

            def one_pass(first, last, start):
                base = start
                if first:
                    for p in range(2):
                        sp_load(e, 0, p, p, True)
                    if halves > 1:
                        sp_step(first, last, base, 0)
                    if halves > 2:
                        with fori(1, halves - 1) as m:
                            sp_step(first, last, base, m)
                else:
                    for p in range(2):
                        sp_load(e, base, p, p, False)
                    if halves > 1:
                        with fori(0, halves - 1) as m:
                            sp_step(first, last, base, m)
                for p in range(2):
                    sp_store(e, base + halves - 1, p, 2 * (halves - 1) + p, last)

            def sp_step(first, last, base, m):
                for p in range(2):
                    sp_load(e, base + m + 1, p, 2 * (m + 1) + p, first)
                    sp_store(e, base + m, p, 2 * m + p, last)

            def mix(layer):
                for p in range(2):
                    sp_mix_load(e, 0, p, layer)
                with fori(0, NY // 2 - 1) as m:
                    for p in range(2):
                        sp_mix_load(e, m + 1, p, layer)
                        sp_mix_store(e, m, p, layer)
                for p in range(2):
                    sp_mix_store(e, NY // 2 - 1, p, layer)

            def layer_body(layer, last):
                for p in range(2):
                    e.dma_start(w_raw[p][:, :], io["w_mix"][layer, p]).then_inc(w_in[p], 16)
                e.wait_ge(act_ready, 8 * halves * (layer + 1))
                sp_layer(e, layer + 1, layer, (io["ln_g"][layer], io["ln_b"][layer]))
                mix(layer)
                for p in range(2):
                    e.wait_ge(y_out[p], 16 * (NY // 2) * (layer + 1))
                one_pass(False, last, halves * (layer + 1))

            one_pass(True, False, 0)
            with fori(0, LAYERS - 1) as layer:
                layer_body(layer, False)
            layer_body(LAYERS - 1, True)
            for p in range(2):
                e.wait_ge(st_h[p], 16 * halves)

        @block.tensor
        def _(e):
            fori = e.Fori
            e.wait_ge(table_in, 16)
            e.wait_ge(set_up, 5)
            e.matmul(TP[0:97, 0:C], const("rinp"), fc0_center[:, :], start=True, stop=True).then_inc(prep_pe, 1)
            e.wait_ge(set_up, 7)
            whole_pass(fori, 0, lambda *at: pe_step(e, *at, None), True, False)

            def body(layer, last):
                e.wait_ge(h_ready, 8 * halves * (layer + 1))
                e.wait_ge(pix_ready, 8 * halves * (layer + 1))
                e.wait_ge(unit_ready, 8 * halves * (layer + 1))
                pe_layer(e, layer)
                for p in range(2):
                    pe_mix(e, 0, p, layer, p == 0)
                with fori(1, NY // 2) as m:
                    for p in range(2):
                        pe_mix(e, m, p, layer, False)
                if last:
                    e.wait_ge(param_in, 16 * 13)
                whole_pass(fori, halves * (layer + 1),
                           lambda *at: pe_step(e, *at, layer), False, last)

            with fori(0, LAYERS - 1) as layer:
                body(layer, False)
            body(LAYERS - 1, True)

        @block.scalar
        def _(e):
            fori = e.Fori
            e.preload_act_table_set("gelu_and_others")
            e.wait_ge(layer_in, 128)
            e.wait_ge(set_up, 3)
            step = lambda *at: act_step(e, *at)
            whole_pass(fori, 0, step, True, False)

            def body(layer, last):
                for p in range(2):
                    act_mix(e, 0, p, layer)
                with fori(1, NY // 2) as m:
                    for p in range(2):
                        act_mix(e, m, p, layer)
                e.wait_ge(layer_in, 128 + 160 * (layer + 1))
                if last:
                    e.wait_ge(param_in, 16 * 13)
                whole_pass(fori, halves * (layer + 1), step, False, last)

            with fori(0, LAYERS - 1) as layer:
                body(layer, False)
            body(LAYERS - 1, True)

        @block.vector
        def _(e):
            fori = e.Fori
            e.memset(fc1_pad[:, :], 0.0).then_inc(set_up, 1)
            e.memset(fc3_pad[:, :], 0.0).then_inc(set_up, 1)
            e.memset(image_t[96:97, :], 1.0).then_inc(set_up, 1)
            e.memset(ones[:, :], 1.0)
            e.memset(minus_half[:, :], -0.5)
            e.memset(eps[:, :], EPS)
            e.wait_ge(param_in, 32)
            e.tensor_reduce(fc0_mean[:, :], fc0_rows[:, :], AX.X, ALU.add).then_inc(set_up, 1)
            e.wait_ge(set_up, 4)
            e.scalar_tensor_tensor(out=fc0_center[:, :], in0=fc0_mean[:, 0:1].to_broadcast([4, C]), scalar=-1.0 / C,
                                   in1=fc0_rows[:, :], op0=ALU.mult, op1=ALU.add).then_inc(set_up, 1)
            e.wait_ge(prep_pe, 1)
            e.tensor_copy(fc0_rep[:, :], TP[0:97, 0:C]).then_inc(set_up, 1)
            e.wait_ge(set_up, 6)
            e.tensor_tensor(fc0_block[:, :].rearrange("p (y c) -> p y c", c=C),
                            const("maski").unsqueeze(2).to_broadcast([97, 32, C]),
                            fc0_rep[:, :].unsqueeze(1).to_broadcast([97, 32, C]), ALU.mult).then_inc(set_up, 1)
            step = lambda *at: dve_step(e, *at)
            whole_pass(fori, 0, step, True, False)

            def body(layer, last):
                dve_layer(e, layer)
                def two_ky(m, more):
                    dve_center(e, m, 1, layer)
                    dve_mix(e, m, 0, layer)
                    if more:
                        dve_center(e, m + 1, 0, layer)
                    dve_mix(e, m, 1, layer)

                dve_center(e, 0, 0, layer)
                two_ky(0, True)
                with fori(1, NY // 2 - 1) as m:
                    two_ky(m, True)
                two_ky(NY // 2 - 1, False)
                if last:
                    e.wait_ge(param_in, 16 * 13)
                whole_pass(fori, halves * (layer + 1), step, False, last)

            with fori(0, LAYERS - 1) as layer:
                body(layer, False)
            body(LAYERS - 1, True)

        @block.gpsimd
        def _(e):
            fori = e.Fori
            e.wait_ge(set_up, 7)
            step = lambda P, p, front, *at: pool_step(e, P, p, front)
            whole_pass(fori, 0, step, True, False)

            def body(layer, last):
                for p in range(2):
                    pool_mix(e, 0, p, layer)
                with fori(1, NY // 2) as m:
                    for p in range(2):
                        pool_mix(e, m, p, layer)
                whole_pass(fori, halves * (layer + 1), step, False, last)

            with fori(0, LAYERS - 1) as layer:
                body(layer, False)
            body(LAYERS - 1, True)

T = S + 1
D = S
NS = 16
R = 16
NH, HD, NKV = 4, 16, 2
NE = 8
HID = 170
HH = HID // 2
Q = 4
GI = 2 * Q
TOK = Q * T


def block_tables():
    t = {}
    t["ident"] = np.eye(128)
    t["mean"] = np.kron(np.eye(2), np.full((D, D), 1.0 / D))
    rot = np.zeros((HD, HD))
    for j in range(HD // 2):
        rot[j, j + HD // 2] = -1
        rot[j + HD // 2, j] = 1
    t["rot"] = np.kron(np.eye(2 * NH), rot).T
    inv = 1.0 / 10000.0 ** (np.arange(0, HD, 2, dtype=np.float32) / HD)
    freqs = np.outer(np.arange(T, dtype=np.float32), inv)
    emb = np.concatenate([freqs, freqs], axis=-1)
    t["cos"] = np.tile(np.cos(emb).T, (2 * NH, 1))
    t["sin"] = np.tile(np.sin(emb).T, (2 * NH, 1))
    t["heads"] = np.tile(np.kron(np.eye(NH), np.ones((HD, 1))), (2, 1)) * HD ** -0.5
    t["causal"] = np.where(np.tril(np.ones((T, T), bool)), 0.0, -1e30)
    t["order"] = np.tile((NE - np.arange(NE))[None, :], (T, 1))
    return {k: v.astype(np.float32) for k, v in t.items()}


def pack(tables):
    at, place, cols = 0, {}, []
    for name, v in tables.items():
        v = np.asarray(v)
        block = np.zeros((128, v.shape[1]), np.float32)
        block[:v.shape[0]] = v
        place[name] = (v.shape[0], at, at + v.shape[1])
        cols.append(block)
        at += v.shape[1]
    return np.concatenate(cols, axis=1), place


def twice(w):
    out = np.zeros((2, w.shape[0], 2, w.shape[1]), np.float32)
    out[0, :, 0], out[1, :, 1] = w, w
    return out.reshape(2 * w.shape[0], 2 * w.shape[1])


def stacked(w):
    return np.concatenate([w, w], axis=0)


def block_weights(a):
    t = {}
    wx = np.asarray(a["L0_attn_W_xproj"])
    wf = np.zeros((D, D), np.float32)
    wf[:, 0:3 * NS] = wx[R:].T
    t["wx"] = twice(wf)
    t["wxr"] = twice(wx[:R])
    t["wxb"] = twice(np.asarray(a["L0_attn_W_xbproj"]))
    t["wdt"] = twice(np.asarray(a["L0_attn_W_dt"]).T)
    t["b_dt"] = stacked(np.asarray(a["L0_attn_b_dt"])[:, None])
    t["a_log"] = stacked(np.asarray(a["L0_attn_A_log"]))
    t["d_skip"] = stacked(np.asarray(a["L0_attn_D_skip"])[:, None])
    t["wout"] = twice(np.asarray(a["L0_attn_W_out"]).T)
    t["ln1"] = stacked(np.asarray(a["L0_ffn_ln1_w"])[:, None])
    t["ln2"] = stacked(np.asarray(a["L0_ffn_ln2_w"])[:, None])
    wq = np.asarray(a["L0_ffn_wq"])
    wk = np.repeat(np.asarray(a["L0_ffn_wk"]).reshape(NKV, 1, HD, D), NH // NKV, axis=1).reshape(D, D)
    wv = np.repeat(np.asarray(a["L0_ffn_wv"]).reshape(NKV, 1, HD, D), NH // NKV, axis=1).reshape(D, D)
    t["wq_t"], t["wq"] = twice(wq.T), twice(wq)
    t["wk_t"], t["wk"] = twice(wk.T), twice(wk)
    t["wv"] = twice(wv.T)
    t["wo"] = twice(np.asarray(a["L0_ffn_wo"]).T)
    t["router"] = twice(np.asarray(a["L0_ffn_router_w"]).T)
    t["cls"] = stacked(np.asarray(a["cls_tok"]).reshape(D, 1))
    for n in ("w1", "w3"):
        t[n] = stacked(np.transpose(np.asarray(a["L0_ffn_" + n]), (2, 0, 1)).reshape(D, NE * HID))
    w2 = np.transpose(np.asarray(a["L0_ffn_w2"]), (2, 0, 1)).reshape(2, HH, NE, D)
    t["w2"] = np.transpose(w2, (1, 2, 0, 3)).reshape(HH, NE * 2 * D)
    return t


def build_block(nc, io, tplace, wplace, h0, out):
    groups = NI // GI
    with ExitStack() as ctx:
        def sb(name, shape):
            return ctx.enter_context(nc.sbuf_tensor("blk_" + name, shape, F32))

        def sem(name):
            return ctx.enter_context(nc.semaphore("b_" + name))

        tables = sb("tables", [128, max(p[2] for p in tplace.values())])
        weights = sb("weights", [128, max(p[2] for p in wplace.values())])

        def const(name):
            r, a, b = tplace[name]
            return tables[0:r, a:b]

        def wt(name):
            r, a, b = wplace[name]
            return weights[0:r, a:b]

        w_delta = sb("w_delta", [128, 128])
        w_delta_b = sb("w_delta_b", [128, 128])
        wq_rot = sb("wq_rot", [128, 128])
        wk_rot = sb("wk_rot", [128, 128])
        wskip = sb("wskip", [128, 128])
        neg_a = sb("neg_a", [128, NS])
        select = sb("select", [128, 3 * NS * 128])
        rows = sb("rows", [S, GI * D])
        h_in = sb("h_in", [128, TOK])
        cen = sb("cen", [128, TOK])
        sqr = sb("sqr", [128, TOK])
        log = sb("log", [128, TOK])
        ve = sb("ve", [128, TOK])
        y0 = sb("y0", [128, TOK])
        y1 = sb("y1", [128, TOK])
        rs = sb("rs", [128, TOK])
        xn = sb("xn", [128, TOK])
        xf = sb("xf", [128, TOK])
        mag = [sb(f"mag{k}", [128, TOK]) for k in range(2)]
        soft = [sb(f"soft{k}", [128, TOK]) for k in range(2)]
        pos = [sb(f"pos{k}", [128, TOK]) for k in range(2)]
        delta = [sb(f"delta{k}", [128, TOK]) for k in range(2)]
        du = sb("du", [128, TOK])
        dub = sb("dub", [128, TOK])
        bc = sb("bc", [128, TOK])
        dA = sb("dA", [128, NS * TOK])
        dB = sb("dB", [128, NS * TOK])
        dB2 = [sb(f"dB2_{p}", [128, TOK]) for p in range(2)]
        h1 = sb("h1", [128, TOK])
        r = sb("r", [128, TOK])
        un = sb("un", [128, TOK])
        qf = sb("qf", [128, TOK])
        kf = sb("kf", [128, TOK])
        tmp = sb("tmp", [128, TOK])
        kx = dA[:, 0:Q * NH * T]
        sc = dB[0:T, 0:GI * NH * T]
        pt = [sb(f"pt{p}", [T, NH * T]) for p in range(2)]
        v_sb = sb("v", [T, GI * D])
        mx = sb("mx", [T, GI * NH])
        sm = sb("sm", [T, GI * NH])
        rc = sb("rc", [T, GI * NH])
        yn = sb("yn", [T, GI * D])
        yt = sb("yt", [128, TOK])
        x2 = sb("x2", [128, TOK])
        lg = [sb(f"lg{k}", [T, GI * NE]) for k in range(6)]
        st = [sb(f"st{k}", [T, GI]) for k in range(6)]
        silu = [sb(f"silu{p}", [HH, TOK]) for p in range(2)]
        hid = [[sb(f"hid{p}{k}", [HH, TOK]) for k in range(4)] for p in range(2)]
        acc = [sb(f"acc{p}", [T, GI * D]) for p in range(2)]
        part = sb("part", [T, GI * D])
        res = sb("res", [128, TOK])
        fin = sb("fin", [T, GI * D])
        B = [ctx.enter_context(nc.psum_tensor(f"bank{j}", [128, 512], F32)) for j in range(8)]

        PER = dict(
            rows_t=1, h_in=2, mean=2, cen=2, square=4, variance=4, var_eps=4, log=4, guess=4, newton=12, scale=4,
            normed=4, flipped=1, proj=1, soft_mag=2, soft_exp=2, soft_log=2, soft_pos=2, delta=2, du=2, bc=1,
            decay=NS, reset=1, bcast=NS, drive=NS, input=NS, scan=1, c_cast=NS, read=NS, scan_out=1, h1=1,
            qk=1, v=1, v_copied=1, rope=6, kx=Q, scores=GI, masked=GI, peak=1, shifted=1, expd=1, total=1, recip=1,
            p_turned=GI, p_copied=GI, yv=1, y_norm=1, y_turned=1, y_copied=1, wo=1, x2=1, router=1, gate=21,
            gate_exp=1, up=4 * NE, silu=4 * NE, hidden=4 * NE, down=NE, gated=NE, summed=NE, residual=1, res_turned=1,
            fin=1)
        sig = {name: sem(name) for name in PER}
        loaded = sem("weights_loaded")
        rows_in = sem("rows_in")
        stored = sem("stored")
        prep = sem("prepared")
        prep_pe = sem("prepared_pe")
        prep_act = sem("prepared_act")

        def wait(e, name, g, c=None):
            e.wait_ge(sig[name], PER[name] * g + (PER[name] if c is None else c))

        def by_token(ap):
            return ap.rearrange("p (q t) -> p q t", t=T)

        h0_rows = h0.rearrange("(g m) x y -> g x m y", m=GI)
        out_rows = out.rearrange("(g m) t d -> g t m d", m=GI)
        IMAGES = [(q, i) for q in range(Q) for i in range(2)]
        block = ctx.enter_context(nc.Block())

        @block.sync
        def _(e):
            e.dma_start(tables[:, :], io["block_tables"]).then_inc(loaded, 16)
            e.dma_start(weights[:, :], io["block_weights"]).then_inc(loaded, 16)

            def load(g):
                e.dma_start(rows[:, :].rearrange("x (m y) -> x m y", m=GI), h0_rows[g]).then_inc(rows_in, 16)

            def store(g):
                wait(e, "fin", g)
                e.dma_start(out_rows[g], fin[:, :].rearrange("t (m d) -> t m d", m=GI)).then_inc(stored, 16)

            load(0)
            with e.Fori(0, groups - 1) as g:
                store(g)
                e.wait_ge(stored, 16 * (g + 1))
                load(g + 1)
            store(groups - 1)
            e.wait_ge(stored, 16 * groups)

        NORMS = ((0, True), (1, True), (2, False), (3, False))

        @block.tensor
        def _(e):
            e.wait_ge(loaded, 32)
            e.matmul(B[0][:, 0:128], wt("wxr"), wt("wdt"), start=True, stop=True)
            e.matmul(B[1][:, 0:128], wt("wxb"), wt("wdt"), start=True, stop=True)
            e.matmul(B[2][:, 0:128], wt("wq"), const("rot"), start=True, stop=True)
            e.matmul(B[3][:, 0:128], wt("wk"), const("rot"), start=True, stop=True).then_inc(prep_pe, 1)
            e.wait_ge(prep, 7)

            def norm(g, k, centred, src):
                if centred:
                    e.matmul(B[1][:, 0:TOK], const("mean"), src[:, :], start=True, stop=True).then_inc(sig["mean"], 1)
                wait(e, "square", g, k + 1)
                e.matmul(B[2][:, 0:TOK], const("mean"), sqr[:, :], start=True, stop=True).then_inc(sig["variance"], 1)

            with e.Fori(0, groups) as g:
                e.wait_ge(rows_in, 16 * (g + 1))
                for q in range(Q):
                    mm = e.matmul(B[0][:, T * q + 1:T * q + T], rows[:, 128 * q:128 * q + 128],
                                  const("ident")[0:S, 0:S], start=True, stop=True, skip_group_check=True)
                mm.then_inc(sig["rows_t"], 1)
                wait(e, "h_in", g)
                norm(g, 0, True, h_in)
                wait(e, "normed", g, 1)
                wait(e, "flipped", g)
                e.matmul(B[0][:, 0:TOK], w_delta[:, :], xn[:, :], start=True, stop=True)
                e.matmul(B[1][:, 0:TOK], w_delta_b[:, :], xf[:, :], start=True, stop=True)
                e.matmul(B[2][:, 0:TOK], wt("wx"), xn[:, :], start=True, stop=True).then_inc(sig["proj"], 1)
                wait(e, "bc", g)

                def spread(row, bank):
                    return e.matmul(B[bank][:, 0:TOK], select[:, 128 * row:128 * row + 128], bc[:, :],
                                    start=True, stop=True)

                for n in range(NS):
                    if n >= 2:
                        wait(e, "drive", g, n - 1)
                    spread(n, 3 + 2 * (n % 2))
                    spread(NS + n, 4 + 2 * (n % 2)).then_inc(sig["bcast"], 1)
                e.matmul(B[7][:, 0:TOK], wskip[:, :], xn[:, :], start=True, stop=False)
                e.matmul(B[7][:, 0:TOK], wskip[:, :], xf[:, :], start=False, stop=False)
                wait(e, "drive", g)
                for n in range(NS + 1):
                    if n < NS:
                        if n >= 2:
                            wait(e, "read", g, n - 1)
                        spread(2 * NS + n, 3 + n % 2).then_inc(sig["c_cast"], 1)
                    if n > 0:
                        wait(e, "read", g, n)
                        mm = e.matmul(B[7][:, 0:TOK], wt("wout"), dB[:, TOK * (n - 1):TOK * n],
                                      start=False, stop=(n == NS))
                mm.then_inc(sig["scan_out"], 1)
                wait(e, "h1", g)
                norm(g, 1, True, h1)
                norm(g, 2, False, None)
                wait(e, "normed", g, 3)
                for b, w in enumerate((wt("wq_t"), wq_rot[:, :], wt("wk_t"), wk_rot[:, :])):
                    if b == 2:
                        wait(e, "var_eps", g, 3)
                    mm = e.matmul(B[b][:, 0:TOK], w, un[:, :], start=True, stop=True)
                mm.then_inc(sig["qk"], 1)
                for q in range(Q):
                    mm = e.matmul(B[4][0:T, 128 * q:128 * q + 128], un[:, T * q:T * q + T], wt("wv"),
                                  start=True, stop=True, skip_group_check=True)
                mm.then_inc(sig["v"], 1)
                wait(e, "rope", g)
                for m, (q, i) in enumerate(IMAGES):
                    a = 64 * i
                    wait(e, "kx", g, q + 1)
                    if m >= 4:
                        wait(e, "masked", g, m - 3)
                    e.matmul(B[m % 4][0:T, 0:NH * T], qf[a:a + 64, T * q:T * q + T],
                             kx[a:a + 64, NH * T * q:NH * T * (q + 1)], start=True, stop=True).then_inc(sig["scores"], 1)
                wait(e, "expd", g)
                wait(e, "v_copied", g)
                for m in range(GI + 1):
                    if m < GI:
                        if m >= 2:
                            wait(e, "p_copied", g, m - 1)
                        for h in range(NH):
                            mm = e.transpose(B[m % 2][0:T, T * h:T * h + T],
                                             sc[:, T * (NH * m + h):T * (NH * m + h) + T], const("ident")[0:T, 0:T])
                        mm.then_inc(sig["p_turned"], 1)
                    if m > 0:
                        wait(e, "p_copied", g, m)
                        for h in range(NH):
                            at = D * (m - 1) + HD * h
                            mm = e.matmul(B[5][0:T, at:at + HD], pt[(m - 1) % 2][:, T * h:T * h + T],
                                          v_sb[:, at:at + HD], start=True, stop=True, skip_group_check=True)
                mm.then_inc(sig["yv"], 1)
                wait(e, "y_norm", g)
                for m, (q, i) in enumerate(IMAGES):
                    mm = e.matmul(B[2][64 * i:64 * i + 64, T * q:T * q + T], yn[:, D * m:D * m + D],
                                  const("ident")[0:T, 0:T], start=True, stop=True, skip_group_check=True)
                mm.then_inc(sig["y_turned"], 1)
                wait(e, "y_copied", g)
                e.matmul(B[3][:, 0:TOK], wt("wo"), yt[:, :], start=True, stop=True).then_inc(sig["wo"], 1)
                wait(e, "x2", g)
                norm(g, 3, False, None)
                wait(e, "normed", g, 4)
                for q in range(Q):
                    mm = e.matmul(B[6][0:T, 2 * NE * q:2 * NE * (q + 1)], un[:, T * q:T * q + T], wt("router"),
                                  start=True, stop=True, skip_group_check=True)
                mm.then_inc(sig["router"], 1)
                for x in range(NE + 1):
                    if x < NE:
                        for k in range(4):
                            i, half, n = k // 2, k % 2, 4 * x + k
                            a, c = 64 * i, HID * x + HH * half
                            if n >= 2:
                                wait(e, "hidden", g, n - 1)
                            e.matmul(B[2 * (n % 2)][0:HH, 0:TOK], wt("w1")[a:a + 64, c:c + HH], un[a:a + 64, :],
                                     start=True, stop=True)
                            e.matmul(B[2 * (n % 2) + 1][0:HH, 0:TOK], wt("w3")[a:a + 64, c:c + HH], un[a:a + 64, :],
                                     start=True, stop=True).then_inc(sig["up"], 1)
                    if x > 0:
                        y = x - 1
                        wait(e, "hidden", g, 4 * y + 4)
                        if y >= 2:
                            wait(e, "gated", g, y - 1)
                        for m, (q, i) in enumerate(IMAGES):
                            for half in range(2):
                                mm = e.matmul(B[4 + y % 2][0:T, D * m:D * m + D],
                                              hid[y % 2][2 * i + half][:, T * q:T * q + T],
                                              wt("w2")[:, D * (2 * y + half):D * (2 * y + half) + D],
                                              start=(half == 0), stop=(half == 1), skip_group_check=True)
                        mm.then_inc(sig["down"], 1)
                wait(e, "residual", g)
                for q in range(Q):
                    mm = e.matmul(B[7][0:T, 128 * q:128 * q + 128], res[:, T * q:T * q + T], const("ident"),
                                  start=True, stop=True, skip_group_check=True)
                mm.then_inc(sig["res_turned"], 1)

        @block.scalar
        def _(e):
            e.preload_act_table_set("natural_log_exp_and_others")
            e.wait_ge(loaded, 32)
            e.activation(neg_a[:, :], wt("a_log"), ACT.Exp).then_inc(prep_act, 1)

            def norm(g, k):
                if k < 2:
                    wait(e, "cen", g, k + 1)
                elif k == 2:
                    wait(e, "normed", g, 2)
                else:
                    wait(e, "x2", g)
                src = (cen, cen, r, x2)[k]
                e.activation(sqr[:, :], src[:, :], ACT.Square).then_inc(sig["square"], 1)
                wait(e, "var_eps", g, k + 1)
                e.activation(log[:, :], ve[:, :], ACT.Ln).then_inc(sig["log"], 1)
                wait(e, "log", g, k + 1)
                e.activation(y0[:, :], log[:, :], ACT.Exp, scale=-0.5).then_inc(sig["guess"], 1)

            with e.Fori(0, groups) as g:
                norm(g, 0)
                wait(e, "proj", g)
                e.activation(bc[:, :], B[2][:, 0:TOK], ACT.Copy).then_inc(sig["bc"], 1)
                for k in range(2):
                    e.activation(mag[k][:, :], B[k][:, 0:TOK], ACT.Abs, bias=wt("b_dt")).then_inc(sig["soft_mag"], 1)
                for k in range(2):
                    wait(e, "soft_mag", g, k + 1)
                    e.activation(soft[k][:, :], mag[k][:, :], ACT.Exp, scale=-1.0).then_inc(sig["soft_exp"], 1)
                for k in range(2):
                    wait(e, "soft_exp", g, k + 1)
                    e.activation(mag[k][:, :], soft[k][:, :], ACT.Ln, bias=1.0).then_inc(sig["soft_log"], 1)
                wait(e, "delta", g, 1)
                for n in range(NS):
                    e.activation(dA[:, TOK * n:TOK * n + TOK], delta[0][:, :], ACT.Exp,
                                 scale=neg_a[:, n:n + 1]).then_inc(sig["decay"], 1)
                norm(g, 1)
                norm(g, 2)
                wait(e, "v", g)
                e.activation(v_sb[:, :], B[4][0:T, :], ACT.Copy).then_inc(sig["v_copied"], 1)
                wait(e, "shifted", g)
                e.activation(sc, sc, ACT.Exp).then_inc(sig["expd"], 1)
                for m in range(GI):
                    wait(e, "p_turned", g, m + 1)
                    e.activation(pt[m % 2][:, :], B[m % 2][0:T, 0:NH * T], ACT.Copy).then_inc(sig["p_copied"], 1)
                wait(e, "y_turned", g)
                e.activation(yt[:, :], B[2][:, 0:TOK], ACT.Copy).then_inc(sig["y_copied"], 1)
                norm(g, 3)
                wait(e, "gate", g, 2)
                e.activation(lg[1][:, :], lg[0][:, :], ACT.Exp).then_inc(sig["gate_exp"], 1)
                for n in range(4 * NE):
                    wait(e, "up", g, n + 1)
                    if n >= 2:
                        wait(e, "hidden", g, n - 1)
                    e.activation(silu[n % 2][:, :], B[2 * (n % 2)][0:HH, 0:TOK], ACT.Silu).then_inc(sig["silu"], 1)

        @block.vector
        def _(e):
            e.wait_ge(prep_pe, 1)
            for k, w in enumerate((w_delta, w_delta_b, wq_rot, wk_rot)):
                e.tensor_copy(w[:, :], B[k][:, 0:128]).then_inc(prep, 1)
            e.tensor_scalar(wskip[:, :], wt("wout"), wt("d_skip"), None, ALU.mult).then_inc(prep, 1)
            e.wait_ge(prep_act, 1)
            e.tensor_scalar(neg_a[:, :], neg_a[:, :], -1.0, None, ALU.mult).then_inc(prep, 1)
            for row in range(3 * NS):
                cp = e.tensor_copy(select[:, 128 * row:128 * row + 128].rearrange("p (i d) -> p i d", i=2),
                                   const("ident").rearrange("p (i d) -> p i d", i=2)[:, :, row:row + 1]
                                   .to_broadcast([128, 2, D]))
            cp.then_inc(prep, 1)

            def norm(g, k, src, dst, eps, weight):
                if k < 2:
                    wait(e, "mean", g, k + 1)
                    e.tensor_tensor(cen[:, :], src[:, :], B[1][:, 0:TOK], ALU.subtract).then_inc(sig["cen"], 1)
                    src = cen
                wait(e, "variance", g, k + 1)
                e.tensor_scalar(ve[:, :], B[2][:, 0:TOK], eps, None, ALU.add).then_inc(sig["var_eps"], 1)
                wait(e, "guess", g, k + 1)
                e.tensor_tensor(y1[:, :], y0[:, :], y0[:, :], ALU.mult).then_inc(sig["newton"], 1)
                wait(e, "newton", g, 3 * k + 1)
                e.tensor_tensor(rs[:, :], y1[:, :], ve[:, :], ALU.mult).then_inc(sig["newton"], 1)
                wait(e, "newton", g, 3 * k + 2)
                e.tensor_scalar(y1[:, :], rs[:, :], -0.5, 1.5, ALU.mult, ALU.add).then_inc(sig["newton"], 1)
                wait(e, "newton", g, 3 * k + 3)
                e.tensor_tensor(rs[:, :], y1[:, :], y0[:, :], ALU.mult).then_inc(sig["scale"], 1)
                wait(e, "scale", g, k + 1)
                if weight is None:
                    e.tensor_tensor(dst[:, :], src[:, :], rs[:, :], ALU.mult).then_inc(sig["normed"], 1)
                else:
                    e.scalar_tensor_tensor(out=dst[:, :], in0=src[:, :], scalar=weight, in1=rs[:, :],
                                           op0=ALU.mult, op1=ALU.mult).then_inc(sig["normed"], 1)

            with e.Fori(0, groups) as g:
                wait(e, "rows_t", g)
                e.tensor_copy(by_token(h_in[:, :])[:, :, 1:T], by_token(B[0][:, 0:TOK])[:, :, 1:T])\
                    .then_inc(sig["h_in"], 1)
                e.tensor_copy(by_token(h_in[:, :])[:, :, 0:1], wt("cls").unsqueeze(1).to_broadcast([128, Q, 1]))\
                    .then_inc(sig["h_in"], 1)
                wait(e, "h_in", g)
                norm(g, 0, h_in, xn, EPS, None)
                wait(e, "normed", g, 1)
                e.tensor_copy(by_token(xf[:, :]), by_token(xn[:, :])[:, :, ::-1]).then_inc(sig["flipped"], 1)
                wait(e, "soft_mag", g)
                for k in range(2):
                    e.tensor_scalar(pos[k][:, :], B[k][:, 0:TOK], wt("b_dt"), 0.0, ALU.add, ALU.max)\
                        .then_inc(sig["soft_pos"], 1)
                for k in range(2):
                    wait(e, "soft_pos", g, k + 1)
                    wait(e, "soft_log", g, k + 1)
                    e.tensor_tensor(delta[k][:, :], pos[k][:, :], mag[k][:, :], ALU.add).then_inc(sig["delta"], 1)
                for k, (dst, src) in enumerate(((du, xn), (dub, xf))):
                    wait(e, "delta", g, k + 1)
                    e.tensor_tensor(dst[:, :], delta[k][:, :], src[:, :], ALU.mult).then_inc(sig["du"], 1)
                wait(e, "du", g)
                for n in range(NS):
                    wait(e, "bcast", g, n + 1)
                    e.tensor_tensor(dB[:, TOK * n:TOK * n + TOK], B[3 + 2 * (n % 2)][:, 0:TOK], du[:, :], ALU.mult)
                    if n >= 2:
                        wait(e, "input", g, n - 1)
                    e.tensor_tensor(dB2[n % 2][:, :], B[4 + 2 * (n % 2)][:, 0:TOK], dub[:, :], ALU.mult)\
                        .then_inc(sig["drive"], 1)
                wait(e, "decay", g)
                e.memset(dA[:, :].rearrange("p (n t) -> p n t", t=T)[:, :, 0:1], 0.0).then_inc(sig["reset"], 1)
                wait(e, "input", g)
                wait(e, "reset", g)
                e.tensor_tensor_scan(dB[:, :], dA[:, :], dB[:, :], 0.0, ALU.mult, ALU.add).then_inc(sig["scan"], 1)
                wait(e, "scan", g)
                for n in range(NS):
                    wait(e, "c_cast", g, n + 1)
                    e.tensor_tensor(dB[:, TOK * n:TOK * n + TOK], dB[:, TOK * n:TOK * n + TOK],
                                    B[3 + n % 2][:, 0:TOK], ALU.mult).then_inc(sig["read"], 1)
                wait(e, "scan_out", g)
                e.tensor_tensor(h1[:, :], h_in[:, :], B[7][:, 0:TOK], ALU.add).then_inc(sig["h1"], 1)
                wait(e, "h1", g)
                norm(g, 1, h1, r, EPS, None)
                wait(e, "normed", g, 2)
                norm(g, 2, r, un, 1e-6, wt("ln1"))
                wait(e, "qk", g)
                for k, dst in enumerate((qf, kf)):
                    cos = const("cos").unsqueeze(1).to_broadcast([128, Q, T])
                    sin = const("sin").unsqueeze(1).to_broadcast([128, Q, T])
                    if k:
                        wait(e, "rope", g, 3)
                    e.tensor_tensor(by_token(dst[:, :]), by_token(B[2 * k][:, 0:TOK]), cos, ALU.mult)\
                        .then_inc(sig["rope"], 1)
                    e.tensor_tensor(by_token(tmp[:, :]), by_token(B[2 * k + 1][:, 0:TOK]), sin, ALU.mult)\
                        .then_inc(sig["rope"], 1)
                    wait(e, "rope", g, 3 * k + 2)
                    e.tensor_tensor(dst[:, :], dst[:, :], tmp[:, :], ALU.add).then_inc(sig["rope"], 1)
                wait(e, "rope", g)
                for q in range(Q):
                    e.tensor_tensor(kx[:, NH * T * q:NH * T * (q + 1)].rearrange("p (h t) -> p h t", t=T),
                                    kf[:, T * q:T * q + T].unsqueeze(1).to_broadcast([128, NH, T]),
                                    const("heads").unsqueeze(2).to_broadcast([128, NH, T]), ALU.mult)\
                        .then_inc(sig["kx"], 1)
                rows_v = sc.rearrange("t (m s) -> t m s", s=T)
                for m in range(GI):
                    wait(e, "scores", g, m + 1)
                    e.tensor_tensor(rows_v[:, NH * m:NH * m + NH, :],
                                    B[m % 4][0:T, 0:NH * T].rearrange("t (h s) -> t h s", s=T),
                                    const("causal").unsqueeze(1).to_broadcast([T, NH, T]), ALU.add)\
                        .then_inc(sig["masked"], 1)
                wait(e, "masked", g)
                e.tensor_reduce(mx[:, :], rows_v, AX.X, ALU.max).then_inc(sig["peak"], 1)
                wait(e, "peak", g)
                e.tensor_tensor(rows_v, rows_v, mx[:, :].unsqueeze(2).to_broadcast([T, GI * NH, T]), ALU.subtract)\
                    .then_inc(sig["shifted"], 1)
                wait(e, "expd", g)
                e.tensor_reduce(sm[:, :], rows_v, AX.X, ALU.add).then_inc(sig["total"], 1)
                wait(e, "total", g)
                e.reciprocal(rc[:, :], sm[:, :]).then_inc(sig["recip"], 1)
                wait(e, "recip", g)
                wait(e, "yv", g)
                e.tensor_tensor(yn[:, :].rearrange("t (m d) -> t m d", d=HD),
                                B[5][0:T, :].rearrange("t (m d) -> t m d", d=HD),
                                rc[:, :].unsqueeze(2).to_broadcast([T, GI * NH, HD]), ALU.mult)\
                    .then_inc(sig["y_norm"], 1)
                wait(e, "wo", g)
                e.tensor_tensor(x2[:, :], r[:, :], B[3][:, 0:TOK], ALU.add).then_inc(sig["x2"], 1)
                wait(e, "x2", g)
                norm(g, 3, x2, un, 1e-6, wt("ln2"))
                e.tensor_tensor(res[:, :], h1[:, :], x2[:, :], ALU.add).then_inc(sig["residual"], 1)

                def e8(ap):
                    return ap.rearrange("t (m e) -> t m e", e=NE)

                def over(ap):
                    return ap.unsqueeze(2).to_broadcast([T, GI, NE])

                count = [0]

                def step(ins):
                    count[0] += 1
                    ins.then_inc(sig["gate"], 1)
                    wait(e, "gate", g, count[0])

                order = const("order").unsqueeze(1).to_broadcast([T, GI, NE])
                wait(e, "router", g)
                logits = e8(B[6][0:T, 0:GI * NE])
                step(e.tensor_reduce(st[0][:, :], logits, AX.X, ALU.max))
                step(e.tensor_tensor(e8(lg[0][:, :]), logits, over(st[0][:, :]), ALU.subtract))
                wait(e, "gate_exp", g)
                step(e.tensor_reduce(st[1][:, :], e8(lg[1][:, :]), AX.X, ALU.add))
                step(e.reciprocal(st[2][:, :], st[1][:, :]))
                step(e.tensor_tensor(e8(lg[0][:, :]), e8(lg[1][:, :]), over(st[2][:, :]), ALU.mult))

                def top(probs, peak, code, chosen):
                    step(e.tensor_reduce(st[peak][:, :], e8(lg[probs][:, :]), AX.X, ALU.max))
                    step(e.tensor_tensor(e8(lg[code][:, :]), e8(lg[probs][:, :]), over(st[peak][:, :]), ALU.is_equal))
                    step(e.tensor_tensor(e8(lg[code][:, :]), e8(lg[code][:, :]), order, ALU.mult))
                    step(e.tensor_reduce(st[0][:, :], e8(lg[code][:, :]), AX.X, ALU.max))
                    step(e.tensor_tensor(e8(lg[chosen][:, :]), e8(lg[code][:, :]), over(st[0][:, :]), ALU.is_equal))

                top(0, 3, 1, 2)
                step(e.scalar_tensor_tensor(out=lg[3][:, :], in0=lg[2][:, :], scalar=-2.0, in1=lg[0][:, :],
                                            op0=ALU.mult, op1=ALU.add))
                top(3, 4, 1, 4)
                step(e.tensor_tensor(lg[2][:, :], lg[2][:, :], lg[4][:, :], ALU.add))
                step(e.tensor_tensor(lg[2][:, :], lg[2][:, :], lg[0][:, :], ALU.mult))
                step(e.scalar_tensor_tensor(out=st[5][:, :], in0=st[3][:, :], scalar=1e-9, in1=st[4][:, :],
                                            op0=ALU.add, op1=ALU.add))
                step(e.reciprocal(st[1][:, :], st[5][:, :]))
                step(e.tensor_tensor(e8(lg[5][:, :]), e8(lg[2][:, :]), over(st[1][:, :]), ALU.mult))
                assert count[0] == PER["gate"], count

                def gated(x):
                    wait(e, "down", g, x + 1)
                    o = B[4 + x % 2][0:T, :].rearrange("t (m d) -> t m d", d=D)
                    w = e8(lg[5][:, :])[:, :, x:x + 1].to_broadcast([T, GI, D])
                    dst = acc[0] if x == 0 else part
                    if x > 1:
                        wait(e, "summed", g, x)
                    e.tensor_tensor(dst[:, :].rearrange("t (m d) -> t m d", d=D), o, w, ALU.mult)\
                        .then_inc(sig["gated"], 1)
                    wait(e, "gated", g, x + 1)
                    if x == 0:
                        e.tensor_copy(acc[1][:, 0:1], acc[0][:, 0:1]).then_inc(sig["summed"], 1)
                    else:
                        e.tensor_tensor(acc[0][:, :], acc[0][:, :], part[:, :], ALU.add).then_inc(sig["summed"], 1)

                for n in range(4 * NE):
                    x = n // 4
                    if n % 4 == 0 and x >= 2:
                        wait(e, "down", g, x - 1)
                    wait(e, "silu", g, n + 1)
                    e.tensor_tensor(hid[x % 2][n % 4][:, :], silu[n % 2][:, :], B[2 * (n % 2) + 1][0:HH, 0:TOK],
                                    ALU.mult).then_inc(sig["hidden"], 1)
                    if n % 4 == 3 and x > 0:
                        gated(x - 1)
                gated(NE - 1)
                wait(e, "summed", g)
                wait(e, "res_turned", g)
                e.tensor_tensor(fin[:, :], acc[0][:, :], B[7][0:T, :], ALU.add).then_inc(sig["fin"], 1)

        @block.gpsimd
        def _(e):
            with e.Fori(0, groups) as g:
                for n in range(NS):
                    wait(e, "drive", g, n + 1)
                    e.tensor_tensor(dB[:, TOK * n:TOK * n + TOK], dB[:, TOK * n:TOK * n + TOK], dB2[n % 2][:, :],
                                    ALU.add).then_inc(sig["input"], 1)


_TOKENIZER = ['x', 'fc0_w', 'fc0_b', 'ln0_g', 'ln0_b', 'conv_w', 'conv_b', 'ln_g', 'ln_b', 'fc1_w', 'fc1_b',
              'fc2_w', 'fc2_b', 'fc3_w', 'fc3_b']
_OUTS = [((NI, T, D), 'float32')]


def build(nc, io, out, place, block_place, weight_place):
    h0 = nc.dram_tensor("tokens", (NI, S, S), F32).ap()
    build_tokenizer(nc, io, place, h0)
    build_block(nc, io, block_place, weight_place, h0, out)


def kernel(**inputs):
    import numpy as _np
    import concourse.bacc as _bacc
    from concourse import mybir as _mybir
    from concourse.bass_utils import run_bass_kernel_spmd as _run

    a = {name: _np.asarray(v) for name, v in inputs.items()}
    laid = {name: a[name if name == 'x' else 'L0_tok_' + name] for name in _TOKENIZER}
    laid["tables"], place = pack(constants())
    laid["w_mix"] = mixing_weights(*(a['L0_tok_' + name] for name in ('w1r', 'w1i', 'w2r', 'w2i')))
    laid["block_tables"], block_place = pack(block_tables())
    laid["block_weights"], weight_place = pack(block_weights(a))

    nc = _bacc.Bacc("TRN2", target_bir_lowering=False, num_devices=1)
    arrays, io = {}, {}
    for name, v in laid.items():
        v = _np.ascontiguousarray(v)
        arrays[f"in_{name}_dram"] = v
        io[name] = nc.dram_tensor(f"in_{name}_dram", v.shape, _mybir.dt.from_np(v.dtype), kind="ExternalInput").ap()
    outs = [nc.dram_tensor(f"out_{i}_dram", shape, _mybir.dt.from_np(_np.dtype(dtype)), kind="ExternalOutput").ap()
            for i, (shape, dtype) in enumerate(_OUTS)]
    build(nc, io, outs[0], place, block_place, weight_place)
    r = _run(nc, [arrays], core_ids=[0])
    return r.results[0]["out_0_dram"]
```

```python
from contextlib import ExitStack

import concourse.bass as bass
import numpy as np
from concourse import mybir

F32 = mybir.dt.float32
ACT = mybir.ActivationFunctionType
ALU = mybir.AluOpType
AX = mybir.AxisListType

NI = 128
S = 64
C = 32
LAYERS = 4
NK = 13
NY = 12
T26 = 2 * NK
B24 = 2 * NY
PX = 2048
CH = 512
MODE = 4 * C
EPS = 1e-5


def constants():
    x = np.arange(S)
    ang = 2 * np.pi / S
    bx = np.zeros((S, NK, 2))
    by = np.zeros((S, NY, 2))
    for k in range(NK):
        bx[:, k, 0], bx[:, k, 1] = np.cos(ang * k * x), np.sin(ang * k * x)
    for k in range(NY):
        by[:, k, 0], by[:, k, 1] = np.cos(ang * k * x), np.sin(ang * k * x)
    bx, by = bx.reshape(S, T26), by.reshape(S, B24)
    alpha = np.repeat(np.where(np.arange(NY) == 0, 1.0, 2.0) / (S * S), 2)
    t = {}
    t["ident"] = np.eye(128)
    forward = bx.reshape(S, NK, 2).transpose(0, 2, 1).reshape(S, T26)
    t["f1"] = np.kron(np.eye(2), forward)
    t["f2"] = np.kron(by, np.eye(2))
    t["ga"] = np.kron(np.eye(2), bx.T)
    t["gb"] = np.kron((by * alpha).T, np.eye(4))
    t["maskc"] = np.kron(np.eye(4), np.ones((C, C)))
    t["center"] = np.eye(C) - 1.0 / C
    t["center_dc"] = (np.eye(C) - 1.0 / C) * (S * S)
    r = np.zeros((4, 97))
    for p in range(96):
        r[p % 3, p] = 1
    r[3, 96] = 1
    t["rinp"] = r
    m = np.zeros((97, 32))
    for p in range(96):
        m[p, p // 3] = 1
    m[96, :] = 1
    t["maski"] = m
    sign = {(0, 0): {(0, 0): (1, 1), (1, 1): (-1, 1), (0, 1): (1, 1), (1, 0): (1, -1)},
            (1, 1): {(0, 0): (-1, 1), (1, 1): (1, 1), (0, 1): (-1, 1), (1, 0): (-1, -1)},
            (1, 0): {(0, 0): (-1, 1), (1, 1): (1, 1), (0, 1): (1, -1), (1, 0): (1, 1)},
            (0, 1): {(0, 0): (-1, -1), (1, 1): (1, -1), (0, 1): (1, 1), (1, 0): (1, -1)}}
    m = np.zeros((2, 2, C, 2, 2, 2, C, 2))
    for (a2, b2), signs in sign.items():
        for (a, b), pair in signs.items():
            for w in range(2):
                m[w, a ^ b ^ a2 ^ b2, np.arange(C), a2, b2, b, np.arange(C), a] = pair[w]
    t["combine"] = m.reshape(128, 512)
    return {k: v.astype(np.float32) for k, v in t.items()}


def mixing_weights(w1r, w1i, w2r, w2i):
    out = np.zeros((w1r.shape[0], NY, 4, C, NK, C), np.float32)
    for part, w in enumerate((w1r, w1i)):
        out[:, :, part, :, 0:12, :] = np.transpose(w, (0, 4, 1, 3, 2))
    for part, w in enumerate((w2r, w2i)):
        out[:, :, 2 + part, :, 1:13, :] = np.transpose(w, (0, 4, 1, 3, 2))[:, :, :, ::-1, :]
    return out.reshape(w1r.shape[0], NY, 4 * C, NK * C)


def build_tokenizer(nc, io, place, h0):
    pairs = NI // 2
    halves = pairs // 2
    with ExitStack() as ctx:
        def sb(name, shape):
            return ctx.enter_context(nc.sbuf_tensor("sb_" + name, shape, F32))

        def sem(name):
            return ctx.enter_context(nc.semaphore(name))

        table = sb("table", [128, max(p[2] for p in place.values())])

        def const(name):
            r, a, b = place[name]
            return table[0:r, a:b]

        act_d = nc.dram_tensor("act_scratch", (pairs, 128, PX), F32).ap()
        x_d = nc.dram_tensor("spectrum_in", (NI, NY, 4 * C * NK), F32).ap()
        y_d = nc.dram_tensor("spectrum_out", (NI, NY, NK, MODE), F32).ap()

        image_in = [sb(f"image_in{p}", [128, 3 * S]) for p in range(2)]
        image_t = sb("image_t", [97, 256])
        fc0_rows = sb("fc0_rows", [4, C])
        fc0_center = sb("fc0_center", [4, C])
        fc0_mean = sb("fc0_mean", [4, 1])
        fc0_rep = sb("fc0_rep", [97, C])
        fc0_block = sb("fc0_block", [97, 32 * C])
        conv_raw = sb("conv_raw", [C, C])
        conv_rep = sb("conv_rep", [C, 128])
        conv_col = sb("conv_col", [128, C])
        conv_block = sb("conv_block", [128, 128])
        bias_raw = sb("bias_raw", [C, 1])
        bias_cols = sb("bias_cols", [C, 128])
        ones = sb("ones", [128, 128])
        gain = sb("gain", [128, 1])
        shift = sb("shift", [128, 1])
        fc1_pad = sb("fc1_pad", [128, 4 * 128])
        fc1_bias = sb("fc1_bias", [128, 1])
        fc2_w = sb("fc2_w", [128, 64])
        fc2_bias = sb("fc2_bias", [128, 1])
        fc3_pad = sb("fc3_pad", [128, 32])
        fc3_bias = sb("fc3_bias", [128, 1])
        act_in = [sb(f"act_in{p}", [128, PX]) for p in range(2)]
        z_in = [sb(f"z_in{p}", [2 * T26, B24 * C]) for p in range(2)]
        v_sb = sb("v_sb", [4 * B24, 1024])
        square = [sb(f"square{p}", [128, CH]) for p in range(2)]
        var = [sb(f"var{p}", [128, 16]) for p in range(2)]
        rstd = [sb(f"rstd{p}", [128, 16]) for p in range(2)]
        minus_half = sb("minus_half", [128, 16])
        unit = [sb(f"unit{p}", [128, CH]) for p in range(2)]
        act_out = [sb(f"act_out{p}", [128, PX]) for p in range(2)]
        pix = sb("pix", [128, PX])
        f1_sb = sb("f1_sb", [128, 32 * T26])
        f2_sb = [sb(f"f2_sb{p}", [112, 16 * T26]) for p in range(2)]
        dense1 = [sb(f"dense1_{p}", [128, CH]) for p in range(4)]
        dense2 = [sb(f"dense2_{p}", [128, CH]) for p in range(2)]
        head_rows = sb("head_rows", [128, CH])
        head = [sb(f"head{p}", [128, S]) for p in range(2)]
        w_raw = [sb(f"w_raw{p}", [128, NK * C]) for p in range(2)]
        w_sum = [sb(f"w_sum{p}", [128, NK]) for p in range(2)]
        w_cen = [sb(f"w_cen{p}", [128, NK * C]) for p in range(2)]
        w_mix = [sb(f"w_mix{p}", [128, NK * MODE]) for p in range(2)]
        x_in = [sb(f"x_in{p}", [NI, NK * MODE]) for p in range(2)]
        x_t = [sb(f"x_t{p}", [128, 4 * NI]) for p in range(2)]
        y_sb = [sb(f"y_sb{p}", [NI, NK * MODE]) for p in range(2)]

        H = [ctx.enter_context(nc.psum_tensor(f"H{j}", [128, CH], F32)) for j in range(4)]
        TC = ctx.enter_context(nc.psum_tensor("TC", [128, CH], F32))
        TP = ctx.enter_context(nc.psum_tensor("TP", [128, CH], F32))
        M = [ctx.enter_context(nc.psum_tensor(f"M{j}", [128, CH], F32)) for j in range(2)]

        table_in = sem("table_in")
        param_in = sem("param_in")
        layer_in = sem("layer_in")
        set_up = sem("set_up")
        prep_pe = sem("prep_pe")
        conv_set = sem("conv_set")
        conv_pe = sem("conv_pe")
        ld = [sem(f"pixels_in{p}") for p in range(2)]
        zl = [sem(f"z_loaded{p}") for p in range(2)]
        st_a = [sem(f"act_stored{p}") for p in range(2)]
        st_x = [sem(f"f2_stored{p}") for p in range(2)]
        st_h = [sem(f"head_stored{p}") for p in range(2)]
        a_done = sem("stepA_done")
        v_ready = sem("v_ready")
        h_ready = sem("h_ready")
        sq_ready = sem("sq_ready")
        var_ready = sem("var_ready")
        var_sum = sem("var_sum")
        rstd_ready = sem("rstd_ready")
        unit_ready = sem("unit_ready")
        tc_ready = sem("tc_ready")
        act_ready = sem("act_ready")
        tp_ready = sem("tp_ready")
        pix_ready = sem("pix_ready")
        f1_done = sem("f1_done")
        f1_ready = sem("f1_ready")
        f2_done = sem("f2_done")
        f2_ready = sem("f2_ready")
        w_in = [sem(f"w_in{p}") for p in range(2)]
        x_inq = [sem(f"x_inq{p}") for p in range(2)]
        y_out = [sem(f"y_out{p}") for p in range(2)]
        w_sum_s = sem("w_summed")
        w_cen_s = sem("w_centered")
        combined = sem("w_combined")
        w_mix_s = sem("w_mixed")
        xt_pe = sem("xt_transposed")
        xt_s = sem("xt_copied")
        y_pe = sem("y_product")
        y_s = sem("y_copied")
        fc1_done = sem("fc1_done")
        fc1_act = sem("fc1_act")
        fc2_done = sem("fc2_done")
        fc2_act = sem("fc2_act")
        fc3_done = sem("fc3_done")
        head_copied = sem("head_copied")
        head_turned = sem("head_turned")
        head_ready = sem("head_ready")

        def at_least(eng, s, n):
            if not isinstance(n, int) or n > 0:
                eng.wait_ge(s, n)

        images = io["x"].rearrange("(n i) h w c -> n (i h) (w c)", i=2)
        y_view = y_d.rearrange("(n i) y k m -> n i k m y", i=2)
        heads = h0.rearrange("(n i) x y -> n (i x) y", i=2)
        x_view = x_d.rearrange("(n i) y m -> n i y m", i=2)
        GROUPS = [(0, 4), (4, 4), (8, 4), (12, 1)]

        def sp_load(e, P, p, n, first):
            if first:
                at_least(e, h_ready, 8 * P + 4 * p - 4)
                e.dma_start(image_in[p][:, :], images[n]).then_inc(ld[p], 16)
                return
            at_least(e, h_ready, 8 * P + 4 * p - 4)
            e.dma_start(act_in[p][:, :], act_d[n]).then_inc(ld[p], 16)
            for i in range(2):
                src = y_d[n * 2 + i].rearrange("y k (a m) -> (k a) y m", a=2)
                e.dma_start(z_in[p][i * T26:(i + 1) * T26, :].rearrange("t (y m) -> t y m", y=NY), src).then_inc(zl[p], 16)

        def sp_store(e, P, p, n, last):
            if last:
                e.wait_ge(head_ready, 8 * (P - 4 * halves) + 4 * p + 4)
                e.dma_start(heads[n], head[p][:, :]).then_inc(st_h[p], 16)
                return
            e.wait_ge(act_ready, 8 * P + 4 * p + 4)
            e.dma_start(act_d[n], act_out[p][:, :]).then_inc(st_a[p], 16)
            e.wait_ge(f2_ready, 2 * P + p + 1)
            for i in range(2):
                e.dma_start(x_d[n * 2 + i].rearrange("y (b m) -> (y b) m", b=4),
                            f2_sb[p][64 * i:64 * i + 48, :]).then_inc(st_x[p], 16)

        HEAD0 = 4 * LAYERS * pairs

        def behind(g0, p, j, lag, front, back):
            if j >= lag:
                return (g0 + j - lag, p, j - lag) if front else None
            return (g0 + j - lag, 1 - p, j - lag + 4) if back else None

        def pe_step(e, P, p, front, back, first, last, layer):
            it = 2 * P + p
            g0 = 4 * it

            def bank(j):
                return H[j % 2] if last else H[j]

            def inverse_x():
                e.wait_ge(ld[p] if first else zl[p], 16 * (P + 1) if first else 32 * (P - halves + 1))
                for u in range(2):
                    if last and back:
                        e.wait_ge(fc1_act, 4 * (g0 - HEAD0 - 4) + 3 + u)
                    elif u == 1:
                        at_least(e, f2_ready, it - 1)
                    if first:
                        e.transpose(M[u][0:96, 0:128], image_in[p][:, 96 * u:96 * u + 96],
                                    const("ident")).then_inc(a_done, 1)
                        continue
                    for g in range(4):
                        z = z_in[p][:, :].rearrange("t (y g) -> t y g", g=8)[:, :, 4 * u + g]
                        mm = e.matmul(M[u][0:96, 128 * g:128 * g + 128], z, const("ga"), start=True, stop=True)
                    mm.then_inc(a_done, 1)

            def conv(j):
                at_least(e, unit_ready, g0 + j + 1 - (2 if last else 4))
                if first:
                    return
                if j == 0:
                    e.wait_ge(ld[p], 16 * (P + 1))
                    e.wait_ge(y_s, 48 * (layer + 1))
                for u in range(4):
                    b = 4 * j + u
                    e.matmul(bank(j)[:, 128 * u:128 * u + 128], act_in[p][:, 128 * b:128 * b + 128],
                             conv_block[:, :], start=(u == 0), stop=False, skip_group_check=True)

            def inverse_y(j):
                if j == 0:
                    e.wait_ge(v_ready, 2 * it + 2)
                if first:
                    e.matmul(bank(j)[:, :], image_t[:, 128 * (j // 2):128 * (j // 2) + 128],
                             fc0_block[:, 512 * (j % 2):512 * (j % 2) + 512],
                             start=True, stop=True).then_inc(h_ready, 1)
                    return
                for og in range(8):
                    mm = e.matmul(bank(j)[:, :].rearrange("p (y g) -> p y g", g=8)[:, :, og],
                                  v_sb[:, 128 * og:128 * og + 128], const("gb")[:, 64 * j:64 * j + 64],
                                  start=False, stop=(og == 7), skip_group_check=True)
                mm.then_inc(h_ready, 1)

            def to_channels(c, q, k):
                e.wait_ge(unit_ready, c + 1)
                at_least(e, act_ready, c)
                for u in range(4):
                    mm = e.transpose(TC[:, 128 * u:128 * u + 128], unit[k % 2][:, 128 * u:128 * u + 128],
                                     const("ident"))
                mm.then_inc(tc_ready, 1)

            def to_pixels(c, q, k):
                e.wait_ge(act_ready, c + 1)
                at_least(e, pix_ready, c)
                for u in range(4):
                    b = 4 * k + u
                    mm = e.transpose(TP[:, 128 * u:128 * u + 128], act_out[q][:, 128 * b:128 * b + 128],
                                     const("ident"))
                mm.then_inc(tp_ready, 1)

            def forward_x():
                e.wait_ge(pix_ready, g0)
                if not front:
                    at_least(e, f2_ready, it - 1)
                for u in range(2):
                    for g in range(8):
                        cols = pix[:, :].rearrange("p (y h c) -> p y h c", h=2, c=16)[:, :, :, 8 * u + g]
                        mm = e.matmul(M[u][:, 52 * g:52 * g + 52], cols, const("f1"), start=True, stop=True)
                    mm.then_inc(f1_done, 1)

            def forward_y():
                e.wait_ge(f1_ready, 2 * it)
                for i in range(2):
                    src = f1_sb[:, :].rearrange("p (c i t) -> p c i t", c=16, i=2)[:, :, i, :]
                    mm = e.matmul(M[1][64 * i:64 * i + 48, 0:16 * T26], const("f2"), src, start=True, stop=True,
                                  skip_group_check=True)
                mm.then_inc(f2_done, 1)

            def dense1_of(w, c, q, k, j):
                n = c - HEAD0
                for v in range(2):
                    at_least(e, fc1_act, 4 * n + 2 * w + v - 1)
                    if w == 0 and v == 0:
                        e.wait_ge(act_ready, c + 1)
                        if j == 0 and front:
                            e.wait_ge(v_ready, 2 * it + 2)
                    e.matmul(M[v][:, :], fc1_pad[:, 128 * (2 * w + v):128 * (2 * w + v) + 128],
                             act_out[q][:, 512 * k:512 * k + 512], start=True, stop=True).then_inc(fc1_done, 1)

            def dense2_of(w, c):
                n = c - HEAD0
                e.wait_ge(fc1_act, 4 * n + 2 * w + 2)
                for v in range(2):
                    mm = e.matmul((TP, H[3])[w][64 * v:64 * v + 64, :], fc2_w[:, :], dense1[2 * w + v][:, :],
                                  start=True, stop=True, skip_group_check=True)
                mm.then_inc(fc2_done, 1)

            def dense3_of(c, q, k):
                n = c - HEAD0
                e.wait_ge(fc2_act, 2 * n + 2)
                if k % 2 == 0:
                    at_least(e, head_ready, n)
                for w in range(2):
                    at = 32 * (2 * (k % 2) + w)
                    mm = e.matmul(H[2][at:at + 32, :], fc3_pad[:, :], dense2[w][:, :],
                                  start=True, stop=True, skip_group_check=True)
                mm.then_inc(fc3_done, 1)

            def turn_heads(c):
                e.wait_ge(head_copied, c - HEAD0 + 1)
                for u in range(4):
                    mm = e.transpose(H[2][:, 128 * u:128 * u + 128], head_rows[:, 128 * u:128 * u + 128],
                                     const("ident"))
                mm.then_inc(head_turned, 2)

            if front:
                inverse_x()
            for j in range(4):
                two, three, four = (behind(g0, p, j, lag, front, back) for lag in (2, 3, 4))
                if front:
                    conv(j)
                if last and four:
                    dense2_of(1, four[0])
                if last and three:
                    dense1_of(0, *three, j)
                if last and four:
                    dense3_of(*four)
                if first and front:
                    for ahead in ((0,), (1,), (2, 3), ())[j]:
                        inverse_y(ahead)
                if not last and three:
                    to_pixels(*three)
                if not last and back and j == 3:
                    forward_y()
                if first and two:
                    to_channels(*two)
                if front and not first:
                    inverse_y(j)
                if not last and back and j == 2:
                    forward_x()
                if last and three:
                    dense1_of(1, *three, j)
                if two and not first:
                    to_channels(*two)
                if last and three:
                    dense2_of(0, three[0])
                if last and four and four[2] % 2:
                    turn_heads(four[0])

        def act_step(e, P, p, front, back, first, last):
            it = 2 * P + p
            g0 = 4 * it
            gelu = ACT.Identity if (first or last) else ACT.Gelu

            def squares(j):
                e.wait_ge(h_ready, g0 + j + 1)
                at_least(e, var_ready, g0 + j - 1)
                e.activation(square[j % 2][:, :], (H[j % 2] if last else H[j])[:, :], ACT.Square,
                             scale=float(C) ** -0.5).then_inc(sq_ready, 1)

            def gelus(c, q, k):
                e.wait_ge(tc_ready, c + 1)
                if not last and k == 0:
                    at_least(e, st_a[p], 16 * P)
                e.activation(act_out[q][:, 512 * k:512 * k + 512], TC[:, :], gelu, bias=shift[:, 0:1],
                             scale=gain[:, 0:1]).then_inc(act_ready, 1)

            def dense1_of(w, c):
                n = c - HEAD0
                for v in range(2):
                    e.wait_ge(fc1_done, 4 * n + 2 * w + v + 1)
                    e.activation(dense1[2 * w + v][:, :], M[v][:, :], ACT.Gelu, bias=fc1_bias[:, 0:1],
                                 scale=1.0).then_inc(fc1_act, 1)

            def dense2_of(w, c):
                n = c - HEAD0
                e.wait_ge(fc2_done, 2 * n + w + 1)
                e.activation(dense2[w][:, :], (TP, H[3])[w][:, :], ACT.Gelu, bias=fc2_bias[:, 0:1],
                             scale=1.0).then_inc(fc2_act, 1)

            if front:
                for u in range(2):
                    e.wait_ge(a_done, 2 * it + u + 1)
                    if first:
                        e.activation(image_t[0:96, 128 * u:128 * u + 128], M[u][0:96, 0:128],
                                     ACT.Copy).then_inc(v_ready, 1)
                    else:
                        e.activation(v_sb[:, 512 * u:512 * u + 512], M[u][0:96, :], ACT.Copy).then_inc(v_ready, 1)
            for j in range(4):
                two, three, four = (behind(g0, p, j, lag, front, back) for lag in (2, 3, 4))
                if last and four:
                    dense2_of(1, four[0])
                if last and three:
                    dense1_of(0, three[0])
                if front:
                    for ahead in (((0,), (1,), (2, 3), ())[j] if first else (j,)):
                        squares(ahead)
                if first and two:
                    gelus(*two)
                if not last and back and j == 2:
                    for u in range(2):
                        e.wait_ge(f1_done, 2 * it + u - 1)
                        e.activation(f1_sb[:, 416 * u:416 * u + 416], M[u][:, 0:416], ACT.Copy).then_inc(f1_ready, 1)
                if last and three:
                    dense1_of(1, three[0])
                if two and not first:
                    gelus(*two)
                if last and three:
                    dense2_of(0, three[0])

        def dve_step(e, P, p, front, back, first, last):
            it = 2 * P + p
            g0 = 4 * it

            def variance(j):
                e.wait_ge(sq_ready, g0 + j + 1)
                e.tensor_reduce(var[j % 2][:, :], square[j % 2][:, :].rearrange("p (y c) -> p y c", c=C), AX.X,
                                ALU.add).then_inc(var_sum, 1)
                e.wait_ge(var_sum, g0 + j + 1)
                e.tensor_scalar(var[j % 2][:, :], var[j % 2][:, :], EPS, None, ALU.add).then_inc(var_ready, 1)

            def normal(c, q, k):
                e.wait_ge(rstd_ready, c + 1)
                at_least(e, tc_ready, c - 1)
                e.tensor_tensor(unit[k % 2][:, :].rearrange("p (y c) -> p y c", c=C),
                                (H[k % 2] if last else H[k])[:, :].rearrange("p (y c) -> p y c", c=C),
                                rstd[k % 2][:, :].unsqueeze(2).to_broadcast([128, 16, C]), ALU.mult).then_inc(unit_ready, 1)

            def pixels(c, q, k):
                e.wait_ge(tp_ready, c + 1)
                e.tensor_copy(pix[:, 512 * k:512 * k + 512], TP[:, :]).then_inc(pix_ready, 1)

            def spectrum():
                e.wait_ge(f2_done, it)
                at_least(e, st_x[1 - p], 32 * (P if p else P - 1))
                for i in range(2):
                    cp = e.tensor_copy(f2_sb[1 - p][64 * i:64 * i + 48, :], M[1][64 * i:64 * i + 48, 0:16 * T26])
                cp.then_inc(f2_ready, 1)

            def copy_heads(c):
                e.wait_ge(fc3_done, c - HEAD0 + 1)
                e.tensor_copy(head_rows[:, :], H[2][:, :]).then_inc(head_copied, 2)

            def heads_out(c, q, k):
                e.wait_ge(head_turned, c - HEAD0 + 1)
                if k == 1:
                    at_least(e, st_h[q], 16 * ((P if p else P - 1) - LAYERS * halves))
                for b in range(2):
                    at = 16 * (k - 1 + b)
                    out = e.tensor_scalar(
                        head[q][:, at:at + 16].rearrange("p (u w v) -> p u w v", u=4, w=2),
                        H[2][:, :].rearrange("p (u b w v) -> p u b w v", u=4, b=2, w=2)[:, :, b, :, 0:2],
                        fc3_bias[:, 0:1], None, ALU.add)
                out.then_inc(head_ready, 2)

            for j in range(4):
                one, three, four = (behind(g0, p, j, lag, front, back) for lag in (1, 3, 4))
                if not last and three:
                    pixels(*three)
                if last and four and four[2] % 2:
                    copy_heads(four[0])
                if not last and back and j == 3:
                    spectrum()
                if front and not (first and j == 3):
                    variance(j)
                if one:
                    normal(*one)
                if first and front and j == 2:
                    variance(3)
                if last and four and four[2] % 2:
                    heads_out(*four)

        def pool_step(e, P, p, front):
            g0 = 8 * P + 4 * p
            if not front:
                return
            for j in range(4):
                e.wait_ge(var_ready, g0 + j + 1)
                e.tensor_tensor(rstd[j % 2][:, :], var[j % 2][:, :], minus_half[:, :], ALU.pow).then_inc(rstd_ready, 1)

        def since(eng, s, before, n):
            if not isinstance(n, int) or n > 0:
                eng.wait_ge(s, before + n)

        def sp_mix_load(e, m, p, layer):
            q, ky = 2 * m + p, 2 * m + p
            if not (isinstance(m, int) and m == 0):
                since(e, w_cen_s, NY * layer, q - 1)
                e.dma_start(w_raw[p][:, :], io["w_mix"][layer, ky]).then_inc(w_in[p], 16)
            since(e, xt_pe, 4 * NY * layer, 4 * (q - 1))
            e.dma_start(x_in[p][:, :], x_d[:, ky, :]).then_inc(x_inq[p], 16)

        def sp_mix_store(e, m, p, layer):
            ky = 2 * m + p
            e.wait_ge(y_s, 4 * NY * layer + 4 * ky + 4)
            e.dma_start(y_d[:, ky, :, :], y_sb[p][:, :].rearrange("n (k m) -> n k m", k=NK)).then_inc(y_out[p], 16)

        COMBINED = (TC, TP, M[0], M[1])

        def pe_combine(e, m, p, layer):
            q, q0 = 2 * m + p, NY * layer
            e.wait_ge(w_cen_s, q0 + q + 1)
            for s in range(4):
                since(e, w_mix_s, 4 * q0, 4 * (q - 1) + s + 1)
                e.matmul(COMBINED[s][:, 0:NK * C], const("combine")[:, 128 * s:128 * s + 128], w_cen[p][:, :],
                         start=True, stop=True).then_inc(combined, 1)

        def pe_mix(e, m, p, layer, more):
            q, q0 = 2 * m + p, NY * layer
            zero = isinstance(m, int) and q == 0
            e.wait_ge(x_inq[p], 16 * (NY // 2 * layer + m + 1))
            xv = x_in[p][:, :].rearrange("n (m k) -> n m k", k=NK)

            def turn(s):
                k0, n = GROUPS[s]
                since(e, xt_s, 4 * q0, 4 * q + s - 1)
                for k in range(k0, k0 + n):
                    mm = e.transpose(H[s % 2][:, NI * (k - k0):NI * (k - k0) + NI], xv[:, :, k],
                                     const("ident")[0:NI, 0:NI])
                mm.then_inc(xt_pe, 1)

            turn(0)
            for s, (k0, n) in enumerate(GROUPS):
                if s < 3:
                    turn(s + 1)
                e.wait_ge(xt_s, 4 * (q0 + q) + s + 1)
                e.wait_ge(w_mix_s, 4 * (q0 + q) + 4)
                since(e, y_s, 4 * q0, 4 * q + s - 1)
                for k in range(k0, k0 + n):
                    dc = zero and k == 0
                    mm = e.matmul(H[2 + s % 2][0:NI, 128 * (k - k0):128 * (k - k0) + 128],
                                  x_t[s % 2][:, NI * (k - k0):NI * (k - k0) + NI],
                                  w_mix[p][:, 128 * k:128 * k + 128], start=True, stop=not dc, skip_group_check=True)
                    if dc:
                        mm = e.matmul(H[2][0:NI, 0:C], bias_cols[:, 0:NI], const("center_dc"),
                                      start=False, stop=True, skip_group_check=True)
                mm.then_inc(y_pe, 1)
                if more and s == 1:
                    pe_combine(e, m + p, 1 - p, layer)

        def act_mix(e, m, p, layer):
            q, q0 = 2 * m + p, NY * layer

            def turned(s):
                n = GROUPS[s][1]
                e.wait_ge(xt_pe, 4 * (q0 + q) + s + 1)
                since(e, y_pe, 4 * q0, 4 * q + s - 1)
                e.activation(x_t[s % 2][:, 0:NI * n], H[s % 2][:, 0:NI * n], ACT.Copy).then_inc(xt_s, 1)

            turned(0)
            for s, (k0, n) in enumerate(GROUPS):
                if s < 3:
                    turned(s + 1)
                e.wait_ge(y_pe, 4 * (q0 + q) + s + 1)
                if s == 0:
                    since(e, y_out[p], 16 * (NY // 2) * layer, 16 * m)
                e.activation(y_sb[p][:, 128 * k0:128 * (k0 + n)], H[2 + s % 2][0:NI, 0:128 * n],
                             ACT.Copy).then_inc(y_s, 1)

        def dve_center(e, m, p, layer):
            q, q0 = 2 * m + p, NY * layer
            e.wait_ge(w_in[p], 16 * (NY // 2 * layer + m + 1))
            raw = w_raw[p][:, :].rearrange("r (k o) -> r k o", o=C)
            e.tensor_reduce(w_sum[p][:, :], raw, AX.X, ALU.add).then_inc(w_sum_s, 1)
            e.wait_ge(w_sum_s, q0 + q + 1)
            since(e, combined, 4 * q0, 4 * (q - 1))
            e.scalar_tensor_tensor(out=w_cen[p][:, :].rearrange("r (k o) -> r k o", o=C),
                                   in0=w_sum[p][:, :].unsqueeze(2).to_broadcast([128, NK, C]), scalar=-1.0 / C,
                                   in1=raw, op0=ALU.mult, op1=ALU.add).then_inc(w_cen_s, 1)

        def dve_mix(e, m, p, layer):
            q, q0 = 2 * m + p, NY * layer
            since(e, y_pe, 4 * q0, 4 * (q - 1))
            for s in range(4):
                e.wait_ge(combined, 4 * (q0 + q) + s + 1)
                e.tensor_copy(w_mix[p][:, :].rearrange("r (k s o) -> r k s o", k=NK, s=4)[:, :, s, :],
                              COMBINED[s][:, 0:NK * C].rearrange("r (k o) -> r k o", o=C)).then_inc(w_mix_s, 1)

        def sp_layer(e, n, layer, norm):
            if layer is not None:
                e.dma_start(conv_raw[:, :], io["conv_w"][layer]).then_inc(layer_in, 16)
                e.dma_start(bias_raw[:, :], io["conv_b"][layer].unsqueeze(1)).then_inc(layer_in, 16)
            g, b = norm
            for u in range(4):
                if layer is not None and u < 2:
                    e.wait_ge(st_a[u], 16 * halves * (layer + 1))
                elif layer is not None:
                    e.wait_ge(st_x[u - 2], 32 * halves * (layer + 1))
                e.dma_start(gain[32 * u:32 * u + 32, :], g.unsqueeze(1)).then_inc(layer_in, 16)
                e.dma_start(shift[32 * u:32 * u + 32, :], b.unsqueeze(1)).then_inc(layer_in, 16)

        def dve_layer(e, n):
            e.wait_ge(layer_in, 128 + 160 * (n + 1))
            e.tensor_copy(conv_rep[:, :].rearrange("o (g c) -> o g c", g=4),
                          conv_raw[:, :].unsqueeze(1).to_broadcast([C, 4, C])).then_inc(conv_set, 1)
            e.tensor_scalar(bias_cols[:, :], ones[0:C, :], bias_raw[:, 0:1], None, ALU.mult).then_inc(conv_set, 1)
            e.wait_ge(conv_pe, n + 1)
            e.tensor_copy(conv_col[:, :], TP[:, 0:C]).then_inc(conv_set, 1)
            e.wait_ge(conv_set, 4 * n + 3)
            e.tensor_tensor(conv_block[:, :].rearrange("p (g o) -> p g o", g=4),
                            const("maskc").rearrange("p (g o) -> p g o", g=4),
                            conv_col[:, :].unsqueeze(1).to_broadcast([128, 4, C]), ALU.mult).then_inc(conv_set, 1)

        def pe_layer(e, n):
            e.wait_ge(conv_set, 4 * n + 2)
            e.matmul(TP[:, 0:C], conv_rep[:, :], const("center"), start=True, stop=True).then_inc(conv_pe, 1)
            e.wait_ge(conv_set, 4 * n + 4)

        def whole_pass(fori, start, step, first, last):
            peeled = 2 if first or last else 1
            for m in range(peeled):
                step(start + m, 0, True, m > 0, first, last)
                step(start + m, 1, True, True, first, last)
            if halves > peeled:
                with fori(peeled, halves) as m:
                    step(start + m, 0, True, True, first, last)
                    step(start + m, 1, True, True, first, last)
            step(start + halves, 0, False, True, first, last)

        block = ctx.enter_context(nc.Block())

        @block.sync
        def _(e):
            fori = e.Fori
            e.dma_start(table[:, :], io["tables"]).then_inc(table_in, 16)
            e.dma_start(fc0_rows[0:3, :], io["fc0_w"]).then_inc(param_in, 16)
            e.dma_start(fc0_rows[3:4, :], io["fc0_b"].unsqueeze(0)).then_inc(param_in, 16)
            e.wait_ge(set_up, 5)
            for g in range(4):
                e.dma_start(fc1_pad[32 * g:32 * g + 32, 128 * g:128 * g + 128], io["fc1_w"]).then_inc(param_in, 16)
            e.dma_start(fc1_bias[:, :], io["fc1_b"].unsqueeze(1)).then_inc(param_in, 16)
            e.dma_start(fc2_w[:, :], io["fc2_w"]).then_inc(param_in, 16)
            for g in range(2):
                e.dma_start(fc2_bias[64 * g:64 * g + 64, :], io["fc2_b"].unsqueeze(1)).then_inc(param_in, 16)
                e.dma_start(fc3_pad[64 * g:64 * g + 64, g:g + 1], io["fc3_w"]).then_inc(param_in, 16)
            e.dma_start(fc3_bias[:, :], io["fc3_b"].partition_broadcast(128)).then_inc(param_in, 16)
            sp_layer(e, 0, None, (io["ln0_g"], io["ln0_b"]))

            def one_pass(first, last, start):
                base = start
                if first:
                    for p in range(2):
                        sp_load(e, 0, p, p, True)
                    if halves > 1:
                        sp_step(first, last, base, 0)
                    if halves > 2:
                        with fori(1, halves - 1) as m:
                            sp_step(first, last, base, m)
                else:
                    for p in range(2):
                        sp_load(e, base, p, p, False)
                    if halves > 1:
                        with fori(0, halves - 1) as m:
                            sp_step(first, last, base, m)
                for p in range(2):
                    sp_store(e, base + halves - 1, p, 2 * (halves - 1) + p, last)

            def sp_step(first, last, base, m):
                for p in range(2):
                    sp_load(e, base + m + 1, p, 2 * (m + 1) + p, first)
                    sp_store(e, base + m, p, 2 * m + p, last)

            def mix(layer):
                for p in range(2):
                    sp_mix_load(e, 0, p, layer)
                with fori(0, NY // 2 - 1) as m:
                    for p in range(2):
                        sp_mix_load(e, m + 1, p, layer)
                        sp_mix_store(e, m, p, layer)
                for p in range(2):
                    sp_mix_store(e, NY // 2 - 1, p, layer)

            def layer_body(layer, last):
                for p in range(2):
                    e.dma_start(w_raw[p][:, :], io["w_mix"][layer, p]).then_inc(w_in[p], 16)
                e.wait_ge(act_ready, 8 * halves * (layer + 1))
                sp_layer(e, layer + 1, layer, (io["ln_g"][layer], io["ln_b"][layer]))
                mix(layer)
                for p in range(2):
                    e.wait_ge(y_out[p], 16 * (NY // 2) * (layer + 1))
                one_pass(False, last, halves * (layer + 1))

            one_pass(True, False, 0)
            with fori(0, LAYERS - 1) as layer:
                layer_body(layer, False)
            layer_body(LAYERS - 1, True)
            for p in range(2):
                e.wait_ge(st_h[p], 16 * halves)

        @block.tensor
        def _(e):
            fori = e.Fori
            e.wait_ge(table_in, 16)
            e.wait_ge(set_up, 5)
            e.matmul(TP[0:97, 0:C], const("rinp"), fc0_center[:, :], start=True, stop=True).then_inc(prep_pe, 1)
            e.wait_ge(set_up, 7)
            whole_pass(fori, 0, lambda *at: pe_step(e, *at, None), True, False)

            def body(layer, last):
                e.wait_ge(h_ready, 8 * halves * (layer + 1))
                e.wait_ge(pix_ready, 8 * halves * (layer + 1))
                e.wait_ge(unit_ready, 8 * halves * (layer + 1))
                e.wait_ge(act_ready, 8 * halves * (layer + 1))
                e.wait_ge(f2_ready, 2 * halves * (layer + 1))
                pe_layer(e, layer)
                pe_combine(e, 0, 0, layer)
                for p in range(2):
                    pe_mix(e, 0, p, layer, True)
                with fori(1, NY // 2 - 1) as m:
                    for p in range(2):
                        pe_mix(e, m, p, layer, True)
                for p in range(2):
                    pe_mix(e, NY // 2 - 1, p, layer, p == 0)
                if last:
                    e.wait_ge(param_in, 16 * 13)
                whole_pass(fori, halves * (layer + 1),
                           lambda *at: pe_step(e, *at, layer), False, last)

            with fori(0, LAYERS - 1) as layer:
                body(layer, False)
            body(LAYERS - 1, True)

        @block.scalar
        def _(e):
            fori = e.Fori
            e.preload_act_table_set("gelu_and_others")
            e.wait_ge(layer_in, 128)
            e.wait_ge(set_up, 3)
            step = lambda *at: act_step(e, *at)
            whole_pass(fori, 0, step, True, False)

            def body(layer, last):
                for p in range(2):
                    act_mix(e, 0, p, layer)
                with fori(1, NY // 2) as m:
                    for p in range(2):
                        act_mix(e, m, p, layer)
                e.wait_ge(layer_in, 128 + 160 * (layer + 1))
                if last:
                    e.wait_ge(param_in, 16 * 13)
                whole_pass(fori, halves * (layer + 1), step, False, last)

            with fori(0, LAYERS - 1) as layer:
                body(layer, False)
            body(LAYERS - 1, True)

        @block.vector
        def _(e):
            fori = e.Fori
            e.memset(fc1_pad[:, :], 0.0).then_inc(set_up, 1)
            e.memset(fc3_pad[:, :], 0.0).then_inc(set_up, 1)
            e.memset(image_t[96:97, :], 1.0).then_inc(set_up, 1)
            e.memset(ones[:, :], 1.0)
            e.memset(minus_half[:, :], -0.5)
            e.wait_ge(param_in, 32)
            e.tensor_reduce(fc0_mean[:, :], fc0_rows[:, :], AX.X, ALU.add).then_inc(set_up, 1)
            e.wait_ge(set_up, 4)
            e.scalar_tensor_tensor(out=fc0_center[:, :], in0=fc0_mean[:, 0:1].to_broadcast([4, C]), scalar=-1.0 / C,
                                   in1=fc0_rows[:, :], op0=ALU.mult, op1=ALU.add).then_inc(set_up, 1)
            e.wait_ge(prep_pe, 1)
            e.tensor_copy(fc0_rep[:, :], TP[0:97, 0:C]).then_inc(set_up, 1)
            e.wait_ge(set_up, 6)
            e.tensor_tensor(fc0_block[:, :].rearrange("p (y c) -> p y c", c=C),
                            const("maski").unsqueeze(2).to_broadcast([97, 32, C]),
                            fc0_rep[:, :].unsqueeze(1).to_broadcast([97, 32, C]), ALU.mult).then_inc(set_up, 1)
            step = lambda *at: dve_step(e, *at)
            whole_pass(fori, 0, step, True, False)

            def body(layer, last):
                dve_layer(e, layer)
                def two_ky(m, more):
                    dve_center(e, m, 1, layer)
                    dve_mix(e, m, 0, layer)
                    if more:
                        dve_center(e, m + 1, 0, layer)
                    dve_mix(e, m, 1, layer)

                dve_center(e, 0, 0, layer)
                two_ky(0, True)
                with fori(1, NY // 2 - 1) as m:
                    two_ky(m, True)
                two_ky(NY // 2 - 1, False)
                if last:
                    e.wait_ge(param_in, 16 * 13)
                whole_pass(fori, halves * (layer + 1), step, False, last)

            with fori(0, LAYERS - 1) as layer:
                body(layer, False)
            body(LAYERS - 1, True)

        @block.gpsimd
        def _(e):
            fori = e.Fori
            e.wait_ge(set_up, 7)
            step = lambda P, p, front, *at: pool_step(e, P, p, front)
            whole_pass(fori, 0, step, True, False)

            def body(layer, last):
                whole_pass(fori, halves * (layer + 1), step, False, last)

            with fori(0, LAYERS - 1) as layer:
                body(layer, False)
            body(LAYERS - 1, True)

T = S + 1
D = S
NS = 16
R = 16
NH, HD, NKV = 4, 16, 2
NE = 8
HID = 170
PARTS = 3
HP = -(-HID // PARTS)
Q = 4
GI = 2 * Q
TOK = Q * T


def block_tables():
    t = {}
    t["ident"] = np.eye(128)
    t["mean"] = np.kron(np.eye(2), np.full((D, D), 1.0 / D))
    rot = np.zeros((HD, HD))
    for j in range(HD // 2):
        rot[j, j + HD // 2] = -1
        rot[j + HD // 2, j] = 1
    t["rot"] = np.kron(np.eye(2 * NH), rot).T
    inv = 1.0 / 10000.0 ** (np.arange(0, HD, 2, dtype=np.float32) / HD)
    freqs = np.outer(np.arange(T, dtype=np.float32), inv)
    emb = np.concatenate([freqs, freqs], axis=-1)
    t["cos"] = np.tile(np.cos(emb).T, (2 * NH, 1))
    t["sin"] = np.tile(np.sin(emb).T, (2 * NH, 1))
    t["heads"] = np.tile(np.kron(np.eye(NH), np.ones((HD, 1))), (2, 1)) * HD ** -0.5
    t["causal"] = np.where(np.tril(np.ones((T, T), bool)), 0.0, -1e30)
    t["image"] = np.kron(np.eye(2), np.ones((D, 1)))
    t["order"] = np.tile((NE - np.arange(NE))[None, :], (T, 1))
    return {k: v.astype(np.float32) for k, v in t.items()}


def pack(tables):
    at, place, cols = 0, {}, []
    for name, v in tables.items():
        v = np.asarray(v)
        block = np.zeros((128, v.shape[1]), np.float32)
        block[:v.shape[0]] = v
        place[name] = (v.shape[0], at, at + v.shape[1])
        cols.append(block)
        at += v.shape[1]
    return np.concatenate(cols, axis=1), place


def twice(w):
    out = np.zeros((2, w.shape[0], 2, w.shape[1]), np.float32)
    out[0, :, 0], out[1, :, 1] = w, w
    return out.reshape(2 * w.shape[0], 2 * w.shape[1])


def stacked(w):
    return np.concatenate([w, w], axis=0)


def block_weights(a):
    t = {}
    wx = np.asarray(a["L0_attn_W_xproj"])
    wf = np.zeros((D, D), np.float32)
    wf[:, 0:3 * NS] = wx[R:].T
    t["wx"] = twice(wf)
    t["wxr"] = twice(wx[:R])
    t["wxb"] = twice(np.asarray(a["L0_attn_W_xbproj"]))
    t["wdt"] = twice(np.asarray(a["L0_attn_W_dt"]).T)
    t["b_dt"] = stacked(np.asarray(a["L0_attn_b_dt"])[:, None])
    t["a_log"] = stacked(np.asarray(a["L0_attn_A_log"]))
    t["d_skip"] = stacked(np.asarray(a["L0_attn_D_skip"])[:, None])
    t["wout"] = twice(np.asarray(a["L0_attn_W_out"]).T)
    t["ln1"] = stacked(np.asarray(a["L0_ffn_ln1_w"])[:, None])
    t["ln2"] = stacked(np.asarray(a["L0_ffn_ln2_w"])[:, None])
    wq = np.asarray(a["L0_ffn_wq"])
    wk = np.repeat(np.asarray(a["L0_ffn_wk"]).reshape(NKV, 1, HD, D), NH // NKV, axis=1).reshape(D, D)
    wv = np.repeat(np.asarray(a["L0_ffn_wv"]).reshape(NKV, 1, HD, D), NH // NKV, axis=1).reshape(D, D)
    t["wq_t"], t["wq"] = twice(wq.T), twice(wq)
    t["wk_t"], t["wk"] = twice(wk.T), twice(wk)
    t["wv"] = twice(wv.T)
    t["wo"] = twice(np.asarray(a["L0_ffn_wo"]).T)
    t["router"] = twice(np.asarray(a["L0_ffn_router_w"]).T)
    t["cls"] = stacked(np.asarray(a["cls_tok"]).reshape(D, 1))
    return t


def expert_weights(a):
    t = {}
    for n in ("w1", "w3", "w2"):
        w = np.asarray(a["L0_ffn_" + n])
        if n == "w2":
            w = np.transpose(w, (0, 2, 1))
        rows = np.zeros((NE, PARTS * HP, D), np.float32)
        rows[:, :HID] = w
        rows = rows.reshape(NE, PARTS, HP, D)
        if n == "w2":
            out = np.zeros((2, HP, NE, PARTS, 2, D), np.float32)
            for i in range(2):
                out[i, :, :, :, i] = np.transpose(rows, (2, 0, 1, 3))
            t[n] = out.reshape(2 * HP, NE * PARTS * 2 * D)
        else:
            out = np.zeros((2, D, NE, PARTS, 2, HP), np.float32)
            for i in range(2):
                out[i, :, :, :, i] = np.transpose(rows, (3, 0, 1, 2))
            t[n] = out.reshape(2 * D, NE * PARTS * 2 * HP)
    return t


def build_block(nc, io, tplace, wplace, eplace, h0, out):
    groups = NI // GI
    with ExitStack() as ctx:
        def sb(name, shape):
            return ctx.enter_context(nc.sbuf_tensor("blk_" + name, shape, F32))

        def sem(name):
            return ctx.enter_context(nc.semaphore("b_" + name))

        tables = sb("tables", [128, max(p[2] for p in tplace.values())])
        weights = sb("weights", [128, max(p[2] for p in wplace.values())])

        experts = sb("experts", [128, max(p[2] for p in eplace.values())])

        def const(name):
            r, a, b = tplace[name]
            return tables[0:r, a:b]

        def wt(name):
            r, a, b = wplace[name]
            return weights[0:r, a:b]

        def expert(name, x, part, width):
            r, a, _ = eplace[name]
            a += width * (PARTS * x + part)
            return experts[0:r, a:a + width]

        w_delta = sb("w_delta", [128, 128])
        w_delta_b = sb("w_delta_b", [128, 128])
        wq_rot = sb("wq_rot", [128, 128])
        wk_rot = sb("wk_rot", [128, 128])
        wskip = sb("wskip", [128, 128])
        neg_a = sb("neg_a", [128, NS])
        select = sb("select", [128, 3 * NS * 128])
        rows = sb("rows", [S, GI * D])
        h_in = sb("h_in", [128, TOK])
        cen = sb("cen", [128, TOK])
        sqr = sb("sqr", [128, TOK])
        log = sb("log", [128, TOK])
        ve = sb("ve", [128, TOK])
        y0 = sb("y0", [128, TOK])
        y1 = sb("y1", [128, TOK])
        rs = sb("rs", [128, TOK])
        xn = sb("xn", [128, TOK])
        xf = sb("xf", [128, TOK])
        mag = [sb(f"mag{k}", [128, TOK]) for k in range(2)]
        soft = [sb(f"soft{k}", [128, TOK]) for k in range(2)]
        pos = [sb(f"pos{k}", [128, TOK]) for k in range(2)]
        delta = [sb(f"delta{k}", [128, TOK]) for k in range(2)]
        du = sb("du", [128, TOK])
        dub = sb("dub", [128, TOK])
        bc = sb("bc", [128, TOK])
        dA = sb("dA", [128, NS * TOK])
        dB = sb("dB", [128, NS * TOK])
        dB2 = [sb(f"dB2_{p}", [128, TOK]) for p in range(2)]
        y_sum = [sb(f"y_sum{p}", [128, TOK]) for p in range(2)]
        h1 = sb("h1", [128, TOK])
        r = sb("r", [128, TOK])
        un = sb("un", [128, TOK])
        qf = sb("qf", [128, TOK])
        kf = sb("kf", [128, TOK])
        q_image = [sb(f"q_image{i}", [128, TOK]) for i in range(2)]
        tmp = sb("tmp", [128, TOK])
        kx = dA[:, 0:Q * NH * T]
        sc = dB[0:T, 0:GI * NH * T]
        pt = [sb(f"pt{p}", [T, NH * T]) for p in range(2)]
        v_sb = sb("v", [T, GI * D])
        mx = sb("mx", [T, GI * NH])
        sm = sb("sm", [T, GI * NH])
        rc = sb("rc", [T, GI * NH])
        yn = sb("yn", [T, GI * D])
        yt = sb("yt", [128, TOK])
        x2 = sb("x2", [128, TOK])
        lg = [sb(f"lg{k}", [T, GI * NE]) for k in range(6)]
        st = [sb(f"st{k}", [T, GI]) for k in range(6)]
        silu = [sb(f"silu{p}", [2 * HP, TOK]) for p in range(2)]
        hid = [[sb(f"hid{p}{k}", [2 * HP, TOK]) for k in range(PARTS)] for p in range(2)]
        acc = sb("acc", [T, GI * D])
        part = sb("part", [T, GI * D])
        res = sb("res", [128, TOK])
        fin = sb("fin", [T, GI * D])
        B = [ctx.enter_context(nc.psum_tensor(f"bank{j}", [128, 512], F32)) for j in range(8)]

        PER = dict(
            rows_t=1, h_in=2, mean=2, cen=2, square=3, variance=3, ratio=2, var_eps=4, log=4, guess=4, newton=12, scale=4,
            normed=4, flipped=1, proj=1, soft_mag=2, soft_exp=2, soft_log=2, soft_pos=2, delta=2, du=2, bc=1,
            decay=NS, reset=1, bcast=NS, drive=NS, input=NS, scan=1, c_cast=NS, read=NS, added=NS - 1, scan_out=1, h1=1,
            qk=1, v=1, v_copied=1, rope=6, q_image=2, kx=Q, scores=GI, masked=GI, peak=2, shifted=2, expd=2, total=2, recip=1,
            p_turned=GI, p_copied=GI, yv=1, y_norm=1, y_turned=1, y_copied=1, wo=1, x2=1, router=1, gate=21,
            gate_exp=1, up=PARTS * NE, silu=PARTS * NE, hidden=PARTS * NE, down=NE, gated=NE, summed=NE - 1, residual=1, res_turned=1,
            fin=1)
        sig = {name: sem(name) for name in PER}
        loaded = sem("weights_loaded")
        experts_in = sem("experts_loaded")
        rows_in = sem("rows_in")
        stored = sem("stored")
        prep = sem("prepared")
        prep_pe = sem("prepared_pe")
        prep_act = sem("prepared_act")

        def wait(e, name, g, c=None):
            e.wait_ge(sig[name], PER[name] * g + (PER[name] if c is None else c))

        SQUARED = (0, 1, None, 2)

        def by_token(ap):
            return ap.rearrange("p (q t) -> p q t", t=T)

        h0_rows = h0.rearrange("(g m) x y -> g x m y", m=GI)
        out_rows = out.rearrange("(g m) t d -> g t m d", m=GI)
        IMAGES = [(q, i) for q in range(Q) for i in range(2)]
        block = ctx.enter_context(nc.Block())

        @block.sync
        def _(e):
            e.dma_start(tables[:, :], io["block_tables"]).then_inc(loaded, 16)
            e.dma_start(weights[:, :], io["block_weights"]).then_inc(loaded, 16)

            def load(g):
                e.dma_start(rows[:, :].rearrange("x (m y) -> x m y", m=GI), h0_rows[g]).then_inc(rows_in, 16)

            def store(g):
                wait(e, "fin", g)
                e.dma_start(out_rows[g], fin[:, :].rearrange("t (m d) -> t m d", m=GI)).then_inc(stored, 16)

            load(0)
            e.dma_start(experts[:, :], io["expert_weights"]).then_inc(experts_in, 16)
            wait(e, "rows_t", 0)
            load(1)
            with e.Fori(1, groups - 1) as g:
                store(g - 1)
                e.wait_ge(stored, 16 * g)
                load(g + 1)
            store(groups - 2)
            store(groups - 1)
            e.wait_ge(stored, 16 * groups)

        SLOTS = PARTS * (NE + 1)
        STEPS = 2 * NS + 1
        AHEAD = 7

        def steps(s):
            lo, hi = (AHEAD + k * (STEPS - AHEAD) // SLOTS for k in (s, s + 1))
            return range(0 if s == 0 else lo, hi)

        PAIRED = min(s for s in range(SLOTS) if NS in steps(s)) | 1

        def pair_of(n):
            return (0, 1) if n >= PAIRED and n % 2 else (5, 6)

        @block.tensor
        def _(e):
            e.wait_ge(loaded, 32)
            e.matmul(B[0][:, 0:128], wt("wxr"), wt("wdt"), start=True, stop=True)
            e.matmul(B[1][:, 0:128], wt("wxb"), wt("wdt"), start=True, stop=True)
            e.matmul(B[2][:, 0:128], wt("wq"), const("rot"), start=True, stop=True)
            e.matmul(B[3][:, 0:128], wt("wk"), const("rot"), start=True, stop=True).then_inc(prep_pe, 1)
            e.wait_ge(prep, 7)

            def norm(g, k, centred, src):
                if centred:
                    e.matmul(B[1][:, 0:TOK], const("mean"), src[:, :], start=True, stop=True).then_inc(sig["mean"], 1)
                wait(e, "square", g, SQUARED[k] + 1)
                e.matmul(B[2][:, 0:TOK], const("mean"), sqr[:, :], start=True, stop=True).then_inc(sig["variance"], 1)

            def experts_slot(g, n):
                x, k = n // PARTS, n % PARTS
                if x < NE:
                    if n == 0:
                        e.wait_ge(experts_in, 16)
                        wait(e, "gate", g)
                    else:
                        wait(e, "hidden", g, n - 1 if n >= PAIRED else n)
                    one, two = pair_of(n)
                    e.matmul(B[one][0:2 * HP, 0:TOK], expert("w1", x, k, 2 * HP), un[:, :], start=True, stop=True)
                    e.matmul(B[two][0:2 * HP, 0:TOK], expert("w3", x, k, 2 * HP), un[:, :],
                             start=True, stop=True).then_inc(sig["up"], 1)
                if x > 0:
                    y = x - 1
                    if k == 0:
                        wait(e, "hidden", g, PARTS * x)
                        if y >= 1:
                            wait(e, "gated", g, y)
                    for q in ((0,), (1,), (2, 3))[k]:
                        for part in range(PARTS):
                            mm = e.matmul(B[7][0:T, 128 * q:128 * q + 128],
                                          hid[y % 2][part][:, T * q:T * q + T], expert("w2", y, part, 2 * D),
                                          start=(part == 0), stop=(part == PARTS - 1), skip_group_check=True)
                    if k == PARTS - 1:
                        mm.then_inc(sig["down"], 1)
                if n == SLOTS - 1:
                    wait(e, "gated", g)
                    for q in range(Q):
                        mm = e.matmul(B[7][0:T, 128 * q:128 * q + 128], res[:, T * q:T * q + T], const("ident"),
                                      start=True, stop=True, skip_group_check=True)
                    mm.then_inc(sig["res_turned"], 1)

            def scan_phase(g, before):
                e.wait_ge(rows_in, 16 * (g + 1))
                for q in range(Q):
                    mm = e.matmul(B[0][:, T * q + 1:T * q + T], rows[:, 128 * q:128 * q + 128],
                                  const("ident")[0:S, 0:S], start=True, stop=True, skip_group_check=True)
                mm.then_inc(sig["rows_t"], 1)
                wait(e, "h_in", g)
                norm(g, 0, True, h_in)
                wait(e, "normed", g, 1)
                wait(e, "flipped", g)
                e.matmul(B[0][:, 0:TOK], w_delta[:, :], xn[:, :], start=True, stop=True)
                e.matmul(B[1][:, 0:TOK], w_delta_b[:, :], xf[:, :], start=True, stop=True)
                e.matmul(B[2][:, 0:TOK], wt("wx"), xn[:, :], start=True, stop=True).then_inc(sig["proj"], 1)
                wait(e, "bc", g)

                def spread(row, bank):
                    return e.matmul(B[bank][:, 0:TOK], select[:, 128 * row:128 * row + 128], bc[:, :],
                                    start=True, stop=True)

                def scan_step(i):
                    n = i if i < NS else i - NS
                    if i < NS:
                        if n == 1:
                            wait(e, "soft_pos", g)
                        if n >= 2:
                            wait(e, "drive", g, n - 1)
                        spread(n, (3, 0)[n % 2])
                        spread(NS + n, (4, 1)[n % 2]).then_inc(sig["bcast"], 1)
                        if n == NS - 1:
                            e.matmul(B[2][:, 0:TOK], wskip[:, :], xn[:, :], start=True, stop=False)
                            e.matmul(B[2][:, 0:TOK], wskip[:, :], xf[:, :], start=False, stop=False)
                        return
                    if n == 0:
                        wait(e, "drive", g)
                    if n < NS:
                        if n >= 2:
                            wait(e, "read", g, n - 1)
                        spread(2 * NS + n, 3 + n % 2).then_inc(sig["c_cast"], 1)
                    if n == NS:
                        wait(e, "added", g)
                        e.matmul(B[2][:, 0:TOK], wt("wout"), y_sum[(NS - 1) % 2][:, :],
                                 start=False, stop=True).then_inc(sig["scan_out"], 1)

                for s in range(SLOTS):
                    for i in steps(s):
                        scan_step(i)
                    if before is not None:
                        experts_slot(before, s)

            def attention_phase(g):
                wait(e, "h1", g)
                norm(g, 1, True, h1)
                wait(e, "normed", g, 3)
                for b, w in enumerate((wt("wq_t"), wq_rot[:, :], wt("wk_t"), wk_rot[:, :])):
                    if b == 2:
                        wait(e, "var_eps", g, 3)
                    mm = e.matmul(B[b][:, 0:TOK], w, un[:, :], start=True, stop=True)
                mm.then_inc(sig["qk"], 1)
                for q in range(Q):
                    mm = e.matmul(B[4][0:T, 128 * q:128 * q + 128], un[:, T * q:T * q + T], wt("wv"),
                                  start=True, stop=True, skip_group_check=True)
                mm.then_inc(sig["v"], 1)
                wait(e, "q_image", g)
                for m, (q, i) in enumerate(IMAGES):
                    wait(e, "kx", g, q + 1)
                    if m >= 4:
                        wait(e, "masked", g, m - 3)
                    e.matmul(B[m % 4][0:T, 0:NH * T], q_image[i][:, T * q:T * q + T],
                             kx[:, NH * T * q:NH * T * (q + 1)], start=True, stop=True).then_inc(sig["scores"], 1)
                wait(e, "v_copied", g)
                for m in range(GI + 1):
                    if m < GI:
                        if m % Q == 0:
                            wait(e, "expd", g, m // Q + 1)
                        if m >= 2:
                            wait(e, "p_copied", g, m - 1)
                        for h in range(NH):
                            mm = e.transpose(B[m % 2][0:T, T * h:T * h + T],
                                             sc[:, T * (NH * m + h):T * (NH * m + h) + T], const("ident")[0:T, 0:T])
                        mm.then_inc(sig["p_turned"], 1)
                    if m > 0:
                        wait(e, "p_copied", g, m)
                        for h in range(NH):
                            at = D * (m - 1) + HD * h
                            mm = e.matmul(B[5][0:T, at:at + HD], pt[(m - 1) % 2][:, T * h:T * h + T],
                                          v_sb[:, at:at + HD], start=True, stop=True, skip_group_check=True)
                mm.then_inc(sig["yv"], 1)
                wait(e, "y_norm", g)
                for m, (q, i) in enumerate(IMAGES):
                    mm = e.matmul(B[2][64 * i:64 * i + 64, T * q:T * q + T], yn[:, D * m:D * m + D],
                                  const("ident")[0:T, 0:T], start=True, stop=True, skip_group_check=True)
                mm.then_inc(sig["y_turned"], 1)
                wait(e, "y_copied", g)
                e.matmul(B[3][:, 0:TOK], wt("wo"), yt[:, :], start=True, stop=True).then_inc(sig["wo"], 1)
                wait(e, "x2", g)
                norm(g, 3, False, None)
                wait(e, "normed", g, 4)
                for q in range(Q):
                    mm = e.matmul(B[6][0:T, 2 * NE * q:2 * NE * (q + 1)], un[:, T * q:T * q + T], wt("router"),
                                  start=True, stop=True, skip_group_check=True)
                mm.then_inc(sig["router"], 1)
            scan_phase(0, None)
            attention_phase(0)
            with e.Fori(1, groups) as g:
                scan_phase(g, g - 1)
                attention_phase(g)
            for s in range(SLOTS):
                experts_slot(groups - 1, s)

        @block.scalar
        def _(e):
            e.wait_ge(loaded, 32)
            e.preload_act_table_set("natural_log_exp_and_others")
            e.activation(neg_a[:, :], wt("a_log"), ACT.Exp).then_inc(prep_act, 1)

            def norm(g, k):
                if k < 2:
                    wait(e, "cen", g, k + 1)
                elif k == 3:
                    wait(e, "x2", g)
                if k != 2:
                    src = (cen, cen, None, x2)[k]
                    e.activation(sqr[:, :], src[:, :], ACT.Square).then_inc(sig["square"], 1)
                wait(e, "var_eps", g, k + 1)
                e.activation(log[:, :], ve[:, :], ACT.Ln).then_inc(sig["log"], 1)
                wait(e, "log", g, k + 1)
                e.activation(y0[:, :], log[:, :], ACT.Exp, scale=-0.5).then_inc(sig["guess"], 1)

            def experts_phase(g):
                e.preload_act_table_set("silu_and_others")
                for n in range(PARTS * NE):
                    wait(e, "up", g, n + 1)
                    if n >= 2:
                        wait(e, "hidden", g, n - 1)
                    e.activation(silu[n % 2][:, :], B[pair_of(n)[0]][0:2 * HP, 0:TOK], ACT.Silu).then_inc(sig["silu"], 1)
                e.preload_act_table_set("natural_log_exp_and_others")

            def scan_phase(g, before):
                norm(g, 0)
                wait(e, "proj", g)
                e.activation(bc[:, :], B[2][:, 0:TOK], ACT.Copy).then_inc(sig["bc"], 1)
                for k in range(2):
                    e.activation(mag[k][:, :], B[k][:, 0:TOK], ACT.Abs, bias=wt("b_dt")).then_inc(sig["soft_mag"], 1)
                for k in range(2):
                    wait(e, "soft_mag", g, k + 1)
                    e.activation(soft[k][:, :], mag[k][:, :], ACT.Exp, scale=-1.0).then_inc(sig["soft_exp"], 1)
                for k in range(2):
                    wait(e, "soft_exp", g, k + 1)
                    e.activation(mag[k][:, :], soft[k][:, :], ACT.Ln, bias=1.0).then_inc(sig["soft_log"], 1)
                wait(e, "delta", g, 1)
                for n in range(NS):
                    e.activation(dA[:, TOK * n:TOK * n + TOK], delta[0][:, :], ACT.Exp,
                                 scale=neg_a[:, n:n + 1]).then_inc(sig["decay"], 1)
                if before is not None:
                    experts_phase(before)

            def attention_phase(g):
                norm(g, 1)
                norm(g, 2)
                wait(e, "v", g)
                e.activation(v_sb[:, :], B[4][0:T, :], ACT.Copy).then_inc(sig["v_copied"], 1)
                for half in range(2):
                    wait(e, "shifted", g, half + 1)
                    rows_h = sc[:, Q * NH * T * half:Q * NH * T * (half + 1)]
                    e.activation(rows_h, rows_h, ACT.Exp).then_inc(sig["expd"], 1)
                for m in range(GI):
                    wait(e, "p_turned", g, m + 1)
                    e.activation(pt[m % 2][:, :], B[m % 2][0:T, 0:NH * T], ACT.Copy).then_inc(sig["p_copied"], 1)
                wait(e, "y_turned", g)
                e.activation(yt[:, :], B[2][:, 0:TOK], ACT.Copy).then_inc(sig["y_copied"], 1)
                norm(g, 3)
                wait(e, "gate", g, 2)
                e.activation(lg[1][:, :], lg[0][:, :], ACT.Exp).then_inc(sig["gate_exp"], 1)

            scan_phase(0, None)
            attention_phase(0)
            with e.Fori(1, groups) as g:
                scan_phase(g, g - 1)
                attention_phase(g)
            experts_phase(groups - 1)

        @block.vector
        def _(e):
            e.wait_ge(prep_pe, 1)
            for k, w in enumerate((w_delta, w_delta_b, wq_rot, wk_rot)):
                e.tensor_copy(w[:, :], B[k][:, 0:128]).then_inc(prep, 1)
            e.tensor_scalar(wskip[:, :], wt("wout"), wt("d_skip"), None, ALU.mult).then_inc(prep, 1)
            e.wait_ge(prep_act, 1)
            e.tensor_scalar(neg_a[:, :], neg_a[:, :], -1.0, None, ALU.mult).then_inc(prep, 1)
            for row in range(3 * NS):
                cp = e.tensor_copy(select[:, 128 * row:128 * row + 128].rearrange("p (i d) -> p i d", i=2),
                                   const("ident").rearrange("p (i d) -> p i d", i=2)[:, :, row:row + 1]
                                   .to_broadcast([128, 2, D]))
            cp.then_inc(prep, 1)

            def norm(g, k, src, dst, eps, weight):
                if k < 2:
                    wait(e, "mean", g, k + 1)
                    e.tensor_tensor(cen[:, :], src[:, :], B[1][:, 0:TOK], ALU.subtract).then_inc(sig["cen"], 1)
                    src = cen
                if k == 2:
                    e.tensor_tensor(y1[:, :], rs[:, :], rs[:, :], ALU.mult).then_inc(sig["ratio"], 1)
                    wait(e, "ratio", g, 1)
                    e.tensor_tensor(y1[:, :], y1[:, :], B[2][:, 0:TOK], ALU.mult).then_inc(sig["ratio"], 1)
                    wait(e, "ratio", g, 2)
                    e.tensor_scalar(ve[:, :], y1[:, :], eps, None, ALU.add).then_inc(sig["var_eps"], 1)
                else:
                    wait(e, "variance", g, SQUARED[k] + 1)
                    e.tensor_scalar(ve[:, :], B[2][:, 0:TOK], eps, None, ALU.add).then_inc(sig["var_eps"], 1)
                wait(e, "guess", g, k + 1)
                e.tensor_tensor(y1[:, :], y0[:, :], y0[:, :], ALU.mult).then_inc(sig["newton"], 1)
                wait(e, "newton", g, 3 * k + 1)
                e.tensor_tensor(rs[:, :], y1[:, :], ve[:, :], ALU.mult).then_inc(sig["newton"], 1)
                wait(e, "newton", g, 3 * k + 2)
                e.tensor_scalar(y1[:, :], rs[:, :], -0.5, 1.5, ALU.mult, ALU.add).then_inc(sig["newton"], 1)
                wait(e, "newton", g, 3 * k + 3)
                e.tensor_tensor(rs[:, :], y1[:, :], y0[:, :], ALU.mult).then_inc(sig["scale"], 1)
                wait(e, "scale", g, k + 1)
                if weight is None:
                    e.tensor_tensor(dst[:, :], src[:, :], rs[:, :], ALU.mult).then_inc(sig["normed"], 1)
                else:
                    e.scalar_tensor_tensor(out=dst[:, :], in0=src[:, :], scalar=weight, in1=rs[:, :],
                                           op0=ALU.mult, op1=ALU.mult).then_inc(sig["normed"], 1)

            def e8(ap):
                return ap.rearrange("t (m e) -> t m e", e=NE)

            def over(ap):
                return ap.unsqueeze(2).to_broadcast([T, GI, NE])

            def gated(g, x):
                wait(e, "down", g, x + 1)
                o = B[7][0:T, :].rearrange("t (m d) -> t m d", d=D)
                w = e8(lg[5][:, :])[:, :, x:x + 1].to_broadcast([T, GI, D])
                dst = acc if x == 0 else part
                e.tensor_tensor(dst[:, :].rearrange("t (m d) -> t m d", d=D), o, w, ALU.mult)\
                    .then_inc(sig["gated"], 1)
                if x > 0:
                    wait(e, "gated", g, x + 1)
                    e.tensor_tensor(acc[:, :], acc[:, :], part[:, :], ALU.add).then_inc(sig["summed"], 1)
                    wait(e, "summed", g, x)

            def experts_slot(g, n):
                x, k = n // PARTS, n % PARTS
                if k == 0 and x > 1:
                    gated(g, x - 2)
                if x < NE:
                    wait(e, "silu", g, n + 1)
                    e.tensor_tensor(hid[x % 2][k][:, :], silu[n % 2][:, :], B[pair_of(n)[1]][0:2 * HP, 0:TOK],
                                    ALU.mult).then_inc(sig["hidden"], 1)
                if n == SLOTS - 1:
                    gated(g, NE - 1)
                    wait(e, "res_turned", g)
                    if isinstance(g, int) and g > 0:
                        e.wait_ge(stored, 16 * g)
                    e.tensor_tensor(fin[:, :], acc[:, :], B[7][0:T, :], ALU.add).then_inc(sig["fin"], 1)

            def scan_phase(g, before):
                wait(e, "rows_t", g)
                e.tensor_copy(by_token(h_in[:, :])[:, :, 1:T], by_token(B[0][:, 0:TOK])[:, :, 1:T])\
                    .then_inc(sig["h_in"], 1)
                e.tensor_copy(by_token(h_in[:, :])[:, :, 0:1], wt("cls").unsqueeze(1).to_broadcast([128, Q, 1]))\
                    .then_inc(sig["h_in"], 1)
                wait(e, "h_in", g)
                norm(g, 0, h_in, xn, EPS, None)
                wait(e, "normed", g, 1)
                e.tensor_copy(by_token(xf[:, :]), by_token(xn[:, :])[:, :, ::-1]).then_inc(sig["flipped"], 1)
                wait(e, "soft_mag", g)
                for k in range(2):
                    e.tensor_scalar(pos[k][:, :], B[k][:, 0:TOK], wt("b_dt"), 0.0, ALU.add, ALU.max)\
                        .then_inc(sig["soft_pos"], 1)
                for k in range(2):
                    wait(e, "soft_pos", g, k + 1)
                    wait(e, "soft_log", g, k + 1)
                    e.tensor_tensor(delta[k][:, :], pos[k][:, :], mag[k][:, :], ALU.add).then_inc(sig["delta"], 1)
                for k, (dst, src) in enumerate(((du, xn), (dub, xf))):
                    wait(e, "delta", g, k + 1)
                    e.tensor_tensor(dst[:, :], delta[k][:, :], src[:, :], ALU.mult).then_inc(sig["du"], 1)
                wait(e, "du", g)
                def scan_step(i):
                    n = i if i < NS else i - NS
                    if i < NS:
                        wait(e, "bcast", g, n + 1)
                        e.tensor_tensor(dB[:, TOK * n:TOK * n + TOK], B[(3, 0)[n % 2]][:, 0:TOK], du[:, :], ALU.mult)
                        if n >= 2:
                            wait(e, "input", g, n - 1)
                        e.tensor_tensor(dB2[n % 2][:, :], B[(4, 1)[n % 2]][:, 0:TOK], dub[:, :], ALU.mult)\
                            .then_inc(sig["drive"], 1)
                        return
                    if n == 0:
                        wait(e, "decay", g)
                        e.memset(dA[:, :].rearrange("p (n t) -> p n t", t=T)[:, :, 0:1], 0.0).then_inc(sig["reset"], 1)
                        wait(e, "input", g)
                        wait(e, "reset", g)
                        e.tensor_tensor_scan(dB[:, :], dA[:, :], dB[:, :], 0.0, ALU.mult, ALU.add)\
                            .then_inc(sig["scan"], 1)
                        wait(e, "scan", g)
                    if n < NS:
                        wait(e, "c_cast", g, n + 1)
                        e.tensor_tensor(dB[:, TOK * n:TOK * n + TOK], dB[:, TOK * n:TOK * n + TOK],
                                        B[3 + n % 2][:, 0:TOK], ALU.mult).then_inc(sig["read"], 1)

                for s in range(SLOTS):
                    for i in steps(s):
                        scan_step(i)
                    if before is not None:
                        experts_slot(before, s)
                wait(e, "scan_out", g)
                e.tensor_tensor(h1[:, :], h_in[:, :], B[2][:, 0:TOK], ALU.add).then_inc(sig["h1"], 1)

            def attention_phase(g):
                wait(e, "h1", g)
                norm(g, 1, h1, r, EPS, None)
                wait(e, "normed", g, 2)
                norm(g, 2, r, un, 1e-6, wt("ln1"))
                wait(e, "qk", g)
                for k, dst in enumerate((qf, kf)):
                    cos = const("cos").unsqueeze(1).to_broadcast([128, Q, T])
                    sin = const("sin").unsqueeze(1).to_broadcast([128, Q, T])
                    if k:
                        wait(e, "rope", g, 3)
                    e.tensor_tensor(by_token(dst[:, :]), by_token(B[2 * k][:, 0:TOK]), cos, ALU.mult)\
                        .then_inc(sig["rope"], 1)
                    e.tensor_tensor(by_token(tmp[:, :]), by_token(B[2 * k + 1][:, 0:TOK]), sin, ALU.mult)\
                        .then_inc(sig["rope"], 1)
                    wait(e, "rope", g, 3 * k + 2)
                    e.tensor_tensor(dst[:, :], dst[:, :], tmp[:, :], ALU.add).then_inc(sig["rope"], 1)
                for i in range(2):
                    e.tensor_scalar(q_image[i][:, :], qf[:, :], const("image")[:, i:i + 1], None, ALU.mult)\
                        .then_inc(sig["q_image"], 1)
                wait(e, "rope", g)
                for q in range(Q):
                    e.tensor_tensor(kx[:, NH * T * q:NH * T * (q + 1)].rearrange("p (h t) -> p h t", t=T),
                                    kf[:, T * q:T * q + T].unsqueeze(1).to_broadcast([128, NH, T]),
                                    const("heads").unsqueeze(2).to_broadcast([128, NH, T]), ALU.mult)\
                        .then_inc(sig["kx"], 1)
                rows_v = sc.rearrange("t (m s) -> t m s", s=T)
                for m in range(GI):
                    wait(e, "scores", g, m + 1)
                    e.tensor_tensor(rows_v[:, NH * m:NH * m + NH, :],
                                    B[m % 4][0:T, 0:NH * T].rearrange("t (h s) -> t h s", s=T),
                                    const("causal").unsqueeze(1).to_broadcast([T, NH, T]), ALU.add)\
                        .then_inc(sig["masked"], 1)
                def half_of(h):
                    cols = slice(Q * NH * h, Q * NH * (h + 1))
                    return rows_v[:, cols, :], mx[:, cols], sm[:, cols]

                for h in range(2):
                    rows_h, peak_h, _ = half_of(h)
                    wait(e, "masked", g, Q * (h + 1))
                    e.tensor_reduce(peak_h, rows_h, AX.X, ALU.max).then_inc(sig["peak"], 1)
                    wait(e, "peak", g, h + 1)
                    e.tensor_tensor(rows_h, rows_h, peak_h.unsqueeze(2).to_broadcast([T, Q * NH, T]), ALU.subtract)\
                        .then_inc(sig["shifted"], 1)
                for h in range(2):
                    rows_h, _, sum_h = half_of(h)
                    wait(e, "expd", g, h + 1)
                    e.tensor_reduce(sum_h, rows_h, AX.X, ALU.add).then_inc(sig["total"], 1)
                wait(e, "total", g)
                e.reciprocal(rc[:, :], sm[:, :]).then_inc(sig["recip"], 1)
                wait(e, "recip", g)
                wait(e, "yv", g)
                e.tensor_tensor(yn[:, :].rearrange("t (m d) -> t m d", d=HD),
                                B[5][0:T, :].rearrange("t (m d) -> t m d", d=HD),
                                rc[:, :].unsqueeze(2).to_broadcast([T, GI * NH, HD]), ALU.mult)\
                    .then_inc(sig["y_norm"], 1)
                wait(e, "wo", g)
                e.tensor_tensor(x2[:, :], r[:, :], B[3][:, 0:TOK], ALU.add).then_inc(sig["x2"], 1)
                wait(e, "x2", g)
                norm(g, 3, x2, un, 1e-6, wt("ln2"))
                e.tensor_tensor(res[:, :], h1[:, :], x2[:, :], ALU.add).then_inc(sig["residual"], 1)

                count = [0]

                def step(ins):
                    count[0] += 1
                    ins.then_inc(sig["gate"], 1)
                    wait(e, "gate", g, count[0])

                order = const("order").unsqueeze(1).to_broadcast([T, GI, NE])
                wait(e, "router", g)
                logits = e8(B[6][0:T, 0:GI * NE])
                step(e.tensor_reduce(st[0][:, :], logits, AX.X, ALU.max))
                step(e.tensor_tensor(e8(lg[0][:, :]), logits, over(st[0][:, :]), ALU.subtract))
                wait(e, "gate_exp", g)
                step(e.tensor_reduce(st[1][:, :], e8(lg[1][:, :]), AX.X, ALU.add))
                step(e.reciprocal(st[2][:, :], st[1][:, :]))
                step(e.tensor_tensor(e8(lg[0][:, :]), e8(lg[1][:, :]), over(st[2][:, :]), ALU.mult))

                def top(probs, peak, code, chosen):
                    step(e.tensor_reduce(st[peak][:, :], e8(lg[probs][:, :]), AX.X, ALU.max))
                    step(e.tensor_tensor(e8(lg[code][:, :]), e8(lg[probs][:, :]), over(st[peak][:, :]), ALU.is_equal))
                    step(e.tensor_tensor(e8(lg[code][:, :]), e8(lg[code][:, :]), order, ALU.mult))
                    step(e.tensor_reduce(st[0][:, :], e8(lg[code][:, :]), AX.X, ALU.max))
                    step(e.tensor_tensor(e8(lg[chosen][:, :]), e8(lg[code][:, :]), over(st[0][:, :]), ALU.is_equal))

                top(0, 3, 1, 2)
                step(e.scalar_tensor_tensor(out=lg[3][:, :], in0=lg[2][:, :], scalar=-2.0, in1=lg[0][:, :],
                                            op0=ALU.mult, op1=ALU.add))
                top(3, 4, 1, 4)
                step(e.tensor_tensor(lg[2][:, :], lg[2][:, :], lg[4][:, :], ALU.add))
                step(e.tensor_tensor(lg[2][:, :], lg[2][:, :], lg[0][:, :], ALU.mult))
                step(e.scalar_tensor_tensor(out=st[5][:, :], in0=st[3][:, :], scalar=1e-9, in1=st[4][:, :],
                                            op0=ALU.add, op1=ALU.add))
                step(e.reciprocal(st[1][:, :], st[5][:, :]))
                step(e.tensor_tensor(e8(lg[5][:, :]), e8(lg[2][:, :]), over(st[1][:, :]), ALU.mult))
                assert count[0] == PER["gate"], count

            scan_phase(0, None)
            attention_phase(0)
            with e.Fori(1, groups) as g:
                scan_phase(g, g - 1)
                attention_phase(g)
            for s in range(SLOTS):
                experts_slot(groups - 1, s)

        @block.gpsimd
        def _(e):
            with e.Fori(0, groups) as g:
                for n in range(NS):
                    wait(e, "drive", g, n + 1)
                    e.tensor_tensor(dB[:, TOK * n:TOK * n + TOK], dB[:, TOK * n:TOK * n + TOK], dB2[n % 2][:, :],
                                    ALU.add).then_inc(sig["input"], 1)
                for n in range(1, NS):
                    before = dB[:, 0:TOK] if n == 1 else y_sum[(n - 1) % 2][:, :]
                    wait(e, "read", g, n + 1)
                    if n > 1:
                        wait(e, "added", g, n - 1)
                    e.tensor_tensor(y_sum[n % 2][:, :], before, dB[:, TOK * n:TOK * n + TOK],
                                    ALU.add).then_inc(sig["added"], 1)


_TOKENIZER = ['x', 'fc0_w', 'fc0_b', 'ln0_g', 'ln0_b', 'conv_w', 'conv_b', 'ln_g', 'ln_b', 'fc1_w', 'fc1_b',
              'fc2_w', 'fc2_b', 'fc3_w', 'fc3_b']
_OUTS = [((NI, T, D), 'float32')]


def build(nc, io, out, place, block_place, weight_place, expert_place):
    h0 = nc.dram_tensor("tokens", (NI, S, S), F32).ap()
    build_tokenizer(nc, io, place, h0)
    build_block(nc, io, block_place, weight_place, expert_place, h0, out)


def kernel(**inputs):
    import numpy as _np
    import concourse.bacc as _bacc
    from concourse import mybir as _mybir
    from concourse.bass_utils import run_bass_kernel_spmd as _run

    a = {name: _np.asarray(v) for name, v in inputs.items()}
    laid = {name: a[name if name == 'x' else 'L0_tok_' + name] for name in _TOKENIZER}
    laid["tables"], place = pack(constants())
    laid["w_mix"] = mixing_weights(*(a['L0_tok_' + name] for name in ('w1r', 'w1i', 'w2r', 'w2i')))
    laid["block_tables"], block_place = pack(block_tables())
    laid["block_weights"], weight_place = pack(block_weights(a))
    laid["expert_weights"], expert_place = pack(expert_weights(a))

    nc = _bacc.Bacc("TRN2", target_bir_lowering=False, num_devices=1)
    arrays, io = {}, {}
    for name, v in laid.items():
        v = _np.ascontiguousarray(v)
        arrays[f"in_{name}_dram"] = v
        io[name] = nc.dram_tensor(f"in_{name}_dram", v.shape, _mybir.dt.from_np(v.dtype), kind="ExternalInput").ap()
    outs = [nc.dram_tensor(f"out_{i}_dram", shape, _mybir.dt.from_np(_np.dtype(dtype)), kind="ExternalOutput").ap()
            for i, (shape, dtype) in enumerate(_OUTS)]
    build(nc, io, outs[0], place, block_place, weight_place, expert_place)
    r = _run(nc, [arrays], core_ids=[0])
    return r.results[0]["out_0_dram"]
```
